# Optimizing a Trainium2 kernel written in Bass

```python
import numpy as np
import jax
import jax.numpy as jnp

def _softmax(x, axis=-1):
    return jax.nn.softmax(x, axis=axis)

def _gelu(x):
    return jax.nn.gelu(x, approximate=True)

def _silu(x):
    return jax.nn.silu(x)

def _sigmoid(x):
    return jax.nn.sigmoid(x)

def _layernorm(x, axis=-1, eps=1e-05):
    m = jnp.mean(x, axis=axis, keepdims=True)
    v = jnp.var(x, axis=axis, keepdims=True)
    return (x - m) / jnp.sqrt(v + eps)

def _scatter_add(tgt, idx, src, axis=0):
    return tgt.at[idx].add(src)

def _segment_sum(src, seg, n):
    return jax.ops.segment_sum(src, seg, n)
kernel_name = 'mk_decoder_preln_d1_seqx_r8_6deb45'

def setup_inputs(seed: int=0):
    np.random.seed(seed)
    _w = jnp.asarray

    def _rec_inputs():
        import jax
        import jax.numpy as jnp
        _rk = jax.random.key(seed)
        x = -0.000125 + 0.9999 * jax.random.normal(jax.random.fold_in(_rk, 1), (4, 256, 256), jnp.float32)
        _lenS = 256 - jax.random.randint(jax.random.fold_in(_rk, 7), (4,), 0, max(1, 256 // 4) + 1, jnp.int32)
        _lenS2 = 256 - jax.random.randint(jax.random.fold_in(_rk, 8), (4,), 0, max(1, 256 // 4) + 1, jnp.int32)
        itok_BxS_13_99985 = jax.random.randint(jax.random.fold_in(_rk, 11), (4, 256), 13, 99986, jnp.int32)
        _ctx_2048P = jax.random.normal(jax.random.fold_in(_rk, 12), (4, 16, 256), jnp.float32)
        _ctx_2048c = jax.random.dirichlet(jax.random.fold_in(_rk, 512), 0.3 * jnp.ones((16,), jnp.float32), (4, 256))
        _ctx_2048t = jnp.einsum('bsk,bkd->bsd', _ctx_2048c, _ctx_2048P)
        _ctx_2048t = _ctx_2048t * jax.lax.rsqrt(jnp.mean(jnp.square(_ctx_2048t)) + 1e-12) * 0.953939
        ctx_2048 = 6.82029e-06 + 0.0200006 * (_ctx_2048t + 0.3 * jax.random.normal(jax.random.fold_in(_rk, 612), (4, 256, 256), jnp.float32))
        return (x, itok_BxS_13_99985, ctx_2048)
    x, itok_BxS_13_99985, ctx_2048 = _rec_inputs()

    def _L0_attn_setup():
        import jax, jax.numpy as jnp
        import numpy as np
        from jax import lax
        BLOCKS = 16
        NUM_HEADS = 8
        KEY_DIM = 64
        WIDTH = 64
        D_MODEL = 256

        def _forward(x, conv_w, conv_b, wq, bq, wk, bk, wv, bv, wo, bo, proj_w, proj_b):
            N, T, D = x.shape
            xp = jnp.pad(x, ((0, 0), (2, 0), (0, 0)))
            qkv = lax.conv_general_dilated(xp, conv_w, window_strides=(1,), padding='VALID', dimension_numbers=('NWC', 'WIO', 'NWC')) + conv_b
            q, k, v = jnp.split(qkv, 3, axis=-1)
            block_len = T // BLOCKS
            qb = q.reshape(N * BLOCKS, block_len, WIDTH)
            kb = k.reshape(N * BLOCKS, block_len, WIDTH)
            vb = v.reshape(N * BLOCKS, block_len, WIDTH)
            qh = jnp.einsum('bsd,dhk->bshk', qb, wq) + bq
            kh = jnp.einsum('bsd,dhk->bshk', kb, wk) + bk
            vh = jnp.einsum('bsd,dhk->bshk', vb, wv) + bv
            scale = 1.0 / jnp.sqrt(jnp.asarray(KEY_DIM, qh.dtype))
            scores = jnp.einsum('bqhk,bshk->bhqs', qh * scale, kh)
            causal = jnp.tril(jnp.ones((block_len, block_len), bool))
            scores = jnp.where(causal[None, None], scores, jnp.asarray(-1000000000.0, scores.dtype))
            attn = jax.nn.softmax(scores, axis=-1)
            ctx = jnp.einsum('bhqs,bshk->bqhk', attn, vh)
            mha_out = jnp.einsum('bqhk,hko->bqo', ctx, wo) + bo
            mha_out = mha_out.reshape(N, T, WIDTH)
            out = mha_out @ proj_w + proj_b
            return out
        key = jax.random.key(seed)
        ks = jax.random.split(key, 8)
        N, T = (4, 512)
        s = lambda *sh: 0.02
        x = jax.random.normal(ks[0], (N, T, D_MODEL), jnp.float32)
        conv_w = jax.random.normal(ks[1], (3, D_MODEL, 3 * WIDTH), jnp.float32) * 0.02
        conv_b = jnp.zeros((3 * WIDTH,), jnp.float32)
        wq = jax.random.normal(ks[2], (WIDTH, NUM_HEADS, KEY_DIM), jnp.float32) * 0.05
        wk = jax.random.normal(ks[3], (WIDTH, NUM_HEADS, KEY_DIM), jnp.float32) * 0.05
        wv = jax.random.normal(ks[4], (WIDTH, NUM_HEADS, KEY_DIM), jnp.float32) * 0.05
        bq = jnp.zeros((NUM_HEADS, KEY_DIM), jnp.float32)
        bk = jnp.zeros((NUM_HEADS, KEY_DIM), jnp.float32)
        bv = jnp.zeros((NUM_HEADS, KEY_DIM), jnp.float32)
        wo = jax.random.normal(ks[5], (NUM_HEADS, KEY_DIM, WIDTH), jnp.float32) * 0.05
        bo = jnp.zeros((WIDTH,), jnp.float32)
        proj_w = jax.random.normal(ks[6], (WIDTH, D_MODEL), jnp.float32) * 0.05
        proj_b = jnp.zeros((D_MODEL,), jnp.float32)
        return dict(x=x, conv_w=conv_w, conv_b=conv_b, wq=wq, bq=bq, wk=wk, bk=bk, wv=wv, bv=bv, wo=wo, bo=bo, proj_w=proj_w, proj_b=proj_b)
    _L0_attn_all = _L0_attn_setup()
    _L0_attn_in = {k: v for k, v in _L0_attn_all.items() if k in ('conv_w', 'conv_b', 'wq', 'bq', 'wk', 'bk', 'wv', 'bv', 'wo', 'bo', 'proj_w', 'proj_b')}
    del _L0_attn_all

    def _L0_xattn_setup():
        import jax, jax.numpy as jnp
        import numpy as np
        B, S, D = (4, 512, 256)
        E = 4
        F = 1024 // E
        VOCAB = 12500
        key = jax.random.key(seed)
        k1, k2, k3, k4, k5 = jax.random.split(key, 5)
        hidden_states = jax.random.normal(k1, (B, S, D), dtype=jnp.float32)
        token_ids = jax.random.randint(k2, (B, S), 0, VOCAB, dtype=jnp.int64)
        Wg = jax.random.normal(k3, (E, F, D), dtype=jnp.float32) * 0.02
        Wu = jax.random.normal(k4, (E, F, D), dtype=jnp.float32) * 0.02
        Wd = jax.random.normal(k5, (E, D, F), dtype=jnp.float32) * 0.02
        return {'hidden_states': hidden_states, 'token_ids': token_ids, 'Wg': Wg, 'Wu': Wu, 'Wd': Wd}
    _L0_xattn_all = _L0_xattn_setup()
    _L0_xattn_in = {k: v for k, v in _L0_xattn_all.items() if k in ()}
    del _L0_xattn_all

    def _L0_ffn_setup():
        import jax, jax.numpy as jnp
        import numpy as np
        D_MODEL = 256
        D_EXPERT = 1024
        EPS = 1e-08

        def ternary_quant(w):
            scale = jnp.mean(jnp.abs(w)) + EPS
            q = jnp.clip(jnp.round(w / scale), -1.0, 1.0) * scale
            return w + jax.lax.stop_gradient(q - w)
        key = jax.random.key(seed)
        k_x, k_up, k_gate, k_down = jax.random.split(key, 4)
        std_in = 1.0 / np.sqrt(D_MODEL)
        std_exp = 1.0 / np.sqrt(D_EXPERT)
        return {'x': jax.random.normal(k_x, (4, 256, D_MODEL), dtype=jnp.float32), 'W_up': jax.random.normal(k_up, (D_EXPERT, D_MODEL), dtype=jnp.float32) * std_in, 'W_gate': jax.random.normal(k_gate, (D_EXPERT, D_MODEL), dtype=jnp.float32) * std_in, 'W_down': jax.random.normal(k_down, (D_MODEL, D_EXPERT), dtype=jnp.float32) * std_exp}
    _L0_ffn_all = _L0_ffn_setup()
    _L0_ffn_in = {k: v for k, v in _L0_ffn_all.items() if k in ('W_up', 'W_gate', 'W_down')}
    del _L0_ffn_all
    return {'x': x, 'itok_BxS_13_99985': itok_BxS_13_99985, 'ctx_2048': ctx_2048, 'L0_attn_conv_w': _L0_attn_in['conv_w'], 'L0_attn_conv_b': _L0_attn_in['conv_b'], 'L0_attn_wq': _L0_attn_in['wq'], 'L0_attn_bq': _L0_attn_in['bq'], 'L0_attn_wk': _L0_attn_in['wk'], 'L0_attn_bk': _L0_attn_in['bk'], 'L0_attn_wv': _L0_attn_in['wv'], 'L0_attn_bv': _L0_attn_in['bv'], 'L0_attn_wo': _L0_attn_in['wo'], 'L0_attn_bo': _L0_attn_in['bo'], 'L0_attn_proj_w': _L0_attn_in['proj_w'], 'L0_attn_proj_b': _L0_attn_in['proj_b'], 'L0_ffn_W_up': _L0_ffn_in['W_up'], 'L0_ffn_W_gate': _L0_ffn_in['W_gate'], 'L0_ffn_W_down': _L0_ffn_in['W_down']}

def reference(x, itok_BxS_13_99985, ctx_2048, L0_attn_conv_w, L0_attn_conv_b, L0_attn_wq, L0_attn_bq, L0_attn_wk, L0_attn_bk, L0_attn_wv, L0_attn_bv, L0_attn_wo, L0_attn_bo, L0_attn_proj_w, L0_attn_proj_b, L0_ffn_W_up, L0_ffn_W_gate, L0_ffn_W_down):
    import jax
    import jax.numpy as jnp

    def _L0_attn_ref(x, conv_w, conv_b, wq, bq, wk, bk, wv, bv, wo, bo, proj_w, proj_b):
        import jax, jax.numpy as jnp
        import numpy as np
        from jax import lax
        BLOCKS = 16
        NUM_HEADS = 8
        KEY_DIM = 64
        WIDTH = 64
        D_MODEL = 256

        def _forward(x, conv_w, conv_b, wq, bq, wk, bk, wv, bv, wo, bo, proj_w, proj_b):
            N, T, D = x.shape
            xp = jnp.pad(x, ((0, 0), (2, 0), (0, 0)))
            qkv = lax.conv_general_dilated(xp, conv_w, window_strides=(1,), padding='VALID', dimension_numbers=('NWC', 'WIO', 'NWC')) + conv_b
            q, k, v = jnp.split(qkv, 3, axis=-1)
            block_len = T // BLOCKS
            qb = q.reshape(N * BLOCKS, block_len, WIDTH)
            kb = k.reshape(N * BLOCKS, block_len, WIDTH)
            vb = v.reshape(N * BLOCKS, block_len, WIDTH)
            qh = jnp.einsum('bsd,dhk->bshk', qb, wq) + bq
            kh = jnp.einsum('bsd,dhk->bshk', kb, wk) + bk
            vh = jnp.einsum('bsd,dhk->bshk', vb, wv) + bv
            scale = 1.0 / jnp.sqrt(jnp.asarray(KEY_DIM, qh.dtype))
            scores = jnp.einsum('bqhk,bshk->bhqs', qh * scale, kh)
            causal = jnp.tril(jnp.ones((block_len, block_len), bool))
            scores = jnp.where(causal[None, None], scores, jnp.asarray(-1000000000.0, scores.dtype))
            attn = jax.nn.softmax(scores, axis=-1)
            ctx = jnp.einsum('bhqs,bshk->bqhk', attn, vh)
            mha_out = jnp.einsum('bqhk,hko->bqo', ctx, wo) + bo
            mha_out = mha_out.reshape(N, T, WIDTH)
            out = mha_out @ proj_w + proj_b
            return out
        return _forward(x, conv_w, conv_b, wq, bq, wk, bk, wv, bv, wo, bo, proj_w, proj_b)

    def _L0_xattn_ref(hidden_states, token_ids, Wg, Wu, Wd):
        import jax, jax.numpy as jnp
        import numpy as np
        B, S, D = (4, 512, 256)
        E = 4
        F = 1024 // E
        VOCAB = 12500
        tokens_per_expert = VOCAB // E
        tid = jnp.clip(token_ids, 0, VOCAB - 1)
        expert_ids = jnp.minimum(tid // tokens_per_expert, E - 1)
        out = jnp.zeros_like(hidden_states)
        for e in range(E):
            g = jax.nn.silu(jnp.einsum('bsd,fd->bsf', hidden_states, Wg[e]))
            u = jnp.einsum('bsd,fd->bsf', hidden_states, Wu[e])
            y = jnp.einsum('bsf,df->bsd', g * u, Wd[e])
            out = jnp.where((expert_ids == e)[..., None], y, out)
        return out

    def _L0_ffn_ref(x, W_up, W_gate, W_down):
        import jax, jax.numpy as jnp
        import numpy as np
        D_MODEL = 256
        D_EXPERT = 1024
        EPS = 1e-08

        def ternary_quant(w):
            scale = jnp.mean(jnp.abs(w)) + EPS
            q = jnp.clip(jnp.round(w / scale), -1.0, 1.0) * scale
            return w + jax.lax.stop_gradient(q - w)
        wu = ternary_quant(W_up)
        wg = ternary_quant(W_gate)
        wd = ternary_quant(W_down)
        up = jnp.einsum('bsd,ed->bse', x, wu)
        gate = jnp.einsum('bsd,ed->bse', x, wg)
        hidden = jax.nn.silu(up) * gate
        return jnp.einsum('bse,de->bsd', hidden, wd)
    x = x + _L0_attn_ref(_layernorm(x, axis=-1), L0_attn_conv_w, L0_attn_conv_b, L0_attn_wq, L0_attn_bq, L0_attn_wk, L0_attn_bk, L0_attn_wv, L0_attn_bv, L0_attn_wo, L0_attn_bo, L0_attn_proj_w, L0_attn_proj_b)
    x = x + _L0_xattn_ref(_layernorm(x, axis=-1), itok_BxS_13_99985, ctx_2048, ctx_2048, ctx_2048)
    x = x + _L0_ffn_ref(_layernorm(x, axis=-1), L0_ffn_W_up, L0_ffn_W_gate, L0_ffn_W_down)
    return x

_drawn_inputs = setup_inputs


def setup_inputs(seed=0):
    import zlib

    import numpy as np

    out = dict(_drawn_inputs(seed))
    spreads = {'L0_attn_conv_b': (0.0, 0.427),
     'L0_attn_bq': (0.0, 0.8),
     'L0_attn_bk': (0.0, 0.8),
     'L0_attn_bv': (0.0, 0.1),
     'L0_attn_bo': (0.0, 0.1),
     'L0_attn_proj_b': (0.0, 0.1)}
    factors = {'L0_attn_wq': 8.0, 'L0_attn_wk': 8.0}
    for name, (base, spread) in spreads.items():
        noise = np.random.default_rng([zlib.crc32(name.encode()), seed]).standard_normal(out[name].shape)
        drawn = base * np.exp(spread * noise) if base else spread * noise
        out[name] = jnp.asarray(drawn.astype(out[name].dtype))
    for name, factor in factors.items():
        out[name] = (out[name] * factor).astype(out[name].dtype)
    return out
```

```python
from contextlib import ExitStack

import concourse.bass as bass
from concourse import mybir

ALU = mybir.AluOpType
ACT = mybir.ActivationFunctionType
AX = mybir.AxisListType
F32 = mybir.dt.float32
F16 = mybir.dt.float16
I32 = mybir.dt.int32
U32 = mybir.dt.uint32
ADD_ALL = bass.bass_isa.ReduceOp.add
ABSMAX_ALL = bass.bass_isa.ReduceOp.absmax

P = 128
B, S, D = 4, 256, 256
TAPS = 3
W = 64
H = 8
BLK = 16
E = 4
FE = 1024
PER_EXPERT = 12500 // E
LN_EPS = 1e-5
Q_EPS = 1e-8
NEG = -1e9
EXPONENT = 0x7F800000

HALVES = 2
TILES = 4
NT = 512
NB = NT // BLK
W1 = W + 1


def plan_banks(uses):
    count, readers, out = {}, {}, {}
    for name, bank, read_by in uses:
        out[name] = (bank, count.get(bank, 0) + 1, readers.get(bank, []))
        count[bank] = count.get(bank, 0) + 1
        readers[bank] = read_by
    return out


def decoder_kernel(nc, x, ids, ctx_w, conv_w, conv_b, wq, bq, wk, bk, wv, bv, wo, bo,
                   proj_w, proj_b, w_up, w_gate, w_down, out):
    stack = ExitStack()
    with stack:
        def sb(name, shape, dt=F32):
            return stack.enter_context(nc.sbuf_tensor(name, shape, dt))

        def sem(name):
            return stack.enter_context(nc.semaphore(name))

        x_sb = sb("x_sb", [P, 8, D])
        ln_sb = sb("ln_sb", [P, 8, D])
        stats = sb("stats", [P, 8, 6])
        mv = sb("mv", [P, 8, 2])
        std = sb("std", [P, 8])
        rstd = sb("rstd", [P, 8])
        ident = sb("ident", [P, P])
        ident16 = sb("ident16", [P, P], F16)
        ones = sb("ones", [P, P])
        eps_col = sb("eps_col", [P, 1])
        key_ok = sb("key_ok", [P, H, BLK])
        causal = sb("causal", [P, BLK])
        blkmask = sb("blkmask", [P, 8])
        convw_sb = sb("convw_sb", [P, TAPS, 2, 3 * W])
        convb_sb = sb("convb_sb", [P, 2])
        wq_sb = sb("wq_sb", [W1, H * W])
        wk_sb = sb("wk_sb", [W1, H * W])
        wv_sb = sb("wv_sb", [W1, H * W])
        wqT = sb("wqT", [P, 4, W1])
        wkT = sb("wkT", [P, 4, 2, W1])
        wvT = sb("wvT", [P, 4, 2, W])
        bvT = sb("bvT", [P, 4])
        wo_sb = sb("wo_sb", [P, 4, 2, W])
        bo_sb = sb("bo_sb", [P, 1])
        proj_sb = sb("proj_sb", [P, 2, D])
        projb_sb = sb("projb_sb", [P, D])
        A_sb = sb("A_sb", [P, H, W1])
        G_sb = sb("G_sb", [P, H, 2, W])
        ybias = sb("ybias", [P, 1])
        ids_sb = sb("ids_sb", [P, 8 * P], I32)
        mask = sb("mask", [P, E, 8 * P], F16)
        up_nat = sb("up_nat", [P, 8, D])
        gate_nat = sb("gate_nat", [P, 8, D])
        down_nat = sb("down_nat", [P, 2, FE])
        tern = sb("tern", [P, 3, FE * 2], F16)
        upT = sb("upT", [P, 2, FE], F16)
        gateT = sb("gateT", [P, 2, FE], F16)
        downT = sb("downT", [P, 8, D], F16)
        ctx_nat = sb("ctx_nat", [P, E, 2, D])
        ctxT_hi = sb("ctxT_hi", [P, 2, E, D], F16)
        ctxT_lo = sb("ctxT_lo", [P, 2, E, D], F16)
        maxes = sb("maxes", [P, 4])
        allmax = sb("allmax", [P, 4])
        wsum = sb("wsum", [P, 3])
        sc = sb("sc", [P, 40])
        xT = sb("xT", [P, 2, B, S + 2])
        q_sb = sb("q_sb", [P, B * S])
        k_sb = sb("k_sb", [W, B * S])
        vT_sb = sb("vT_sb", [P, B * S])
        k_hi = sb("k_hi", [W1, B * S], F16)
        k_lo = sb("k_lo", [W1, B * S], F16)
        t_hi_st = sb("t_hi_st", [P, 2 * NB * P], F16)
        t_lo_st = sb("t_lo_st", [P, 2 * NB * P], F16)
        t_hi = t_hi_st[0:W1, :].rearrange("p (b h q) -> p b h q", h=H, q=BLK)
        t_lo = t_lo_st[0:W1, :].rearrange("p (b h q) -> p b h q", h=H, q=BLK)
        s_sb = sb("s_sb", [P, HALVES, NB, BLK])
        smax = sb("smax", [P, HALVES, NB])
        ssum = sb("ssum", [P, HALVES, NB])
        rsum = sb("rsum", [P, HALVES, NB])
        pT_sb = sb("pT_sb", [P, HALVES, TILES, P])
        v_tok = sb("v_tok", [P, HALVES, TILES, W])
        v_bd = sb("v_bd", [P, 8, 4, 2, W])

        t_lo_all = t_lo_st[:, :]
        hm_hi = t_lo_all[:, 0:4096].rearrange("p (e c n) -> p e c n", e=E, c=2)
        hm_lo = t_lo_all[:, 4096:8192].rearrange("p (e c n) -> p e c n", e=E, c=2)
        t_hi_all = t_hi_st[:, :]
        hT_hi = t_hi_all[:, 0:2048].rearrange("p (c n) -> p c n", c=2)
        hT_lo = t_hi_all[:, 2048:4096].rearrange("p (c n) -> p c n", c=2)
        silu_sb = t_hi_all[:, 4096:6144].bitcast(F32).rearrange("p (s n) -> p s n", s=2)
        hid = t_hi_all[:, 6144:8192].bitcast(F32).rearrange("p (s n) -> p s n", s=2)
        hid_hi = v_bd[:, 0:2, :, :, :].rearrange("p a c b w -> p (a c b w)")[:, 0:3 * NT // 2].bitcast(F16) \
            .rearrange("p (s n) -> p s n", s=3)
        hid_lo = v_bd[:, 2:4, :, :, :].rearrange("p a c b w -> p (a c b w)")[:, 0:3 * NT // 2].bitcast(F16) \
            .rearrange("p (s n) -> p s n", s=3)
        y_sb = vT_sb[:, 0:NT].rearrange("p (h n) -> p h n", h=HALVES)
        u_sb = xT[:, :, :, :].rearrange("p c n s -> p (c n s)")[:, 0:H * NT // 2].rearrange("p (h n) -> p h n", h=H)

        bank = [stack.enter_context(nc.psum_tensor(f"bank{i}", [P, 512], F32)) for i in range(8)]

        names = ["bound", "bound1", "pow_b", "inv_b", "one_k", "amax", "pow_a", "inv_a", "t_ab", "t_scale",
                 "f_ab", "f_scale", "cmax", "pow_c", "inv_c", "c_scale", "silu_x", "hid_x", "c2", "y_x",
                 "m0", "m1", "m2", "h0", "h1", "h2", "n0", "n1", "n2", "silu_f", "inv_u", "hid_f",
                 "sg", "y_f", "kb"]
        col = {n: sc[:, i:i + 1] for i, n in enumerate(names)}

        dma = {n: sem("loaded_" + n) for n in
               ["x0", "x1", "convw", "convb", "wq", "wk", "wv", "wo", "bo", "proj", "projb", "up", "gate",
                "down", "ctx", "ids"]}
        written = [sem(f"bank{i}_written") for i in range(8)]
        consts = sem("consts")
        acc_w = sem("acc_w")
        mxs = sem("mxs")
        allm = sem("allm")
        scal = sem("scal")
        xb_ready = sem("xb_ready")
        wT_ready = sem("wT_ready")
        A_ready = sem("A_ready")
        G_ready = sem("G_ready")
        yb_ready = sem("yb_ready")
        dve_ln = sem("dve_ln")
        ln_std = sem("ln_std")
        ln_done = sem("ln_done")
        xT_ready = sem("xT_ready")
        qv_ready = sem("qv_ready")
        k_ready = sem("k_ready")
        ks_ready = sem("ks_ready")
        vtok_ready = sem("vtok_ready")
        vbd_ready = sem("vbd_ready")
        thi_ready = sem("thi_ready")
        tlo_ready = sem("tlo_ready")
        sm = sem("sm")
        exp_ready = sem("exp_ready")
        p_ready = sem("p_ready")
        pT_ready = sem("pT_ready")
        u_ready = sem("u_ready")
        y_ready = sem("y_ready")
        x1_ready = sem("x1_ready")
        chi_ready = sem("chi_ready")
        clo_ready = sem("clo_ready")
        mask_ready = sem("mask_ready")
        tlow_ready = sem("tlow_ready")
        tern_ready = sem("tern_ready")
        ffT_ready = sem("ffT_ready")
        hhi_ready = sem("hhi_ready")
        hlo_ready = sem("hlo_ready")
        mhi_ready = sem("mhi_ready")
        mlo_ready = sem("mlo_ready")
        silu_ready = sem("silu_ready")
        hid_ready = sem("hid_ready")
        hidhi_ready = sem("hidhi_ready")
        hidlo_ready = sem("hidlo_ready")
        x2_ready = sem("x2_ready")
        stored = sem("stored")
        down_used = sem("down_used")
        down_done = sem("down_done")
        rs_ready = sem("rs_ready")

        uses = [("wqT", 0, [(wT_ready, 1)]), ("wkT", 1, [(wT_ready, 3)]), ("wvT", 2, [(wT_ready, 6)])]
        for h in range(HALVES):
            uses += [(("tr1", h, c), 6 + c, [(xT_ready, 4 * h + 2 * c + 2)]) for c in range(2)]
        uses += [("A0", 3, [(A_ready, 1)]), ("A1", 4, [(A_ready, 2)]), ("G", 5, [(G_ready, 2)]),
                 ("yb", 2, [(yb_ready, 1)])]
        for h in range(HALVES):
            uses += [(("qv", h), 2 * h, [(qv_ready, 2 * h + 2)]), (("k", h), 2 * h + 1, [(k_ready, h + 1)])]
        uses += []
        uses += [(("v", h), 4, [(vtok_ready, h + 1)]) for h in range(HALVES)]

        def t_uses(h):
            return [(("t", h, i), (6, 7, 0, 1)[i % 4], [(thi_ready, H * h + i + 1), (tlo_ready, H * h + i + 1)])
                    for i in range(H)]

        uses += t_uses(0) + [(("s", 0), 2, [(sm, 1)])]
        uses += [(("ctx", e), (3, 4, 5, 3)[e], [(chi_ready, e + 1), (clo_ready, e + 1)]) for e in range(E)]
        uses += [("wsum", 5, [(scal, C_SCALE + 7)])]
        uses += t_uses(1) + [(("s", 1), 3, [(sm, 6)])]
        FF = [("up", 0), ("up", 1), ("gate", 0), ("gate", 1), ("down", 0), ("down", 1)]
        for h in range(HALVES):
            uses += [(("pT", h), 4, [(pT_ready, h + 1)])]
            uses += [(("u", h, i), (5, 6, 7, 0)[i], [(u_ready, TILES * h + i + 1)]) for i in range(TILES)]
            uses += [(("y", h), 1, [(y_ready, h + 1)])]
            uses += [(("proj", h, n), (2, 4)[n], [(x1_ready, 2 * h + n + 1)]) for n in range(2)]
            uses += [(("ff", i), (5, 6, 7)[i % 3], [(ffT_ready, i + 1)]) for i in range(3 * h, 3 * h + 3)]

        def ln_uses(which, h):
            k = HALVES * (which - 2) + h
            return [((f"tr{which}", h, c), 2 + c, [(hhi_ready, 2 * k + c + 1), (hlo_ready, 2 * k + c + 1)])
                    for c in range(2)]

        def x_uses(h):
            return [(("x_up", h, c), c % 2, [(silu_ready, 8 * h + c + 1), (hid_ready, 8 * h + c + 1)])
                    for c in range(8)]

        def f_uses(h):
            out_ = []
            for c in range(8):
                k = 16 + 8 * h + c + 1
                out_ += [(("f_up", h, c), c % 2, [(silu_ready, k)]),
                         (("f_gate", h, c), 2 + c % 2, [(hid_ready, k)])]
            return out_

        def down_uses(layer, h):
            return [((layer, h, j), 4 + 2 * h + j, [(down_used, 8 * (layer == "f_down") + 4 * h + 2 * j + 2)])
                    for j in range(2)]

        uses += ln_uses(2, 0) + x_uses(0) + down_uses("x_down", 0)
        uses += ln_uses(2, 1) + x_uses(1) + down_uses("x_down", 1)
        uses += ln_uses(3, 0) + f_uses(0) + down_uses("f_down", 0)
        uses += ln_uses(3, 1) + f_uses(1) + down_uses("f_down", 1)
        plan = plan_banks(uses)

        def filled(eng, name):
            b, n, _ = plan[name]
            eng.wait_ge(written[b], n)
            return bank[b]

        def down_read(eng, k):
            if k % 8 == 7:
                filled(eng, ("f_down" if k >= 16 else "x_down", k // 8 % 2, 1))
            else:
                eng.wait_ge(down_done, 7 * (k // 8) + k % 8 + 1)

        block = stack.enter_context(nc.Block())

        @block.sync
        def _(sp):
            xin = x.rearrange("n (t b r) d -> t r n b d", t=2, b=2)
            for h in range(HALVES):
                dst = x_sb[:, TILES * h:TILES * (h + 1), :].rearrange("p (n b) d -> p n b d", n=2)
                for n in range(2):
                    for t in range(2):
                        sp.dma_start(dst[64 * t:64 * t + 64, n], xin[t, :, 2 * h + n]).then_inc(dma[f"x{h}"], 16)
            sp.dma_start(convb_sb[0:W, 0:1], conv_b[0:W].unsqueeze(1)).then_inc(dma["convb"], 16)
            sp.dma_start(convb_sb[W:P, 0:1], conv_b[2 * W:3 * W].unsqueeze(1)).then_inc(dma["convb"], 16)
            sp.wait_ge(consts, 1)
            sp.dma_start(convb_sb[0:W, 1:2], conv_b[W:2 * W].unsqueeze(1)).then_inc(dma["convb"], 16)
            sp.wait_ge(consts, 3)
            for s in range(2):
                sp.dma_start(proj_sb[W * s:W * s + W, s, :], proj_w).then_inc(dma["proj"], 16)
                sp.dma_start(wo_sb[W * s:W * s + W, :, s, :],
                             wo.rearrange("(i s) k o -> s k i o", s=2)[s]).then_inc(dma["wo"], 16)
                sp.dma_start(bo_sb[W * s:W * s + W, :], bo.unsqueeze(1)).then_inc(dma["bo"], 16)
            sp.dma_start(projb_sb[:, :], proj_b.partition_broadcast(P)).then_inc(dma["projb"], 16)
            sp.dma_start(ctx_nat[:, :, :, :], ctx_w.rearrange("e (c p) d -> p e c d", p=P)).then_inc(dma["ctx"], 16)
            sp.dma_start(up_nat[:, :, :], w_up.rearrange("(c p) d -> p c d", p=P)).then_inc(dma["up"], 16)
            sp.dma_start(gate_nat[:, :, :], w_gate.rearrange("(c p) d -> p c d", p=P)).then_inc(dma["gate"], 16)
            sp.dma_start(down_nat[:, :, :], w_down.rearrange("(c p) d -> p c d", p=P)).then_inc(dma["down"], 16)
            for n in range(B):
                src = ids[n].rearrange("(t b r) -> b t r", t=2, b=2)
                for b in range(2):
                    sp.dma_start(ids_sb[:, S * n + P * b:S * n + P * (b + 1)].rearrange("p (t r) -> p t r", t=2),
                                 src[b].partition_broadcast(P)).then_inc(dma["ids"], 16)
            xout = out.rearrange("n (t b r) d -> t r n b d", t=2, b=2)
            for h in range(HALVES):
                sp.wait_ge(down_used, 8 + 4 * h + 4)
                src = x_sb[:, TILES * h:TILES * (h + 1), :].rearrange("p (n b) d -> p n b d", n=2)
                for n in range(2):
                    for t in range(2):
                        sp.dma_start(xout[t, :, 2 * h + n], src[64 * t:64 * t + 64, n]).then_inc(stored, 16)
            sp.wait_ge(stored, 16 * 4 * HALVES)

        @block.gpsimd
        def _(pool):
            built = 0

            def const(ins):
                nonlocal built
                built += 1
                ins.then_inc(consts, 1)
                pool.wait_ge(consts, built)

            const(nc.gpsimd.memset(convb_sb[W:P, 1:2], 0.0))
            const(nc.gpsimd.memset(proj_sb[:, :, :], 0.0))
            const(nc.gpsimd.memset(wo_sb[:, :, :, :], 0.0))
            const(nc.gpsimd.memset(ident[:, :], 0.0))
            const(nc.gpsimd.memset(ones[:, :], 1.0))
            const(nc.gpsimd.affine_select(out=ident[:, :], in_=ident[:, :], compare_op=ALU.not_equal, fill=1.0,
                                    base=0, pattern=[[-1, P]], channel_multiplier=1))
            const(nc.gpsimd.memset(eps_col[:, :], LN_EPS))
            const(nc.gpsimd.memset(wkT[:, :, :, :], 0.0))
            const(nc.gpsimd.memset(xT[:, :, :, 0:2], 0.0))
            const(nc.gpsimd.memset(A_sb[W:P, :, :], 0.0))
            const(nc.gpsimd.memset(q_sb[W:P, :], 0.0))
            const(nc.gpsimd.memset(q_sb[W:W1, :], 1.0))
            const(nc.gpsimd.memset(G_sb[:, :, :, :], 0.0))
            const(nc.gpsimd.memset(key_ok[:, :, :], 1.0))
            const(nc.gpsimd.memset(blkmask[:, :], 1.0))
            const(nc.gpsimd.memset(k_lo[W:W1, :], 0.0))
            const(nc.gpsimd.affine_select(out=key_ok[:, :, :], in_=key_ok[:, :, :], compare_op=ALU.is_ge, fill=0.0,
                                    base=0, pattern=[[-BLK, H], [-1, BLK]], channel_multiplier=1))
            const(nc.gpsimd.affine_select(out=key_ok[:, :, :], in_=key_ok[:, :, :], compare_op=ALU.is_ge, fill=0.0,
                                    base=BLK - 1, pattern=[[BLK, H], [0, BLK]], channel_multiplier=-1))
            const(nc.gpsimd.affine_select(out=blkmask[:, :], in_=blkmask[:, :], compare_op=ALU.is_ge, fill=0.0,
                                    base=0, pattern=[[-BLK, 8]], channel_multiplier=1))
            const(nc.gpsimd.affine_select(out=blkmask[:, :], in_=blkmask[:, :], compare_op=ALU.is_ge, fill=0.0,
                                    base=BLK - 1, pattern=[[BLK, 8]], channel_multiplier=-1))
            const(nc.gpsimd.tensor_copy(ident16[:, :], ident[:, :]))
            pool.wait_ge(mxs, 2)
            nc.gpsimd.partition_all_reduce(allmax[:, 0:2], maxes[:, 0:2], P, ABSMAX_ALL).then_inc(allm, 1)
            pool.wait_ge(mxs, 3)
            nc.gpsimd.partition_all_reduce(allmax[:, 3:4], maxes[:, 3:4], P, ABSMAX_ALL).then_inc(allm, 1)
            pool.wait_ge(mxs, 4)
            nc.gpsimd.partition_all_reduce(allmax[:, 2:3], maxes[:, 2:3], P, ABSMAX_ALL).then_inc(allm, 1)
            pool.wait_ge(dma["projb"], 16)
            pool.wait_ge(ln_done, 8)
            nc.gpsimd.tensor_tensor(x_sb[:, :, :], x_sb[:, :, :],
                                    projb_sb[:, :].unsqueeze(1).to_broadcast([P, 8, D]), ALU.add).then_inc(xb_ready, 1)
            m = blkmask[:, :].rearrange("p (b c) -> p c b", b=2).unsqueeze(3).to_broadcast([P, 4, 2, W])
            pool.wait_ge(consts, 20)
            for h in range(HALVES):
                pool.wait_ge(vtok_ready, h + 1)
                for i in range(TILES):
                    for b in range(2):
                        v = v_tok[:, h, i, :].unsqueeze(1).to_broadcast([P, 4, W])
                        nc.gpsimd.tensor_tensor(v_bd[:, TILES * h + i, :, b, :], v, m[:, :, b, :],
                                                ALU.mult).then_inc(vbd_ready, 1)
            pool.wait_ge(dma["ids"], 16 * 2 * B)
            for e in range(1, E):
                nc.gpsimd.tensor_scalar(mask[:, e, :], ids_sb[:, :], float(e * PER_EXPERT), None,
                                        ALU.is_ge).then_inc(mask_ready, 1)
            pool.wait_ge(mask_ready, 1)
            nc.gpsimd.tensor_scalar(mask[:, 0, :], mask[:, 1, :], -1.0, 1.0, ALU.mult, ALU.add).then_inc(mask_ready, 1)
            pool.wait_ge(mask_ready, 4)
            nc.gpsimd.tensor_tensor(mask[:, 1, :], mask[:, 1, :], mask[:, 2, :], ALU.subtract).then_inc(mask_ready, 1)
            pool.wait_ge(mask_ready, 5)
            nc.gpsimd.tensor_tensor(mask[:, 2, :], mask[:, 2, :], mask[:, 3, :], ALU.subtract).then_inc(mask_ready, 1)
            pool.wait_ge(scal, TERN)
            for i, w_nat in enumerate((up_nat, gate_nat, down_nat)):
                nc.gpsimd.tensor_scalar(tern[:, i, :], w_nat[:, :, :].rearrange("p a b -> p (a b)"),
                                        col[f"n{i}"], None, ALU.is_lt).then_inc(tlow_ready, 1)
            for h in range(HALVES):
                pool.wait_ge(hlo_ready, 2 * h + 2)
                pool.wait_ge(mask_ready, 6)
                if h:
                    filled(pool, ("x_up", h - 1, 7))
                for e in range(E):
                    for c in range(2):
                        nc.gpsimd.tensor_tensor(hm_lo[:, e, c, :], hT_lo[:, c, NT * h:NT * (h + 1)],
                                                mask[:, e, NT * h:NT * (h + 1)], ALU.mult).then_inc(mlo_ready, 1)

        @block.scalar
        def _(act):
            for name, dst, wsrc, bsrc in (("wq", wq_sb, wq, bq), ("wk", wk_sb, wk, bk), ("wv", wv_sb, wv, bv)):
                act.dma_start(dst[0:W, :], wsrc.rearrange("d h k -> d (h k)")).then_inc(dma[name], 16)
                act.dma_start(dst[W:W1, :], bsrc.rearrange("h k -> (h k)").unsqueeze(0)).then_inc(dma[name], 16)
            cw = conv_w.rearrange("t (c p) f -> p (t c) f", p=P)
            for src, dst in ((0, 0), (2, 1), (1, 2)):
                act.dma_start(convw_sb[:, :, :, W * dst:W * dst + W].rearrange("p t c w -> p (t c) w"),
                              cw[:, :, W * src:W * src + W]).then_inc(dma["convw"], 16)

            def root(k, tiles):
                act.wait_ge(dve_ln, 8 * (k + 1))
                nc.scalar.activation(std[:, tiles], mv[:, tiles, 1], ACT.Sqrt, bias=eps_col[:, :]).then_inc(ln_std, 1)

            def tiles_of(h):
                return slice(TILES * h, TILES * (h + 1))

            act.wait_ge(consts, 7)
            for h in range(HALVES):
                root(h, tiles_of(h))
            act.wait_ge(consts, 9)
            for h in range(HALVES):
                for c in range(2):
                    src = filled(act, ("tr1", h, c))[:, :].rearrange("p (n b t r) -> p n b t r", n=2, b=2, t=2)
                    for n in range(2):
                        dst = xT[:, c, 2 * h + n, 2:].rearrange("p (t b r) -> p b t r", t=2, b=2)
                        nc.scalar.activation(dst, src[:, n], ACT.Copy).then_inc(xT_ready, 1)
            act.wait_ge(dma["convb"], 48)
            act.wait_ge(consts, 12)
            for h in range(HALVES):
                half = slice(NT * h, NT * (h + 1))
                src = filled(act, ("qv", h))
                nc.scalar.activation(q_sb[0:W, half], src[0:W, :], ACT.Identity,
                                     bias=convb_sb[0:W, 0:1]).then_inc(qv_ready, 1)
                nc.scalar.activation(vT_sb[W:P, half], src[W:P, :], ACT.Identity,
                                     bias=convb_sb[W:P, 0:1]).then_inc(qv_ready, 1)
                src = filled(act, ("k", h))
                nc.scalar.activation(k_sb[:, half], src[0:W, :], ACT.Identity,
                                     bias=convb_sb[0:W, 1:2]).then_inc(k_ready, 1)
            for h in range(HALVES):
                src = filled(act, ("v", h))
                nc.scalar.activation(v_tok[:, h, :, :], src[:, 0:TILES * W].rearrange("p (i w) -> p i w", w=W),
                                     ACT.Copy).then_inc(vtok_ready, 1)

            def t_high(h):
                act.wait_ge(scal, T_SCALE)
                for i in range(H):
                    src = filled(act, ("t", h, i))[0:W1, :].rearrange("p (b q) -> p b q", q=BLK)
                    nc.scalar.activation(t_hi[:, NB * h:NB * (h + 1), i, :], src, ACT.Copy,
                                         scale=col["t_scale"][0:W1]).then_inc(thi_ready, 1)

            def softmax_exp(h):
                act.wait_ge(sm, 5 * h + 3)
                nc.scalar.activation(s_sb[:, h], s_sb[:, h], ACT.Exp).then_inc(exp_ready, 1)

            def attention_out(h):
                src = filled(act, ("pT", h))
                nc.scalar.activation(pT_sb[:, h], src[:, :].rearrange("p (i m) -> p i m", m=P),
                                     ACT.Copy).then_inc(pT_ready, 1)
                if h:
                    act.wait_ge(written[plan[("y", h - 1)][0]], plan[("y", h - 1)][1])
                for i in range(TILES):
                    src = filled(act, ("u", h, i))[:, :].rearrange("p (c h q) -> p h c q", c=4, h=H)
                    nc.scalar.activation(u_sb[:, :, 64 * i:64 * i + 64].rearrange("p h (c q) -> p h c q", c=4),
                                         src, ACT.Copy).then_inc(u_ready, 1)
                act.wait_ge(yb_ready, 1)
                src = filled(act, ("y", h))
                nc.scalar.activation(y_sb[:, h], src[:, 0:NT // 2], ACT.Identity, bias=ybias[:, :]).then_inc(y_ready, 1)

            def ff_evac(i):
                name, j = FF[i]
                src = filled(act, ("ff", i))[:, :].bitcast(F16)
                if name == "down":
                    nc.scalar.activation(downT[:, 4 * j:4 * j + 4, :], src.rearrange("p (c d) -> p c d", d=D),
                                         ACT.Copy).then_inc(ffT_ready, 1)
                else:
                    dst = upT if name == "up" else gateT
                    nc.scalar.activation(dst[:, j, :], src, ACT.Copy).then_inc(ffT_ready, 1)

            t_high(0)
            softmax_exp(0)
            act.wait_ge(scal, C_SCALE)
            for e in range(E):
                src = filled(act, ("ctx", e))[:, :].rearrange("p (c r) -> p c r", c=2)
                nc.scalar.activation(ctxT_hi[:, :, e, :], src, ACT.Copy, scale=col["c_scale"]).then_inc(chi_ready, 1)
            for i, (name, w_nat) in enumerate((("up", up_nat), ("gate", gate_nat), ("down", down_nat))):
                act.wait_ge(dma[name], 16)
                nc.scalar.activation(tern[:, i, :], w_nat[:, :, :].rearrange("p a b -> p (a b)"), ACT.Abs,
                                     accum_out=wsum[:, i:i + 1]).then_inc(acc_w, 1)
            t_high(1)
            softmax_exp(1)
            for h in range(HALVES):
                attention_out(h)
                for i in range(3 * h, 3 * h + 3):
                    ff_evac(i)

            def ln_high(which, h):
                k = HALVES * (which - 2) + h
                if which == 3:
                    act.wait_ge(mhi_ready, E * (h + 1))
                for c in range(2):
                    src = filled(act, (f"tr{which}", h, c))
                    nc.scalar.activation(hT_hi[:, c, NT * h:NT * (h + 1)], src[:, :], ACT.Copy,
                                         scale=2048.0).then_inc(hhi_ready, 1)

            def hidden(layer, h):
                for c in range(8):
                    k = 16 * (layer == "f") + 8 * h + c
                    src = filled(act, (f"{layer}_up", h, c))
                    if k >= 2:
                        act.wait_ge(hid_ready, k - 1)
                    nc.scalar.activation(silu_sb[:, k % 2, :], src[:, :], ACT.Silu,
                                         scale=col["silu_x" if layer == "x" else "silu_f"]).then_inc(silu_ready, 1)
                    if c:
                        hid_high(k - 1)
                hid_high(k)

            def hid_high(k):
                act.wait_ge(hid_ready, k + 1)
                if k >= 3:
                    down_read(act, k - 3)
                nc.scalar.activation(hid_hi[:, k % 3, :], hid[:, k % 2, :], ACT.Copy).then_inc(hidhi_ready, 1)

            root(2, tiles_of(0))
            ln_high(2, 0)
            root(3, tiles_of(1))
            act.wait_ge(scal, TERN)
            hidden("x", 0)
            ln_high(2, 1)
            root(4, tiles_of(0))
            hidden("x", 1)
            ln_high(3, 0)
            root(5, tiles_of(1))
            hidden("f", 0)
            ln_high(3, 1)
            hidden("f", 1)

        @block.vector
        def _(dve):
            def stats_of(k, h):
                for i in range(TILES):
                    T = TILES * h + i
                    nc.vector.bn_stats(stats[:, T, :], x_sb[:, T, :]).then_inc(dve_ln, 1)
                for i in range(TILES):
                    T = TILES * h + i
                    dve.wait_ge(dve_ln, 8 * k + i + 1)
                    nc.vector.bn_aggr(mv[:, T, :], stats[:, T, :]).then_inc(dve_ln, 1)

            def normalise(k, h):
                tiles = slice(TILES * h, TILES * (h + 1))
                dve.wait_ge(ln_std, k + 1)
                nc.vector.reciprocal(rstd[:, tiles], std[:, tiles]).then_inc(rs_ready, 1)
                dve.wait_ge(rs_ready, k + 1)
                if k >= 2:
                    which = k // 2
                    for c in range(2):
                        b_, n_, _ = plan[(f"tr{which}", h, c)]
                        dve.wait_ge(written[b_], n_)
                for i in range(TILES):
                    T = TILES * h + i
                    nc.vector.tensor_scalar(ln_sb[:, T, :], x_sb[:, T, :], mv[:, T, 0:1], rstd[:, T:T + 1],
                                            ALU.subtract, ALU.mult).then_inc(ln_done, 1)

            def chain(ins, step):
                ins.then_inc(scal, 1)
                dve.wait_ge(scal, step)

            for h in range(HALVES):
                dve.wait_ge(dma[f"x{h}"], 64)
                stats_of(h, h)
            for h in range(HALVES):
                normalise(h, h)

            src = filled(dve, "wqT")[:, 0:4 * W1].rearrange("p (i w) -> p i w", w=W1)
            nc.vector.tensor_copy(wqT[:, :, :], src).then_inc(wT_ready, 1)
            dve.wait_ge(consts, 8)
            src = filled(dve, "wkT")[:, 0:4 * W1].rearrange("p (i w) -> p i w", w=W1)
            for s in range(2):
                rows = slice(W * s, W * s + W)
                nc.vector.tensor_copy(wkT[rows, :, s, :], src[rows]).then_inc(wT_ready, 1)
            src = filled(dve, "wvT")[:, 0:4 * W1].rearrange("p (i w) -> p i w", w=W1)
            for s in range(2):
                nc.vector.tensor_copy(wvT[:, :, s, :], src[:, :, 0:W]).then_inc(wT_ready, 1)
            nc.vector.tensor_copy(bvT[:, :], src[:, :, W]).then_inc(wT_ready, 1)
            dve.wait_ge(consts, 10)
            for j in range(2):
                src = filled(dve, f"A{j}")[0:W1, 0:4 * W1].rearrange("p (i w) -> p i w", w=W1)
                nc.vector.tensor_copy(A_sb[0:W1, 4 * j:4 * j + 4, :], src).then_inc(A_ready, 1)
            dve.wait_ge(dma["convw"], 48)
            nc.vector.tensor_reduce(maxes[:, 0:1], convw_sb[:, :, :, :].rearrange("p a b c -> p (a b c)"), AX.X,
                                    ALU.max, apply_absolute_value=True).then_inc(mxs, 1)
            dve.wait_ge(dma["convb"], 48)
            dve.wait_ge(consts, 1)
            nc.vector.tensor_reduce(maxes[:, 1:2], convb_sb[:, :], AX.X, ALU.max,
                                    apply_absolute_value=True).then_inc(mxs, 1)
            dve.wait_ge(A_ready, 2)
            nc.vector.tensor_reduce(maxes[:, 3:4], A_sb[:, :, :].rearrange("p h w -> p (h w)"), AX.X, ALU.max,
                                    apply_absolute_value=True).then_inc(mxs, 1)
            dve.wait_ge(consts, 13)
            src = filled(dve, "G")[:, :].rearrange("p (h w) -> p h w", w=W)
            for s in range(2):
                rows = slice(W * s, W * s + W)
                nc.vector.tensor_copy(G_sb[rows, :, s, :], src[rows]).then_inc(G_ready, 1)
            dve.wait_ge(dma["bo"], 32)
            src = filled(dve, "yb")
            nc.vector.tensor_tensor(ybias[:, :], src[:, 0:1], bo_sb[:, :], ALU.add).then_inc(yb_ready, 1)
            step = 0

            def scalar(ins):
                nonlocal step
                step += 1
                ins.then_inc(scal, 1)
                dve.wait_ge(scal, step)
            ts = nc.vector.tensor_scalar
            dve.wait_ge(allm, 1)
            bound = float(TAPS * D)
            scalar(nc.vector.scalar_tensor_tensor(col["bound"], allmax[:, 0:1], bound, allmax[:, 1:2],
                                                  ALU.mult, ALU.add))
            scalar(nc.vector.tensor_scalar_add(col["bound1"], col["bound"], 1.0))
            scalar(nc.vector.tensor_single_scalar(col["pow_b"].bitcast(U32), col["bound1"].bitcast(U32), EXPONENT,
                                                  ALU.bitwise_and))
            scalar(nc.vector.reciprocal(col["inv_b"], col["pow_b"]))
            scalar(ts(col["one_k"], col["inv_b"], 2.0 ** 14, None, ALU.mult))
            dve.wait_ge(allm, 2)
            scalar(ts(col["amax"], allmax[:, 3:4], 1e-30, None, ALU.max))
            scalar(nc.vector.tensor_single_scalar(col["pow_a"].bitcast(U32), col["amax"].bitcast(U32), EXPONENT,
                                                  ALU.bitwise_and))
            scalar(nc.vector.reciprocal(col["inv_a"], col["pow_a"]))
            scalar(ts(col["t_scale"], col["inv_a"], col["inv_b"], 2.0 ** 6, ALU.mult, ALU.mult))
            assert step == T_SCALE
            scalar(ts(col["f_ab"], col["pow_a"], col["pow_b"], 2.0 ** -23, ALU.mult, ALU.mult))
            scalar(ts(col["f_scale"], col["f_ab"], col["pow_b"], None, ALU.mult))
            dve.wait_ge(consts, 18)
            scalar(nc.vector.tensor_reduce(causal[:, :], key_ok[:, :, :].rearrange("p h k -> p k h"), AX.X, ALU.add))
            scalar(ts(causal[:, :], causal[:, :], 1.0, -NEG, ALU.subtract, ALU.mult))

            def k_split(h):
                half = slice(NT * h, NT * (h + 1))
                dve.wait_ge(k_ready, h + 1)
                ts(k_hi[0:W, half], k_sb[:, half], col["one_k"][0:W], None, ALU.mult).then_inc(ks_ready, 1)
                dve.wait_ge(ks_ready, 3 * h + 1)
                nc.vector.scalar_tensor_tensor(k_lo[0:W, half], k_sb[:, half], col["one_k"][0:W], k_hi[0:W, half],
                                               ALU.mult, ALU.subtract).then_inc(ks_ready, 1)
                ts(k_hi[W:W1, half], q_sb[W:W1, half], col["one_k"][W:W1], None, ALU.mult).then_inc(ks_ready, 1)

            def t_low(h):
                for i in range(H):
                    src = filled(dve, ("t", h, i))[0:W1, :].rearrange("p (b q) -> p b q", q=BLK)
                    dve.wait_ge(thi_ready, H * h + i + 1)
                    nc.vector.scalar_tensor_tensor(t_lo[:, NB * h:NB * (h + 1), i, :], src, col["t_scale"][0:W1],
                                                   t_hi[:, NB * h:NB * (h + 1), i, :], ALU.mult,
                                                   ALU.subtract).then_inc(tlo_ready, 1)

            def softmax_in(h):
                src = filled(dve, ("s", h))[:, :].rearrange("p (b k) -> p b k", k=BLK)
                nc.vector.scalar_tensor_tensor(s_sb[:, h], src, col["f_scale"],
                                               causal[:, :].unsqueeze(1).to_broadcast([P, NB, BLK]),
                                               ALU.mult, ALU.add).then_inc(sm, 1)
                dve.wait_ge(sm, 5 * h + 1)
                nc.vector.tensor_reduce(smax[:, h], s_sb[:, h], AX.X, ALU.max).then_inc(sm, 1)
                dve.wait_ge(sm, 5 * h + 2)
                nc.vector.tensor_tensor(s_sb[:, h], s_sb[:, h], smax[:, h].unsqueeze(2).to_broadcast([P, NB, BLK]),
                                        ALU.subtract).then_inc(sm, 1)

            def softmax_out(h):
                dve.wait_ge(exp_ready, h + 1)
                nc.vector.tensor_reduce(ssum[:, h], s_sb[:, h], AX.X, ALU.add).then_inc(sm, 1)
                dve.wait_ge(sm, 5 * h + 4)
                nc.vector.reciprocal(rsum[:, h], ssum[:, h]).then_inc(sm, 1)
                dve.wait_ge(sm, 5 * h + 5)
                nc.vector.tensor_tensor(s_sb[:, h], s_sb[:, h], rsum[:, h].unsqueeze(2).to_broadcast([P, NB, BLK]),
                                        ALU.mult).then_inc(p_ready, 1)

            def ctx_low():
                for e in range(E):
                    dve.wait_ge(chi_ready, e + 1)
                    src = filled(dve, ("ctx", e))[:, :].rearrange("p (c r) -> p c r", c=2)
                    nc.vector.scalar_tensor_tensor(ctxT_lo[:, :, e, :], src, col["c_scale"], ctxT_hi[:, :, e, :],
                                                   ALU.mult, ALU.subtract).then_inc(clo_ready, 1)

            for h in range(HALVES):
                k_split(h)
            dve.wait_ge(dma["ctx"], 16)
            nc.vector.tensor_reduce(maxes[:, 2:3], ctx_nat[:, :, :, :].rearrange("p e c d -> p (e c d)"), AX.X,
                                    ALU.max, apply_absolute_value=True).then_inc(mxs, 1)
            dve.wait_ge(allm, 3)
            scalar(ts(col["cmax"], allmax[:, 2:3], 1e-12, None, ALU.max))
            scalar(nc.vector.tensor_single_scalar(col["pow_c"].bitcast(U32), col["cmax"].bitcast(U32), EXPONENT,
                                                  ALU.bitwise_and))
            scalar(nc.vector.reciprocal(col["inv_c"], col["pow_c"]))
            scalar(ts(col["c_scale"], col["inv_c"], 2.0 ** 14, None, ALU.mult))
            assert step == C_SCALE
            scalar(ts(col["silu_x"], col["pow_c"], 2.0 ** -25, None, ALU.mult))
            scalar(ts(col["hid_x"], col["inv_c"], 2.0 ** -28, None, ALU.mult))
            scalar(ts(col["c2"], col["pow_c"], col["pow_c"], 2.0 ** -11, ALU.mult, ALU.mult))
            scalar(ts(col["y_x"], col["c2"], col["pow_c"], None, ALU.mult))

            t_low(0)
            softmax_in(0)
            ctx_low()
            softmax_out(0)
            src = filled(dve, "wsum")
            for i in range(3):
                scalar(ts(col[f"m{i}"], src[:, i:i + 1], 1.0 / (FE * D), Q_EPS, ALU.mult, ALU.add))
            for i in range(3):
                scalar(ts(col[f"h{i}"], col[f"m{i}"], 0.5, None, ALU.mult))
                scalar(ts(col[f"n{i}"], col[f"m{i}"], -0.5, None, ALU.mult))
            scalar(ts(col["silu_f"], col["m0"], 2.0 ** -11, None, ALU.mult))
            scalar(nc.vector.reciprocal(col["inv_u"], col["m0"]))
            scalar(ts(col["hid_f"], col["inv_u"], 2.0 ** -12, None, ALU.mult))
            scalar(ts(col["sg"], col["m0"], col["m1"], 2.0, ALU.mult, ALU.mult))
            scalar(ts(col["y_f"], col["sg"], col["m2"], None, ALU.mult))
            assert step == TERN
            t_low(1)
            softmax_in(1)
            softmax_out(1)
            for i, w_nat in enumerate((up_nat, gate_nat, down_nat)):
                dve.wait_ge(tlow_ready, i + 1)
                nc.vector.scalar_tensor_tensor(tern[:, i, :], w_nat[:, :, :].rearrange("p a b -> p (a b)"),
                                               col[f"h{i}"], tern[:, i, :], ALU.is_gt,
                                               ALU.subtract).then_inc(tern_ready, 1)

            dve.wait_ge(xb_ready, 1)
            for h in range(HALVES):
                for n in range(2):
                    src = filled(dve, ("proj", h, n))[:, :].rearrange("p (b d) -> p b d", b=2)
                    tiles = slice(TILES * h + 2 * n, TILES * h + 2 * n + 2)
                    nc.vector.tensor_tensor(x_sb[:, tiles, :], src, x_sb[:, tiles, :], ALU.add).then_inc(x1_ready, 1)
                dve.wait_ge(x1_ready, 2 * h + 2)
                stats_of(2 + h, h)
                normalise(2 + h, h)
                if h == 0:
                    pass

            def ln_low(which, h):
                if which == 3:
                    dve.wait_ge(mlo_ready, 2 * E * (h + 1))
                k = HALVES * (which - 2) + h
                for c in range(2):
                    src = filled(dve, (f"tr{which}", h, c))
                    dve.wait_ge(hhi_ready, 2 * k + c + 1)
                    nc.vector.scalar_tensor_tensor(hT_lo[:, c, NT * h:NT * (h + 1)], src[:, :], 2048.0,
                                                   hT_hi[:, c, NT * h:NT * (h + 1)], ALU.mult,
                                                   ALU.subtract).then_inc(hlo_ready, 1)

            def mask_high(h, e):
                half = slice(NT * h, NT * (h + 1))
                dve.wait_ge(hhi_ready, 2 * h + 2)
                nc.vector.tensor_tensor(hm_hi[:, e, :, :], hT_hi[:, :, half],
                                        mask[:, e, half].unsqueeze(1).to_broadcast([P, 2, NT]),
                                        ALU.mult).then_inc(mhi_ready, 1)

            def hid_low(k):
                dve.wait_ge(hidhi_ready, k + 1)
                nc.vector.tensor_tensor(hid_lo[:, k % 3, :], hid[:, k % 2, :], hid_hi[:, k % 3, :],
                                        ALU.subtract).then_inc(hidlo_ready, 1)

            def hidden(layer, h):
                for c in range(8):
                    k = 16 * (layer == "f") + 8 * h + c
                    if layer == "x" and c % 2 == 0 and c // 2 + 1 < E:
                        mask_high(h, c // 2 + 1)
                    src = filled(dve, (f"{layer}_up" if layer == "x" else "f_gate", h, c))
                    dve.wait_ge(silu_ready, k + 1)
                    if k >= 2:
                        dve.wait_ge(hidlo_ready, k - 1)
                    nc.vector.scalar_tensor_tensor(hid[:, k % 2, :], src[:, :],
                                                   col["hid_x" if layer == "x" else "hid_f"],
                                                   silu_sb[:, k % 2, :], ALU.mult, ALU.mult).then_inc(hid_ready, 1)
                    if c:
                        hid_low(k - 1)
                hid_low(k)

            def add_down(layer, h):
                scale = col["y_x" if layer == "x" else "y_f"]
                for i in range(TILES):
                    src = filled(dve, (f"{layer}_down", h, i // 2))[:, D * (i % 2):D * (i % 2) + D]
                    T = TILES * h + i
                    nc.vector.scalar_tensor_tensor(x_sb[:, T, :], src, scale, x_sb[:, T, :], ALU.mult,
                                                   ALU.add).then_inc(down_used, 1)

            ln_low(2, 0)
            dve.wait_ge(mask_ready, 6)
            mask_high(0, 0)
            hidden("x", 0)
            ln_low(2, 1)
            add_down("x", 0)
            dve.wait_ge(down_used, 4)
            mask_high(1, 0)
            stats_of(4, 0)
            normalise(4, 0)
            hidden("x", 1)
            ln_low(3, 0)
            add_down("x", 1)
            dve.wait_ge(down_used, 8)
            stats_of(5, 1)
            normalise(5, 1)
            hidden("f", 0)
            ln_low(3, 1)
            add_down("f", 0)
            hidden("f", 1)
            add_down("f", 1)

        @block.tensor
        def _(pe):
            def begin(name):
                b, _, readers = plan[name]
                for s, v in readers:
                    pe.wait_ge(s, v)
                return bank[b]

            def end(name, ins):
                ins.then_inc(written[plan[name][0]], 1)

            mm = nc.tensor.matmul
            pe.wait_ge(consts, 6)
            for name, w_sb in (("wq", wq_sb), ("wk", wk_sb), ("wv", wv_sb)):
                o = begin(name + "T")
                pe.wait_ge(dma[name], 32)
                for i in range(4):
                    last = nc.tensor.transpose(o[:, W1 * i:W1 * i + W1], w_sb[:, P * i:P * i + P], ident[0:W1, 0:W1])
                end(name + "T", last)

            def transposes(which, h):
                pe.wait_ge(ln_done, 8 * (which - 1) + TILES * (h + 1))
                for c in range(2):
                    o = begin((f"tr{which}", h, c))
                    for i in range(TILES):
                        last = nc.tensor.transpose(o[:, P * i:P * i + P],
                                                   ln_sb[:, TILES * h + i, P * c:P * c + P], ident[:, :])
                    end((f"tr{which}", h, c), last)

            for h in range(HALVES):
                transposes(1, h)
            pe.wait_ge(wT_ready, 6)
            for j in range(2):
                o = begin(f"A{j}")
                for i in range(2):
                    last = mm(o[0:W1, 2 * W1 * i:2 * W1 * (i + 1)], wqT[:, 2 * j + i, :],
                              wkT[:, 2 * j + i, :, :].rearrange("p s w -> p (s w)"), start=True, stop=True)
                end(f"A{j}", last)
            o = begin("G")
            pe.wait_ge(dma["wo"], 32)
            for i in range(4):
                last = mm(o[:, P * i:P * i + P], wvT[:, i, :, :].rearrange("p s w -> p (s w)"),
                          wo_sb[:, i, :, :].rearrange("p s w -> p (s w)"), start=True, stop=True)
            end("G", last)
            o = begin("yb")
            for s in range(2):
                for i in range(4):
                    for g in range(2):
                        last = mm(o[W * s:W * s + W, 0:1], wo_sb[:, i, g, :], bvT[:, i:i + 1],
                                  start=(i == 0 and g == 0), stop=(i == 3 and g == 1))
            end("yb", last)

            pe.wait_ge(dma["convw"], 48)
            for h in range(HALVES):
                pe.wait_ge(xT_ready, 4 * h + 4)
                for name in ("qv", "k"):
                    o = begin((name, h))
                    m = P if name == "qv" else W
                    for tap in range(TAPS):
                        for c in range(2):
                            w = convw_sb[:, tap, c, 0:P] if name == "qv" else convw_sb[:, tap, c, P:P + W]
                            last = mm(o[0:m, :].rearrange("p (n s) -> p n s", n=2), w,
                                      xT[:, c, 2 * h:2 * h + 2, tap:tap + S],
                                      start=(tap == 0 and c == 0), stop=(tap == TAPS - 1 and c == 1))
                    end((name, h), last)
            for h in range(HALVES):
                o = begin(("v", h))
                pe.wait_ge(qv_ready, 2 * h + 2)
                for i in range(TILES):
                    last = nc.tensor.transpose(o[:, W * i:W * i + W],
                                               vT_sb[W:P, NT * h + P * i:NT * h + P * (i + 1)], ident[W:P, W:P])
                end(("v", h), last)

            def t_products(h):
                pe.wait_ge(A_ready, 2)
                for i in range(H):
                    o = begin(("t", h, i))
                    end(("t", h, i), mm(o[0:W1, :], A_sb[:, i, :], q_sb[:, NT * h:NT * (h + 1)], start=True, stop=True))

            def scores(h):
                o = begin(("s", h))
                pe.wait_ge(ks_ready, 3 * h + 3)
                pe.wait_ge(tlo_ready, H * (h + 1))
                for j in range(NB):
                    g = NB * h + j
                    cols = slice(BLK * g, BLK * (g + 1))
                    th = t_hi[:, g, :, :].rearrange("p h q -> p (h q)")
                    tl = t_lo[:, g, :, :].rearrange("p h q -> p (h q)")
                    d = o[:, BLK * j:BLK * (j + 1)]
                    mm(d, th, k_hi[:, cols], start=True, stop=False)
                    mm(d, th, k_lo[:, cols], start=False, stop=False)
                    last = mm(d, tl, k_hi[:, cols], start=False, stop=True)
                end(("s", h), last)

            def attention_out(h):
                o = begin(("pT", h))
                pe.wait_ge(p_ready, h + 1)
                for i in range(TILES):
                    last = nc.tensor.transpose(o[:, P * i:P * i + P],
                                               s_sb[:, h, 8 * i:8 * i + 8, :].rearrange("p b k -> p (b k)"), ident[:, :])
                end(("pT", h), last)
                pe.wait_ge(pT_ready, h + 1)
                for i in range(TILES):
                    o = begin(("u", h, i))
                    pe.wait_ge(vbd_ready, 2 * (TILES * h + i + 1))
                    for c in range(4):
                        last = mm(o[:, P * c:P * c + P],
                                  v_bd[:, TILES * h + i, c, :, :].rearrange("p b w -> p (b w)"),
                                  pT_sb[:, h, i, :], start=True, stop=True)
                    end(("u", h, i), last)
                pe.wait_ge(G_ready, 2)
                o = begin(("y", h))
                pe.wait_ge(u_ready, TILES * (h + 1))
                for i in range(H):
                    last = mm(o[:, 0:NT // 2], G_sb[:, i, :, :].rearrange("p b w -> p (b w)"), u_sb[:, i, :],
                              start=(i == 0), stop=(i == H - 1))
                end(("y", h), last)
                pe.wait_ge(y_ready, h + 1)
                pe.wait_ge(dma["proj"], 32)
                for n in range(2):
                    o = begin(("proj", h, n))
                    end(("proj", h, n), mm(o[:, :], y_sb[:, h, P * n:P * n + P],
                                           proj_sb[:, :, :].rearrange("p b d -> p (b d)"), start=True, stop=True))

            def ff_transposes(i):
                name, j = FF[i]
                k = ("up", "gate", "down").index(name)
                o = begin(("ff", i))[:, :].bitcast(F16)
                pe.wait_ge(tern_ready, k + 1)
                for a in range(8):
                    if name == "down":
                        c, f = a % 2, 4 * j + a // 2
                        src = tern[:, 2, FE * c + P * f:FE * c + P * f + P]
                        dst = o[:, D * (a // 2) + P * c:D * (a // 2) + P * c + P]
                    else:
                        src = tern[:, k, D * a + P * j:D * a + P * j + P]
                        dst = o[:, P * a:P * a + P]
                    last = nc.tensor.transpose(dst, src, ident16[:, :])
                end(("ff", i), last)

            t_products(0)
            scores(0)
            for e in range(E):
                o = begin(("ctx", e))
                pe.wait_ge(dma["ctx"], 16)
                for c in range(2):
                    for r in range(2):
                        last = nc.tensor.transpose(o[:, D * c + P * r:D * c + P * r + P],
                                                   ctx_nat[:, e, r, P * c:P * c + P], ident[:, :])
                end(("ctx", e), last)
            o = begin("wsum")
            pe.wait_ge(acc_w, 3)
            end("wsum", mm(o[:, 0:3], ones[:, :], wsum[:, :], start=True, stop=True))
            t_products(1)
            scores(1)
            for h in range(HALVES):
                attention_out(h)
                pe.wait_ge(consts, 21)
                for i in range(3 * h, 3 * h + 3):
                    ff_transposes(i)

            def layer(name, h):
                outs = [begin((f"{name}_down", h, j)) for j in range(2)]

                def up(c):
                    if name == "x":
                        e, r = c // 2, c % 2
                        o = begin(("x_up", h, c))
                        pe.wait_ge(mhi_ready, E * h + e + 1)
                        pe.wait_ge(mlo_ready, 2 * (E * h + e + 1))
                        n = 0
                        for w, m in ((ctxT_hi, hm_hi), (ctxT_lo, hm_hi), (ctxT_hi, hm_lo)):
                            for k in range(2):
                                last = mm(o[:, :], w[:, k, e, P * r:P * r + P], m[:, e, k, :],
                                          start=(n == 0), stop=(n == 5))
                                n += 1
                        end(("x_up", h, c), last)
                    else:
                        for use, w in (("f_up", upT), ("f_gate", gateT)):
                            o = begin((use, h, c))
                            n = 0
                            for k in range(2):
                                for m in (hT_hi, hT_lo):
                                    last = mm(o[:, :], w[:, k, P * c:P * c + P], m[:, k, NT * h:NT * (h + 1)],
                                              start=(n == 0), stop=(n == 3))
                                    n += 1
                            end((use, h, c), last)

                def down(c):
                    k = 16 * (name == "f") + 8 * h + c
                    pe.wait_ge(hidlo_ready, k + 1)
                    for i in range(TILES):
                        o = outs[i // 2][:, D * (i % 2):D * (i % 2) + D]
                        tok = slice(P * i, P * i + P)
                        if name == "x":
                            e, cc = c // 2, c % 2
                            pairs = [(hid_hi, ctxT_hi[:, cc, e, :]), (hid_hi, ctxT_lo[:, cc, e, :]),
                                     (hid_lo, ctxT_hi[:, cc, e, :])]
                        else:
                            pairs = [(hid_hi, downT[:, c, :]), (hid_lo, downT[:, c, :])]
                        for n, (l, r) in enumerate(pairs):
                            last = mm(o, l[:, k % 3, tok], r, start=(c == 0 and n == 0 and i % 2 == 0),
                                      stop=(c == 7 and n == len(pairs) - 1), skip_group_check=True)
                        if c == 7 and i % 2:
                            end((f"{name}_down", h, i // 2), last)
                            last = None
                    if c < 7:
                        last.then_inc(down_done, 1)

                up(0)
                for c in range(8):
                    if c < 7:
                        up(c + 1)
                    down(c)

            transposes(2, 0)
            pe.wait_ge(hlo_ready, 2)
            pe.wait_ge(chi_ready, E)
            pe.wait_ge(clo_ready, E)
            layer("x", 0)
            transposes(2, 1)
            layer("x", 1)
            transposes(3, 0)
            pe.wait_ge(hlo_ready, 6)
            pe.wait_ge(ffT_ready, 6)
            layer("f", 0)
            transposes(3, 1)
            pe.wait_ge(hlo_ready, 8)
            layer("f", 1)


T_SCALE = 9
C_SCALE = 17
TERN = 35

_INS = [("x", "x"), ("ids", "itok_BxS_13_99985"), ("ctx", "ctx_2048"), ("conv_w", "L0_attn_conv_w"),
        ("conv_b", "L0_attn_conv_b"), ("wq", "L0_attn_wq"), ("bq", "L0_attn_bq"), ("wk", "L0_attn_wk"),
        ("bk", "L0_attn_bk"), ("wv", "L0_attn_wv"), ("bv", "L0_attn_bv"), ("wo", "L0_attn_wo"),
        ("bo", "L0_attn_bo"), ("proj_w", "L0_attn_proj_w"), ("proj_b", "L0_attn_proj_b"),
        ("w_up", "L0_ffn_W_up"), ("w_gate", "L0_ffn_W_gate"), ("w_down", "L0_ffn_W_down")]


def kernel(**inputs):
    import numpy as _np
    import concourse.bacc as _bacc
    from concourse import mybir as _mybir
    from concourse.bass_utils import run_bass_kernel_spmd as _run

    nc = _bacc.Bacc("TRN2", target_bir_lowering=False, num_devices=1)
    arrays, args = {}, []
    for short, name in _INS:
        a = _np.ascontiguousarray(inputs[name])
        arrays[f"in_{short}_dram"] = a
        args.append(nc.dram_tensor(f"in_{short}_dram", a.shape, _mybir.dt.from_np(a.dtype), kind="ExternalInput").ap())
    result = nc.dram_tensor("out_dram", (B, S, D), F32, kind="ExternalOutput").ap()
    decoder_kernel(nc, *args, result)
    r = _run(nc, [arrays], core_ids=[0])
    return r.results[0]["out_dram"]
```

```python
from contextlib import ExitStack

import concourse.bass as bass
from concourse import mybir

ALU = mybir.AluOpType
ACT = mybir.ActivationFunctionType
AX = mybir.AxisListType
F32 = mybir.dt.float32
F16 = mybir.dt.float16
I32 = mybir.dt.int32
U32 = mybir.dt.uint32
ADD_ALL = bass.bass_isa.ReduceOp.add
ABSMAX_ALL = bass.bass_isa.ReduceOp.absmax

P = 128
B, S, D = 4, 256, 256
TAPS = 3
W = 64
H = 8
BLK = 16
E = 4
FE = 1024
PER_EXPERT = 12500 // E
LN_EPS = 1e-5
Q_EPS = 1e-8
NEG = -1e9
EXPONENT = 0x7F800000

HALVES = 2
TILES = 4
NT = 512
NB = NT // BLK
LAG = 3
HID = 4
CHUNKS = 8
NX = HALVES * CHUNKS
MAGIC = 0x5F3759DF
W1 = W + 1


def plan_banks(uses):
    count, readers, out = {}, {}, {}
    for name, bank, read_by in uses:
        out[name] = (bank, count.get(bank, 0) + 1, readers.get(bank, []))
        count[bank] = count.get(bank, 0) + 1
        readers[bank] = read_by
    return out


def decoder_kernel(nc, x, ids, ctx_w, conv_w, conv_b, wq, bq, wk, bk, wv, bv, wo, bo,
                   proj_w, proj_b, w_up, w_gate, w_down, out):
    stack = ExitStack()
    with stack:
        def sb(name, shape, dt=F32):
            return stack.enter_context(nc.sbuf_tensor(name, shape, dt))

        def sem(name):
            return stack.enter_context(nc.semaphore(name))

        x_sb = sb("x_sb", [P, 8, D])
        ln_sb = sb("ln_sb", [P, 8, D])
        stats = sb("stats", [P, 8, 6])
        mv = sb("mv", [P, 8, 2])
        root = sb("root", [P, 3, 8])
        rstd = sb("rstd", [P, 8])
        ident = sb("ident", [P, P])
        ident16 = sb("ident16", [P, P], F16)
        ones = sb("ones", [P, P])
        key_ok = sb("key_ok", [P, H, BLK])
        causal = sb("causal", [P, BLK])
        blkmask = sb("blkmask", [P, 8])
        convw_sb = sb("convw_sb", [P, TAPS, 2, 3 * W])
        convb_sb = sb("convb_sb", [P, 2])
        wq_sb = sb("wq_sb", [W1, H * W])
        wk_sb = sb("wk_sb", [W1, H * W])
        wv_sb = sb("wv_sb", [W1, H * W])
        wqT = sb("wqT", [P, 4, W1])
        wkT = sb("wkT", [P, 4, 2, W1])
        wvT = sb("wvT", [P, 4, 2, W])
        bvT = sb("bvT", [P, 4])
        wo_sb = sb("wo_sb", [P, 4, 2, W])
        bo_sb = sb("bo_sb", [P, 1])
        proj_sb = sb("proj_sb", [P, 2, D])
        projb_sb = sb("projb_sb", [P, D])
        A_sb = sb("A_sb", [P, H, W1])
        G_sb = sb("G_sb", [P, H, 2, W])
        ybias = sb("ybias", [P, 1])
        ids_sb = sb("ids_sb", [P, 8 * P], I32)
        mask = sb("mask", [P, E, 8 * P], F16)
        up_nat = sb("up_nat", [P, 8, D])
        gate_nat = sb("gate_nat", [P, 8, D])
        down_nat = sb("down_nat", [P, 2, FE])
        tern = sb("tern", [P, 3, FE * 2], F16)
        upT = sb("upT", [P, 2, FE], F16)
        gateT = sb("gateT", [P, 2, FE], F16)
        downT = sb("downT", [P, 8, D], F16)
        ctx_nat = sb("ctx_nat", [P, E, 2, D])
        ctxT_hi = sb("ctxT_hi", [P, 2, E, D], F16)
        ctxT_lo = sb("ctxT_lo", [P, 2, E, D], F16)
        maxes = sb("maxes", [P, 4])
        allmax = sb("allmax", [P, 4])
        wsum = sb("wsum", [P, 3])
        sc = sb("sc", [P, 40])
        xT = sb("xT", [P, 2, B, S + 2])
        q_sb = sb("q_sb", [P, B * S])
        k_sb = sb("k_sb", [W, B * S])
        vT_sb = sb("vT_sb", [P, B * S])
        k_hi = sb("k_hi", [W1, B * S], F16)
        k_lo = sb("k_lo", [W1, B * S], F16)
        t_hi_st = sb("t_hi_st", [P, 2 * NB * P], F16)
        t_lo_st = sb("t_lo_st", [P, 2 * NB * P], F16)
        t_hi = t_hi_st[0:W1, :].rearrange("p (b h q) -> p b h q", h=H, q=BLK)
        t_lo = t_lo_st[0:W1, :].rearrange("p (b h q) -> p b h q", h=H, q=BLK)
        s_sb = sb("s_sb", [P, HALVES, NB, BLK])
        smax = sb("smax", [P, HALVES, NB])
        ssum = sb("ssum", [P, HALVES, NB])
        rsum = sb("rsum", [P, HALVES, NB])
        pT_sb = sb("pT_sb", [P, HALVES, TILES, P])
        v_tok = sb("v_tok", [P, HALVES, TILES, W])
        v_bd = sb("v_bd", [P, 8, 4, 2, W])

        t_lo_all = t_lo_st[:, :]
        hm_hi = [None, None]
        hm_lo = [None, None]
        hm_hi[0] = t_lo_all[:, 0:4096].rearrange("p (e c n) -> p e c n", e=E, c=2)
        hm_lo[0] = t_lo_all[:, 4096:8192].rearrange("p (e c n) -> p e c n", e=E, c=2)
        hm_hi[1] = up_nat[:, :, :].rearrange("p a b -> p (a b)").bitcast(F16).rearrange(
            "p (e c n) -> p e c n", e=E, c=2)
        hm_lo[1] = gate_nat[:, :, :].rearrange("p a b -> p (a b)").bitcast(F16).rearrange(
            "p (e c n) -> p e c n", e=E, c=2)
        t_hi_all = t_hi_st[:, :]
        hT_hi = t_hi_all[:, 0:2048].rearrange("p (c n) -> p c n", c=2)
        hT_lo = t_hi_all[:, 2048:4096].rearrange("p (c n) -> p c n", c=2)
        silu_sb = t_hi_all[:, 4096:6144].bitcast(F32).rearrange("p (s n) -> p s n", s=2)
        y_sb = sb("y_sb", [P, HALVES, NT // 2])
        v_all = v_bd[:, :, :, :, :].rearrange("p i c b w -> p (i c b w)")
        hid = v_all[:, 0:2048].rearrange("p (s n) -> p s n", s=HID)
        hid_hi = v_all[:, 2048:3072].bitcast(F16).rearrange("p (s n) -> p s n", s=HID)
        hid_lo = v_all[:, 3072:4096].bitcast(F16).rearrange("p (s n) -> p s n", s=HID)
        x_nat = v_all[:, 0:2048].rearrange("p (i d) -> p i d", i=8)
        u_sb = xT[:, :, :, :].rearrange("p c n s -> p (c n s)")[:, 0:H * NT // 2].rearrange("p (h n) -> p h n", h=H)

        bank = [stack.enter_context(nc.psum_tensor(f"bank{i}", [P, 512], F32)) for i in range(8)]

        names = ["bound", "bound1", "pow_b", "inv_b", "one_k", "amax", "pow_a", "inv_a", "t_ab", "t_scale",
                 "f_ab", "f_scale", "cmax", "pow_c", "inv_c", "c_scale", "silu_x", "hid_x", "c2", "y_x",
                 "m0", "m1", "m2", "h0", "h1", "h2", "n0", "n1", "n2", "silu_f", "inv_u", "hid_f",
                 "sg", "y_f", "kb"]
        col = {n: sc[:, i:i + 1] for i, n in enumerate(names)}

        dma = {n: sem("loaded_" + n) for n in
               ["n0", "n1", "x0", "x1", "convw", "convb", "wq", "wk", "wv", "wo", "bo", "proj", "projb", "up", "gate",
                "down", "ctx", "ids"]}
        written = [sem(f"bank{i}_written") for i in range(8)]
        consts = sem("consts")
        acc_w = sem("acc_w")
        mxs = sem("mxs")
        allm = sem("allm")
        scal = sem("scal")
        xb_ready = sem("xb_ready")
        wT_ready = sem("wT_ready")
        A_ready = sem("A_ready")
        G_ready = sem("G_ready")
        yb_ready = sem("yb_ready")
        dve_ln = sem("dve_ln")
        ln_seed = sem("ln_seed")
        newton = sem("newton")
        ln_done = sem("ln_done")
        xT_ready = sem("xT_ready")
        kv_ready = sem("kv_ready")
        q_ready = sem("q_ready")
        ks_ready = sem("ks_ready")
        vtok_ready = sem("vtok_ready")
        vbd_ready = sem("vbd_ready")
        thi_ready = sem("thi_ready")
        tlo_ready = sem("tlo_ready")
        sm = sem("sm")
        exp_ready = sem("exp_ready")
        p_ready = sem("p_ready")
        pT_ready = sem("pT_ready")
        u_ready = sem("u_ready")
        y_ready = sem("y_ready")
        x1_ready = sem("x1_ready")
        chi_ready = sem("chi_ready")
        clo_ready = sem("clo_ready")
        mask_ready = sem("mask_ready")
        tlow_ready = sem("tlow_ready")
        tern_ready = sem("tern_ready")
        ffT_ready = sem("ffT_ready")
        hhi_ready = sem("hhi_ready")
        hlo_ready = sem("hlo_ready")
        mhi_ready = sem("mhi_ready")
        mlo_ready = sem("mlo_ready")
        silu_ready = sem("silu_ready")
        hid_ready = sem("hid_ready")
        hidhi_ready = sem("hidhi_ready")
        hidlo_ready = sem("hidlo_ready")
        x2_ready = sem("x2_ready")
        stored = sem("stored")
        down_used = sem("down_used")
        down_done = sem("down_done")
        dve_set = sem("dve_set")
        mlo0_ready = sem("mlo0_ready")

        def read_t(h, i):
            return [(thi_ready, H * h + i + 1), (tlo_ready, H * h + i + 1)]

        uses = [("wqT", 0, [(wT_ready, 1)]), ("wkT", 1, [(wT_ready, 3)]), ("wvT", 2, [(wT_ready, 6)])]
        uses += [(("tr1", 0, c), 6 + c, [(xT_ready, c + 1)]) for c in range(2)]
        uses += [("A0", 3, [(A_ready, 1)]), ("A1", 4, [(A_ready, 2)]), ("G", 5, [(G_ready, 2)]),
                 ("yb", 2, [(yb_ready, 1)])]
        uses += [(("tr1", 1, c), 6 + c, [(xT_ready, c + 3)]) for c in range(2)]
        uses += [(("kv", 0), 0, [(kv_ready, 2)]), (("q", 0), 1, [(q_ready, 1)]), (("kv", 1), 2, [(kv_ready, 4)])]
        uses += [(("t", 0, i), 3 + i % 4, read_t(0, i)) for i in range(H)]
        uses += [(("q", 1), 7, [(q_ready, 2)]), (("s", 0), 0, [(sm, 1)])]
        uses += [(("v", h), 1 + h, [(vtok_ready, h + 1)]) for h in range(HALVES)]
        uses += [("wsum", 7, [(scal, WMEAN)])]
        uses += [(("t", 1, i), 3 + i % 4, read_t(1, i)) for i in range(H)]
        uses += [(("ctx", e), (7, 2)[e % 2], [(chi_ready, e + 1), (clo_ready, e + 1)]) for e in range(E)]
        uses += [(("pT", 0), 0, [(pT_ready, 1)]), (("s", 1), 1, [(sm, 6)])]
        uses += [(("u", 0, i), 3 + i, [(u_ready, i + 1)]) for i in range(TILES)]
        uses += [(("y", 0), 7, [(y_ready, 1)]), (("pT", 1), 0, [(pT_ready, 2)])]
        uses += [(("proj", 0, n), 1 + n, [(x1_ready, n + 1)]) for n in range(2)]
        uses += [(("u", 1, i), 3 + i, [(u_ready, TILES + i + 1)]) for i in range(TILES)]
        uses += [(("y", 1), 7, [(y_ready, 2)])]

        def ln_uses(which, h, first):
            k = HALVES * (which - 2) + h
            return [((f"tr{which}", h, c), first + c, [(hhi_ready, 2 * k + c + 1), (hlo_ready, 2 * k + c + 1)])
                    for c in range(2)]

        uses += ln_uses(2, 0, 4)
        uses += [(("proj", 1, n), 6 + n, [(x1_ready, 2 + n + 1)]) for n in range(2)]
        FF = [("up", 0), ("up", 1), ("gate", 0), ("gate", 1), ("down", 0), ("down", 1)]
        for k in range(2 * NX):
            if k < NX:
                uses += [(("up", k), k % 4, [(silu_ready, k + 1), (hid_ready, k + 1)])]
            else:
                uses += [(("up", k), 2 * (k % 2), [(silu_ready, k + 1)]),
                         (("gate", k), 2 * (k % 2) + 1, [(hid_ready, k + 1)])]
            if k == TR2:
                uses += ln_uses(2, 1, 6)
            if k in FF_AT:
                uses += [(("ff", i), 6 + i % 2, [(ffT_ready, i + 1)]) for i in FF_AT[k]]
            if k == TR3:
                uses += ln_uses(3, 0, 4)
            if k == TR3 + CHUNKS:
                uses += ln_uses(3, 1, 6)
            if k >= LAG and (k - LAG) % CHUNKS == 0:
                n = (k - LAG) // CHUNKS
                uses += [(("down", n, j), 4 + 2 * (n % 2) + j, [(down_used, 4 * n + 2 * j + 2)]) for j in range(2)]
        plan = plan_banks(uses)

        def filled(eng, name):
            b, n, _ = plan[name]
            eng.wait_ge(written[b], n)
            return bank[b]

        def down_read(eng, k):
            if k % CHUNKS == CHUNKS - 1:
                filled(eng, ("down", k // CHUNKS, 1))
            else:
                eng.wait_ge(down_done, (CHUNKS - 1) * (k // CHUNKS) + k % CHUNKS + 1)

        block = stack.enter_context(nc.Block())

        @block.sync
        def _(sp):
            xnat = x.rearrange("n (t p) d -> p (n t) d", p=P)
            for h in range(HALVES):
                sp.dma_start(x_nat[:, TILES * h:TILES * (h + 1), :],
                             xnat[:, TILES * h:TILES * (h + 1), :]).then_inc(dma[f"n{h}"], 16)
            sp.dma_start(convb_sb[:, 0:1], conv_b[W:3 * W].unsqueeze(1)).then_inc(dma["convb"], 16)
            sp.dma_start(convb_sb[0:W, 1:2], conv_b[0:W].unsqueeze(1)).then_inc(dma["convb"], 16)
            sp.dma_start(up_nat[:, :, :], w_up.rearrange("(c p) d -> p c d", p=P)).then_inc(dma["up"], 16)
            sp.dma_start(gate_nat[:, :, :], w_gate.rearrange("(c p) d -> p c d", p=P)).then_inc(dma["gate"], 16)
            sp.dma_start(down_nat[:, :, :], w_down.rearrange("(c p) d -> p c d", p=P)).then_inc(dma["down"], 16)
            sp.dma_start(ctx_nat[:, :, :, :], ctx_w.rearrange("e (c p) d -> p e c d", p=P)).then_inc(dma["ctx"], 16)
            sp.wait_ge(dve_set, 4)
            for s in range(2):
                sp.dma_start(wo_sb[W * s:W * s + W, :, s, :],
                             wo.rearrange("(i s) k o -> s k i o", s=2)[s]).then_inc(dma["wo"], 16)
                sp.dma_start(bo_sb[W * s:W * s + W, :], bo.unsqueeze(1)).then_inc(dma["bo"], 16)
                sp.dma_start(proj_sb[W * s:W * s + W, s, :], proj_w).then_inc(dma["proj"], 16)
            sp.dma_start(projb_sb[:, :], proj_b.partition_broadcast(P)).then_inc(dma["projb"], 16)
            xin = x.rearrange("n (t b r) d -> t r n b d", t=2, b=2)
            for h in range(HALVES):
                dst = x_sb[:, TILES * h:TILES * (h + 1), :].rearrange("p (n b) d -> p n b d", n=2)
                for n in range(2):
                    for t in range(2):
                        sp.dma_start(dst[64 * t:64 * t + 64, n], xin[t, :, 2 * h + n]).then_inc(dma["x0"], 16)
            for n in range(B):
                src = ids[n].rearrange("(t b r) -> b t r", t=2, b=2)
                for b in range(2):
                    sp.dma_start(ids_sb[:, S * n + P * b:S * n + P * (b + 1)].rearrange("p (t r) -> p t r", t=2),
                                 src[b].partition_broadcast(P)).then_inc(dma["ids"], 16)
            xout = out.rearrange("n (t b r) d -> t r n b d", t=2, b=2)
            for h in range(HALVES):
                sp.wait_ge(down_used, 8 + 4 * h + 4)
                src = x_sb[:, TILES * h:TILES * (h + 1), :].rearrange("p (n b) d -> p n b d", n=2)
                for n in range(2):
                    for t in range(2):
                        sp.dma_start(xout[t, :, 2 * h + n], src[64 * t:64 * t + 64, n]).then_inc(stored, 16)
            sp.wait_ge(stored, 16 * 4 * HALVES)

        @block.gpsimd
        def _(pool):
            built = 0

            def const(ins):
                nonlocal built
                built += 1
                ins.then_inc(consts, 1)
                pool.wait_ge(consts, built)

            const(nc.gpsimd.memset(ident[:, :], 0.0))
            const(nc.gpsimd.affine_select(out=ident[:, :], in_=ident[:, :], compare_op=ALU.not_equal, fill=1.0,
                                          base=0, pattern=[[-1, P]], channel_multiplier=1))
            const(nc.gpsimd.memset(key_ok[:, :, :], 1.0))
            const(nc.gpsimd.affine_select(out=key_ok[:, :, :], in_=key_ok[:, :, :], compare_op=ALU.is_ge, fill=0.0,
                                          base=0, pattern=[[-BLK, H], [-1, BLK]], channel_multiplier=1))
            const(nc.gpsimd.affine_select(out=key_ok[:, :, :], in_=key_ok[:, :, :], compare_op=ALU.is_ge, fill=0.0,
                                          base=BLK - 1, pattern=[[BLK, H], [0, BLK]], channel_multiplier=-1))
            const(nc.gpsimd.memset(blkmask[:, :], 1.0))
            const(nc.gpsimd.affine_select(out=blkmask[:, :], in_=blkmask[:, :], compare_op=ALU.is_ge, fill=0.0,
                                          base=0, pattern=[[-BLK, 8]], channel_multiplier=1))
            const(nc.gpsimd.affine_select(out=blkmask[:, :], in_=blkmask[:, :], compare_op=ALU.is_ge, fill=0.0,
                                          base=BLK - 1, pattern=[[BLK, 8]], channel_multiplier=-1))
            const(nc.gpsimd.tensor_copy(ident16[:, :], ident[:, :]))

            steps = 0

            def inverse_root(k):
                nonlocal steps
                tiles = slice(TILES * (k % 2), TILES * (k % 2 + 1))
                v, y, a = (root[:, j, tiles] for j in range(3))
                pool.wait_ge(ln_seed, 3 * (k + 1))

                def step(ins):
                    nonlocal steps
                    steps += 1
                    ins.then_inc(newton, 1)
                    if steps % NEWTON:
                        pool.wait_ge(newton, steps)
                for n in range(3):
                    step(nc.gpsimd.tensor_tensor(a, y, y, ALU.mult))
                    step(nc.gpsimd.tensor_tensor(a, a, v, ALU.mult))
                    step(nc.gpsimd.tensor_scalar(a, a, -0.5, 1.5, ALU.mult, ALU.add))
                    step(nc.gpsimd.tensor_tensor(y if n < 2 else rstd[:, tiles], y, a, ALU.mult))

            inverse_root(0)
            inverse_root(1)
            pool.wait_ge(mxs, 2)
            nc.gpsimd.partition_all_reduce(allmax[:, 0:2], maxes[:, 0:2], P, ABSMAX_ALL).then_inc(allm, 1)
            pool.wait_ge(mxs, 3)
            nc.gpsimd.partition_all_reduce(allmax[:, 3:4], maxes[:, 3:4], P, ABSMAX_ALL).then_inc(allm, 1)
            pool.wait_ge(mxs, 4)
            nc.gpsimd.partition_all_reduce(allmax[:, 2:3], maxes[:, 2:3], P, ABSMAX_ALL).then_inc(allm, 1)

            def spread_v(h):
                m = blkmask[:, :].rearrange("p (b c) -> p c b", b=2).unsqueeze(3).to_broadcast([P, 4, 2, W])
                pool.wait_ge(vtok_ready, h + 1)
                for i in range(TILES):
                    for b in range(2):
                        v = v_tok[:, h, i, :].unsqueeze(1).to_broadcast([P, 4, W])
                        nc.gpsimd.tensor_tensor(v_bd[:, TILES * h + i, :, b, :], v, m[:, :, b, :],
                                                ALU.mult).then_inc(vbd_ready, 1)

            def negative(i):
                w_nat = (up_nat, gate_nat, down_nat)[i]
                pool.wait_ge(scal, TERN)
                nc.gpsimd.tensor_scalar(tern[:, i, :], w_nat[:, :, :].rearrange("p a b -> p (a b)"),
                                        col[f"n{i}"], None, ALU.is_lt).then_inc(tlow_ready, 1)

            pool.wait_ge(ln_done, 8)
            spread_v(0)
            spread_v(1)
            pool.wait_ge(dma["projb"], 16)
            pool.wait_ge(dma["x0"], 16 * 8)
            nc.gpsimd.tensor_tensor(x_sb[:, :, :], x_sb[:, :, :],
                                    projb_sb[:, :].unsqueeze(1).to_broadcast([P, 8, D]), ALU.add).then_inc(xb_ready, 1)
            negative(0)
            negative(1)
            inverse_root(2)
            negative(2)

            def mask_low(h):
                half = slice(NT * h, NT * (h + 1))
                pool.wait_ge(hlo_ready, 2 * h + 2)
                for e in range(1, E):
                    for c in range(2):
                        nc.gpsimd.tensor_tensor(hm_lo[h][:, e, c, :], hT_lo[:, c, half], mask[:, e, half],
                                                ALU.mult).then_inc(mlo_ready, 1)

            pool.wait_ge(mask_ready, 6)
            mask_low(0)
            inverse_root(3)
            pool.wait_ge(tern_ready, 2)
            mask_low(1)
            inverse_root(4)
            inverse_root(5)

        @block.scalar
        def _(act):
            act.dma_start(convw_sb[:, :, :, :], conv_w.rearrange("t (c p) f -> p t c f", p=P)).then_inc(dma["convw"], 16)
            for name, dst, wsrc, bsrc in (("wq", wq_sb, wq, bq), ("wk", wk_sb, wk, bk), ("wv", wv_sb, wv, bv)):
                act.dma_start(dst[0:W, :], wsrc.rearrange("d h k -> d (h k)")).then_inc(dma[name], 16)
                act.dma_start(dst[W:W1, :], bsrc.rearrange("h k -> (h k)").unsqueeze(0)).then_inc(dma[name], 16)

            act.wait_ge(dve_set, 1)
            for h in range(HALVES):
                for c in range(2):
                    src = filled(act, ("tr1", h, c))[:, :].rearrange("p (n s) -> p n s", n=2)
                    nc.scalar.activation(xT[:, c, 2 * h:2 * h + 2, 2:], src, ACT.Copy).then_inc(xT_ready, 1)

            def keys_values(h):
                half = slice(NT * h, NT * (h + 1))
                src = filled(act, ("kv", h))
                nc.scalar.activation(k_sb[:, half], src[0:W, :], ACT.Identity,
                                     bias=convb_sb[0:W, 0:1]).then_inc(kv_ready, 1)
                nc.scalar.activation(vT_sb[W:P, half], src[W:P, :], ACT.Identity,
                                     bias=convb_sb[W:P, 0:1]).then_inc(kv_ready, 1)

            def queries(h):
                src = filled(act, ("q", h))
                nc.scalar.activation(q_sb[0:W, NT * h:NT * (h + 1)], src[0:W, :], ACT.Identity,
                                     bias=convb_sb[0:W, 1:2]).then_inc(q_ready, 1)

            def value_tokens(h):
                src = filled(act, ("v", h))
                nc.scalar.activation(v_tok[:, h, :, :], src[:, 0:TILES * W].rearrange("p (i w) -> p i w", w=W),
                                     ACT.Copy).then_inc(vtok_ready, 1)

            def t_high(h, heads):
                for i in heads:
                    src = filled(act, ("t", h, i))[0:W1, :].rearrange("p (b q) -> p b q", q=BLK)
                    nc.scalar.activation(t_hi[:, NB * h:NB * (h + 1), i, :], src, ACT.Copy,
                                         scale=col["t_scale"][0:W1]).then_inc(thi_ready, 1)

            def softmax_exp(h):
                act.wait_ge(sm, 5 * h + 3)
                nc.scalar.activation(s_sb[:, h], s_sb[:, h], ACT.Exp).then_inc(exp_ready, 1)

            def transposed_p(h):
                src = filled(act, ("pT", h))
                nc.scalar.activation(pT_sb[:, h], src[:, :].rearrange("p (i m) -> p i m", m=P),
                                     ACT.Copy).then_inc(pT_ready, 1)

            def mixed_values(h):
                if h:
                    filled(act, ("y", h - 1))
                for i in range(TILES):
                    src = filled(act, ("u", h, i))[:, :].rearrange("p (c h q) -> p h c q", c=4, h=H)
                    nc.scalar.activation(u_sb[:, :, 64 * i:64 * i + 64].rearrange("p h (c q) -> p h c q", c=4),
                                         src, ACT.Copy).then_inc(u_ready, 1)

            def heads_out(h):
                src = filled(act, ("y", h))
                nc.scalar.activation(y_sb[:, h], src[:, 0:NT // 2], ACT.Identity, bias=ybias[:, :]).then_inc(y_ready, 1)

            act.wait_ge(dma["convb"], 32)
            keys_values(0)
            queries(0)
            for i, (name, w_nat) in enumerate((("up", up_nat), ("gate", gate_nat), ("down", down_nat))):
                act.wait_ge(dma[name], 16)
                nc.scalar.activation(tern[:, i, :], w_nat[:, :, :].rearrange("p a b -> p (a b)"), ACT.Abs,
                                     accum_out=wsum[:, i:i + 1]).then_inc(acc_w, 1)
                if i == 0:
                    keys_values(1)
                    act.wait_ge(scal, T_SCALE)
                    t_high(0, range(H))
                    queries(1)
            for h in range(HALVES):
                value_tokens(h)
            t_high(1, range(0, 4))
            softmax_exp(0)
            t_high(1, range(4, H))
            act.wait_ge(scal, C_SCALE)
            for e in range(E):
                src = filled(act, ("ctx", e))[:, :].rearrange("p (c r) -> p c r", c=2)
                nc.scalar.activation(ctxT_hi[:, :, e, :], src, ACT.Copy, scale=col["c_scale"]).then_inc(chi_ready, 1)
            transposed_p(0)
            softmax_exp(1)
            mixed_values(0)
            act.wait_ge(yb_ready, 1)
            heads_out(0)
            transposed_p(1)
            mixed_values(1)
            heads_out(1)

            def ln_high(which, h):
                if which == 3:
                    act.wait_ge(mhi_ready, E * (h + 1))
                for c in range(2):
                    src = filled(act, (f"tr{which}", h, c))
                    nc.scalar.activation(hT_hi[:, c, NT * h:NT * (h + 1)], src[:, :], ACT.Copy,
                                         scale=2048.0).then_inc(hhi_ready, 1)

            def ff_evac(i):
                name, j = FF[i]
                src = filled(act, ("ff", i))[:, :].bitcast(F16)
                dst = {"up": upT, "gate": gateT}.get(name)
                dst = dst[:, j, :] if dst is not None else downT[:, 4 * j:4 * j + 4, :]
                if name == "down":
                    src = src.rearrange("p (c d) -> p c d", d=D)
                nc.scalar.activation(dst, src, ACT.Copy).then_inc(ffT_ready, 1)

            def hid_high(k):
                act.wait_ge(hid_ready, k + 1)
                if k >= HID:
                    down_read(act, k - HID)
                nc.scalar.activation(hid_hi[:, k % HID, :], hid[:, k % HID, :], ACT.Copy).then_inc(hidhi_ready, 1)

            ln_high(2, 0)
            for k in range(2 * NX):
                if k == NX:
                    act.wait_ge(scal, TERN)
                src = filled(act, ("up", k))
                if k >= 2:
                    act.wait_ge(hid_ready, k - 1)
                nc.scalar.activation(silu_sb[:, k % 2, :], src[:, :], ACT.Silu,
                                     scale=col["silu_x" if k < NX else "silu_f"]).then_inc(silu_ready, 1)
                if k:
                    hid_high(k - 1)
                if k == TR2:
                    ln_high(2, 1)
                for i in FF_AT.get(k, ()):
                    ff_evac(i)
                if k in (TR3, TR3 + CHUNKS):
                    ln_high(3, (k - TR3) // CHUNKS)
            hid_high(2 * NX - 1)

        @block.vector
        def _(dve):
            nc.vector.memset(xT[:, :, :, 0:2], 0.0).then_inc(dve_set, 1)
            nc.vector.memset(convb_sb[W:P, 1:2], 0.0).then_inc(dve_set, 1)
            nc.vector.memset(wo_sb[:, :, :, :], 0.0).then_inc(dve_set, 1)
            nc.vector.memset(proj_sb[:, :, :], 0.0).then_inc(dve_set, 1)
            nc.vector.memset(wkT[:, :, :, :], 0.0).then_inc(dve_set, 1)
            nc.vector.memset(A_sb[W:P, :, :], 0.0).then_inc(dve_set, 1)
            nc.vector.memset(q_sb[W:P, :], 0.0).then_inc(dve_set, 1)
            nc.vector.memset(G_sb[:, :, :, :], 0.0).then_inc(dve_set, 1)
            nc.vector.memset(ones[:, :], 1.0).then_inc(dve_set, 1)
            nc.vector.memset(k_lo[W:W1, :], 0.0).then_inc(dve_set, 1)
            dve.wait_ge(dve_set, 7)
            nc.vector.memset(q_sb[W:W1, :], 1.0).then_inc(dve_set, 1)

            def stats_of(k, x_of):
                tiles = slice(TILES * (k % 2), TILES * (k % 2 + 1))
                for i in range(TILES):
                    T = TILES * (k % 2) + i
                    nc.vector.bn_stats(stats[:, T, :], x_of[:, T, :]).then_inc(dve_ln, 1)
                for i in range(TILES):
                    T = TILES * (k % 2) + i
                    dve.wait_ge(dve_ln, 8 * k + i + 1)
                    nc.vector.bn_aggr(mv[:, T, :], stats[:, T, :]).then_inc(dve_ln, 1)
                dve.wait_ge(dve_ln, 8 * (k + 1))
                if k >= 2:
                    dve.wait_ge(newton, NEWTON * (k - 1))
                v, y = root[:, 0, tiles], root[:, 1, tiles]
                nc.vector.tensor_scalar_add(v, mv[:, tiles, 1], LN_EPS).then_inc(ln_seed, 1)
                dve.wait_ge(ln_seed, 3 * k + 1)
                nc.vector.tensor_single_scalar(y.bitcast(U32), v.bitcast(U32), 1,
                                               ALU.logical_shift_right).then_inc(ln_seed, 1)
                dve.wait_ge(ln_seed, 3 * k + 2)
                nc.vector.tensor_scalar(y.bitcast(I32), y.bitcast(I32), -1.0, float(MAGIC), ALU.mult,
                                        ALU.add).then_inc(ln_seed, 1)

            def normalise(k, x_of):
                dve.wait_ge(newton, NEWTON * (k + 1))
                if k >= 2:
                    for c in range(2):
                        filled(dve, (f"tr{k // 2}", k % 2, c))
                for i in range(TILES):
                    T = TILES * (k % 2) + i
                    nc.vector.tensor_scalar(ln_sb[:, T, :], x_of[:, T, :], mv[:, T, 0:1], rstd[:, T:T + 1],
                                            ALU.subtract, ALU.mult).then_inc(ln_done, 1)

            step = 0

            def scalar(ins):
                nonlocal step
                step += 1
                ins.then_inc(scal, 1)
                dve.wait_ge(scal, step)

            ts = nc.vector.tensor_scalar
            dve.wait_ge(dma["n0"], 16)
            stats_of(0, x_nat)
            dve.wait_ge(dma["n1"], 16)
            stats_of(1, x_nat)
            normalise(0, x_nat)
            normalise(1, x_nat)

            src = filled(dve, "wqT")[:, 0:4 * W1].rearrange("p (i w) -> p i w", w=W1)
            nc.vector.tensor_copy(wqT[:, :, :], src).then_inc(wT_ready, 1)
            dve.wait_ge(dve_set, 11)
            src = filled(dve, "wkT")[:, 0:4 * W1].rearrange("p (i w) -> p i w", w=W1)
            for s in range(2):
                rows = slice(W * s, W * s + W)
                nc.vector.tensor_copy(wkT[rows, :, s, :], src[rows]).then_inc(wT_ready, 1)
            src = filled(dve, "wvT")[:, 0:4 * W1].rearrange("p (i w) -> p i w", w=W1)
            for s in range(2):
                nc.vector.tensor_copy(wvT[:, :, s, :], src[:, :, 0:W]).then_inc(wT_ready, 1)
            nc.vector.tensor_copy(bvT[:, :], src[:, :, W]).then_inc(wT_ready, 1)
            for j in range(2):
                src = filled(dve, f"A{j}")[0:W1, 0:4 * W1].rearrange("p (i w) -> p i w", w=W1)
                nc.vector.tensor_copy(A_sb[0:W1, 4 * j:4 * j + 4, :], src).then_inc(A_ready, 1)
            dve.wait_ge(dma["convw"], 16)
            nc.vector.tensor_reduce(maxes[:, 0:1], convw_sb[:, :, :, :].rearrange("p a b c -> p (a b c)"), AX.X,
                                    ALU.max, apply_absolute_value=True).then_inc(mxs, 1)
            dve.wait_ge(dma["convb"], 32)
            nc.vector.tensor_reduce(maxes[:, 1:2], convb_sb[:, :], AX.X, ALU.max,
                                    apply_absolute_value=True).then_inc(mxs, 1)
            dve.wait_ge(A_ready, 2)
            nc.vector.tensor_reduce(maxes[:, 3:4], A_sb[:, :, :].rearrange("p h w -> p (h w)"), AX.X, ALU.max,
                                    apply_absolute_value=True).then_inc(mxs, 1)
            src = filled(dve, "G")[:, :].rearrange("p (h w) -> p h w", w=W)
            for s in range(2):
                rows = slice(W * s, W * s + W)
                nc.vector.tensor_copy(G_sb[rows, :, s, :], src[rows]).then_inc(G_ready, 1)
            dve.wait_ge(dma["bo"], 32)
            src = filled(dve, "yb")
            nc.vector.tensor_tensor(ybias[:, :], src[:, 0:1], bo_sb[:, :], ALU.add).then_inc(yb_ready, 1)
            dve.wait_ge(allm, 1)
            bound = float(TAPS * D)
            scalar(nc.vector.scalar_tensor_tensor(col["bound"], allmax[:, 0:1], bound, allmax[:, 1:2],
                                                  ALU.mult, ALU.add))
            scalar(nc.vector.tensor_scalar_add(col["bound1"], col["bound"], 1.0))
            scalar(nc.vector.tensor_single_scalar(col["pow_b"].bitcast(U32), col["bound1"].bitcast(U32), EXPONENT,
                                                  ALU.bitwise_and))
            scalar(nc.vector.reciprocal(col["inv_b"], col["pow_b"]))
            scalar(ts(col["one_k"], col["inv_b"], 2.0 ** 14, None, ALU.mult))
            dve.wait_ge(allm, 2)
            scalar(ts(col["amax"], allmax[:, 3:4], 1e-30, None, ALU.max))
            scalar(nc.vector.tensor_single_scalar(col["pow_a"].bitcast(U32), col["amax"].bitcast(U32), EXPONENT,
                                                  ALU.bitwise_and))
            scalar(nc.vector.reciprocal(col["inv_a"], col["pow_a"]))
            scalar(ts(col["t_scale"], col["inv_a"], col["inv_b"], 2.0 ** 6, ALU.mult, ALU.mult))
            assert step == T_SCALE
            scalar(ts(col["f_ab"], col["pow_a"], col["pow_b"], 2.0 ** -23, ALU.mult, ALU.mult))
            scalar(ts(col["f_scale"], col["f_ab"], col["pow_b"], None, ALU.mult))
            dve.wait_ge(consts, 5)
            scalar(nc.vector.tensor_reduce(causal[:, :], key_ok[:, :, :].rearrange("p h k -> p k h"), AX.X, ALU.add))
            scalar(ts(causal[:, :], causal[:, :], 1.0, -NEG, ALU.subtract, ALU.mult))

            def k_split(h):
                half = slice(NT * h, NT * (h + 1))
                dve.wait_ge(kv_ready, 2 * h + 1)
                ts(k_hi[0:W, half], k_sb[:, half], col["one_k"][0:W], None, ALU.mult).then_inc(ks_ready, 1)
                dve.wait_ge(ks_ready, 3 * h + 1)
                nc.vector.scalar_tensor_tensor(k_lo[0:W, half], k_sb[:, half], col["one_k"][0:W], k_hi[0:W, half],
                                               ALU.mult, ALU.subtract).then_inc(ks_ready, 1)
                ts(k_hi[W:W1, half], q_sb[W:W1, half], col["one_k"][W:W1], None, ALU.mult).then_inc(ks_ready, 1)

            def t_low(h, heads):
                for i in heads:
                    src = filled(dve, ("t", h, i))[0:W1, :].rearrange("p (b q) -> p b q", q=BLK)
                    dve.wait_ge(thi_ready, H * h + i + 1)
                    nc.vector.scalar_tensor_tensor(t_lo[:, NB * h:NB * (h + 1), i, :], src, col["t_scale"][0:W1],
                                                   t_hi[:, NB * h:NB * (h + 1), i, :], ALU.mult,
                                                   ALU.subtract).then_inc(tlo_ready, 1)

            def softmax_in(h):
                src = filled(dve, ("s", h))[:, :].rearrange("p (b k) -> p b k", k=BLK)
                nc.vector.scalar_tensor_tensor(s_sb[:, h], src, col["f_scale"],
                                               causal[:, :].unsqueeze(1).to_broadcast([P, NB, BLK]),
                                               ALU.mult, ALU.add).then_inc(sm, 1)
                dve.wait_ge(sm, 5 * h + 1)
                nc.vector.tensor_reduce(smax[:, h], s_sb[:, h], AX.X, ALU.max).then_inc(sm, 1)
                dve.wait_ge(sm, 5 * h + 2)
                nc.vector.tensor_tensor(s_sb[:, h], s_sb[:, h], smax[:, h].unsqueeze(2).to_broadcast([P, NB, BLK]),
                                        ALU.subtract).then_inc(sm, 1)

            def softmax_out(h):
                dve.wait_ge(exp_ready, h + 1)
                nc.vector.tensor_reduce(ssum[:, h], s_sb[:, h], AX.X, ALU.add).then_inc(sm, 1)
                dve.wait_ge(sm, 5 * h + 4)
                nc.vector.reciprocal(rsum[:, h], ssum[:, h]).then_inc(sm, 1)
                dve.wait_ge(sm, 5 * h + 5)
                nc.vector.tensor_tensor(s_sb[:, h], s_sb[:, h], rsum[:, h].unsqueeze(2).to_broadcast([P, NB, BLK]),
                                        ALU.mult).then_inc(p_ready, 1)

            def ctx_low():
                for e in range(E):
                    dve.wait_ge(chi_ready, e + 1)
                    src = filled(dve, ("ctx", e))[:, :].rearrange("p (c r) -> p c r", c=2)
                    nc.vector.scalar_tensor_tensor(ctxT_lo[:, :, e, :], src, col["c_scale"], ctxT_hi[:, :, e, :],
                                                   ALU.mult, ALU.subtract).then_inc(clo_ready, 1)

            k_split(0)
            dve.wait_ge(dma["ctx"], 16)
            nc.vector.tensor_reduce(maxes[:, 2:3], ctx_nat[:, :, :, :].rearrange("p e c d -> p (e c d)"), AX.X,
                                    ALU.max, apply_absolute_value=True).then_inc(mxs, 1)
            k_split(1)
            t_low(0, range(H))
            dve.wait_ge(allm, 3)
            scalar(ts(col["cmax"], allmax[:, 2:3], 1e-12, None, ALU.max))
            scalar(nc.vector.tensor_single_scalar(col["pow_c"].bitcast(U32), col["cmax"].bitcast(U32), EXPONENT,
                                                  ALU.bitwise_and))
            scalar(nc.vector.reciprocal(col["inv_c"], col["pow_c"]))
            scalar(ts(col["c_scale"], col["inv_c"], 2.0 ** 14, None, ALU.mult))
            assert step == C_SCALE
            scalar(ts(col["silu_x"], col["pow_c"], 2.0 ** -25, None, ALU.mult))
            scalar(ts(col["hid_x"], col["inv_c"], 2.0 ** -28, None, ALU.mult))
            scalar(ts(col["c2"], col["pow_c"], col["pow_c"], 2.0 ** -11, ALU.mult, ALU.mult))
            scalar(ts(col["y_x"], col["c2"], col["pow_c"], None, ALU.mult))
            softmax_in(0)
            dve.wait_ge(dma["ids"], 16 * 2 * B)
            for e in range(1, E):
                ts(mask[:, e, :], ids_sb[:, :], float(e * PER_EXPERT), None, ALU.is_ge).then_inc(mask_ready, 1)
            dve.wait_ge(mask_ready, 1)
            ts(mask[:, 0, :], mask[:, 1, :], -1.0, 1.0, ALU.mult, ALU.add).then_inc(mask_ready, 1)
            t_low(1, range(0, 4))
            softmax_out(0)
            t_low(1, range(4, H))
            src = filled(dve, "wsum")
            for i in range(3):
                scalar(ts(col[f"m{i}"], src[:, i:i + 1], 1.0 / (FE * D), Q_EPS, ALU.mult, ALU.add))
            assert step == WMEAN
            for i in range(3):
                scalar(ts(col[f"h{i}"], col[f"m{i}"], 0.5, None, ALU.mult))
                scalar(ts(col[f"n{i}"], col[f"m{i}"], -0.5, None, ALU.mult))
            scalar(ts(col["silu_f"], col["m0"], 2.0 ** -11, None, ALU.mult))
            scalar(nc.vector.reciprocal(col["inv_u"], col["m0"]))
            scalar(ts(col["hid_f"], col["inv_u"], 2.0 ** -12, None, ALU.mult))
            scalar(ts(col["sg"], col["m0"], col["m1"], 2.0, ALU.mult, ALU.mult))
            scalar(ts(col["y_f"], col["sg"], col["m2"], None, ALU.mult))
            assert step == TERN
            ctx_low()
            softmax_in(1)
            for e in (1, 2):
                dve.wait_ge(mask_ready, 3 + e)
                nc.vector.tensor_tensor(mask[:, e, :], mask[:, e, :], mask[:, e + 1, :],
                                        ALU.subtract).then_inc(mask_ready, 1)
            softmax_out(1)

            def add_attention(h):
                for n in range(2):
                    src = filled(dve, ("proj", h, n))[:, :].rearrange("p (b d) -> p b d", b=2)
                    tiles = slice(TILES * h + 2 * n, TILES * h + 2 * n + 2)
                    nc.vector.tensor_tensor(x_sb[:, tiles, :], src, x_sb[:, tiles, :], ALU.add).then_inc(x1_ready, 1)
                dve.wait_ge(x1_ready, 2 * h + 2)

            def ternary(i):
                w_nat = (up_nat, gate_nat, down_nat)[i]
                dve.wait_ge(tlow_ready, i + 1)
                nc.vector.scalar_tensor_tensor(tern[:, i, :], w_nat[:, :, :].rearrange("p a b -> p (a b)"),
                                               col[f"h{i}"], tern[:, i, :], ALU.is_gt,
                                               ALU.subtract).then_inc(tern_ready, 1)

            dve.wait_ge(xb_ready, 1)
            add_attention(0)
            stats_of(2, x_sb)
            normalise(2, x_sb)

            def ln_low(which, h):
                if which == 3:
                    dve.wait_ge(mlo_ready, MLO * (h + 1))
                k = HALVES * (which - 2) + h
                for c in range(2):
                    src = filled(dve, (f"tr{which}", h, c))
                    dve.wait_ge(hhi_ready, 2 * k + c + 1)
                    nc.vector.scalar_tensor_tensor(hT_lo[:, c, NT * h:NT * (h + 1)], src[:, :], 2048.0,
                                                   hT_hi[:, c, NT * h:NT * (h + 1)], ALU.mult,
                                                   ALU.subtract).then_inc(hlo_ready, 1)

            def masked(dst, src, h, e):
                half = slice(NT * h, NT * (h + 1))
                return nc.vector.tensor_tensor(dst[h][:, e, :, :], src[:, :, half],
                                               mask[:, e, half].unsqueeze(1).to_broadcast([P, 2, NT]), ALU.mult)

            def mask_high(h, e):
                masked(hm_hi, hT_hi, h, e).then_inc(mhi_ready, 1)
                if e == 0:
                    dve.wait_ge(hlo_ready, 2 * h + 2)
                    masked(hm_lo, hT_lo, h, e).then_inc(mlo0_ready, 1)

            def hid_low(k):
                dve.wait_ge(hidhi_ready, k + 1)
                nc.vector.tensor_tensor(hid_lo[:, k % HID, :], hid[:, k % HID, :], hid_hi[:, k % HID, :],
                                        ALU.subtract).then_inc(hidlo_ready, 1)

            def add_down(n):
                for i in range(TILES):
                    src = filled(dve, ("down", n, i // 2))[:, D * (i % 2):D * (i % 2) + D]
                    T = TILES * (n % 2) + i
                    nc.vector.scalar_tensor_tensor(x_sb[:, T, :], src, col["y_x" if n < 2 else "y_f"],
                                                   x_sb[:, T, :], ALU.mult, ALU.add).then_inc(down_used, 1)

            ln_low(2, 0)
            dve.wait_ge(mask_ready, 6)
            mask_high(0, 0)
            add_attention(1)
            mask_high(0, 1)
            between = {k: [] for k in range(2 * NX)}
            between[0] = [lambda: mask_high(0, 2), lambda: mask_high(0, 3), lambda: stats_of(3, x_sb)]
            between[1] = [lambda: normalise(3, x_sb)]
            between[2] = [lambda: ternary(0)]
            between[3] = [lambda: ternary(1)]
            between[TR2] = [lambda: ln_low(2, 1), lambda: mask_high(1, 0)]
            between[TR2 + 1] = [lambda: mask_high(1, 1)]
            between[TR2 + 2] = [lambda: mask_high(1, 2), lambda: mask_high(1, 3)]
            between[TR2 + 3] = [lambda: ternary(2)]
            for n in range(3):
                last = CHUNKS * (n + 1) - 1 + LAG
                between[last] = [lambda n=n: add_down(n)]
                if n < 2:
                    between[last] += [lambda n=n: dve.wait_ge(down_used, 4 * n + 4), lambda n=n: stats_of(4 + n, x_sb)]
                    between[last + 2] = [lambda n=n: normalise(4 + n, x_sb)]
                    between[TR3 + CHUNKS * n] += [lambda n=n: ln_low(3, n)]
            for k in range(2 * NX):
                src = filled(dve, ("up", k) if k < NX else ("gate", k))
                dve.wait_ge(silu_ready, k + 1)
                if k >= HID:
                    dve.wait_ge(hidlo_ready, k - HID + 1)
                nc.vector.scalar_tensor_tensor(hid[:, k % HID, :], src[:, :], col["hid_x" if k < NX else "hid_f"],
                                               silu_sb[:, k % 2, :], ALU.mult, ALU.mult).then_inc(hid_ready, 1)
                if k:
                    hid_low(k - 1)
                for do in between[k]:
                    do()
            hid_low(2 * NX - 1)
            add_down(3)

        @block.tensor
        def _(pe):
            def begin(name):
                b, _, readers = plan[name]
                for s, v in readers:
                    pe.wait_ge(s, v)
                return bank[b]

            def end(name, ins):
                ins.then_inc(written[plan[name][0]], 1)

            mm = nc.tensor.matmul
            pe.wait_ge(consts, 2)
            for name, w_sb in (("wq", wq_sb), ("wk", wk_sb), ("wv", wv_sb)):
                o = begin(name + "T")
                pe.wait_ge(dma[name], 32)
                for i in range(4):
                    last = nc.tensor.transpose(o[:, W1 * i:W1 * i + W1], w_sb[:, P * i:P * i + P], ident[0:W1, 0:W1])
                end(name + "T", last)

            def transposes(which, h):
                pe.wait_ge(ln_done, 8 * (which - 1) + TILES * (h + 1))
                for c in range(2):
                    o = begin((f"tr{which}", h, c))
                    for i in range(TILES):
                        last = nc.tensor.transpose(o[:, P * i:P * i + P],
                                                   ln_sb[:, TILES * h + i, P * c:P * c + P], ident[:, :])
                    end((f"tr{which}", h, c), last)

            transposes(1, 0)
            pe.wait_ge(wT_ready, 6)
            for j in range(2):
                o = begin(f"A{j}")
                for i in range(2):
                    last = mm(o[0:W1, 2 * W1 * i:2 * W1 * (i + 1)], wqT[:, 2 * j + i, :],
                              wkT[:, 2 * j + i, :, :].rearrange("p s w -> p (s w)"), start=True, stop=True)
                end(f"A{j}", last)
            o = begin("G")
            pe.wait_ge(dma["wo"], 32)
            for i in range(4):
                last = mm(o[:, P * i:P * i + P], wvT[:, i, :, :].rearrange("p s w -> p (s w)"),
                          wo_sb[:, i, :, :].rearrange("p s w -> p (s w)"), start=True, stop=True)
            end("G", last)
            o = begin("yb")
            for s in range(2):
                for i in range(4):
                    for g in range(2):
                        last = mm(o[W * s:W * s + W, 0:1], wo_sb[:, i, g, :], bvT[:, i:i + 1],
                                  start=(i == 0 and g == 0), stop=(i == 3 and g == 1))
            end("yb", last)

            transposes(1, 1)

            def conv(name, h):
                pe.wait_ge(xT_ready, 2 * h + 2)
                o = begin((name, h))
                cols = slice(W, 3 * W) if name == "kv" else slice(0, W)
                m = P if name == "kv" else W
                for tap in range(TAPS):
                    for c in range(2):
                        last = mm(o[0:m, :].rearrange("p (n s) -> p n s", n=2), convw_sb[:, tap, c, cols],
                                  xT[:, c, 2 * h:2 * h + 2, tap:tap + S],
                                  start=(tap == 0 and c == 0), stop=(tap == TAPS - 1 and c == 1))
                end((name, h), last)

            def value_tokens(h):
                o = begin(("v", h))
                pe.wait_ge(kv_ready, 2 * h + 2)
                for i in range(TILES):
                    last = nc.tensor.transpose(o[:, W * i:W * i + W],
                                               vT_sb[W:P, NT * h + P * i:NT * h + P * (i + 1)], ident[W:P, W:P])
                end(("v", h), last)

            def t_products(h):
                pe.wait_ge(A_ready, 2)
                pe.wait_ge(q_ready, h + 1)
                for i in range(H):
                    o = begin(("t", h, i))
                    end(("t", h, i), mm(o[0:W1, :], A_sb[:, i, :], q_sb[:, NT * h:NT * (h + 1)], start=True, stop=True))

            def scores(h):
                o = begin(("s", h))
                pe.wait_ge(ks_ready, 3 * h + 3)
                pe.wait_ge(tlo_ready, H * (h + 1))
                for j in range(NB):
                    g = NB * h + j
                    cols = slice(BLK * g, BLK * (g + 1))
                    th = t_hi[:, g, :, :].rearrange("p h q -> p (h q)")
                    tl = t_lo[:, g, :, :].rearrange("p h q -> p (h q)")
                    d = o[:, BLK * j:BLK * (j + 1)]
                    mm(d, th, k_hi[:, cols], start=True, stop=False)
                    mm(d, th, k_lo[:, cols], start=False, stop=False)
                    last = mm(d, tl, k_hi[:, cols], start=False, stop=True)
                end(("s", h), last)

            def transposed_p(h):
                o = begin(("pT", h))
                pe.wait_ge(p_ready, h + 1)
                for i in range(TILES):
                    last = nc.tensor.transpose(o[:, P * i:P * i + P],
                                               s_sb[:, h, 8 * i:8 * i + 8, :].rearrange("p b k -> p (b k)"), ident[:, :])
                end(("pT", h), last)

            def mixed_values(h):
                pe.wait_ge(pT_ready, h + 1)
                for i in range(TILES):
                    o = begin(("u", h, i))
                    pe.wait_ge(vbd_ready, 2 * (TILES * h + i + 1))
                    for c in range(4):
                        last = mm(o[:, P * c:P * c + P],
                                  v_bd[:, TILES * h + i, c, :, :].rearrange("p b w -> p (b w)"),
                                  pT_sb[:, h, i, :], start=True, stop=True)
                    end(("u", h, i), last)

            def heads_out(h):
                pe.wait_ge(G_ready, 2)
                o = begin(("y", h))
                pe.wait_ge(u_ready, TILES * (h + 1))
                for i in range(H):
                    last = mm(o[:, 0:NT // 2], G_sb[:, i, :, :].rearrange("p b w -> p (b w)"), u_sb[:, i, :],
                              start=(i == 0), stop=(i == H - 1))
                end(("y", h), last)

            def project(h):
                pe.wait_ge(y_ready, h + 1)
                pe.wait_ge(dma["proj"], 32)
                for n in range(2):
                    o = begin(("proj", h, n))
                    end(("proj", h, n), mm(o[:, :], y_sb[:, h, P * n:P * n + P],
                                           proj_sb[:, :, :].rearrange("p b d -> p (b d)"), start=True, stop=True))

            def ff_transposes(i):
                name, j = FF[i]
                k = ("up", "gate", "down").index(name)
                o = begin(("ff", i))[:, :].bitcast(F16)
                pe.wait_ge(tern_ready, k + 1)
                pe.wait_ge(consts, 9)
                for a in range(8):
                    if name == "down":
                        c, f = a % 2, 4 * j + a // 2
                        src = tern[:, 2, FE * c + P * f:FE * c + P * f + P]
                        dst = o[:, D * (a // 2) + P * c:D * (a // 2) + P * c + P]
                    else:
                        src = tern[:, k, D * a + P * j:D * a + P * j + P]
                        dst = o[:, P * a:P * a + P]
                    last = nc.tensor.transpose(dst, src, ident16[:, :])
                end(("ff", i), last)

            def ctx_transposes(e):
                o = begin(("ctx", e))
                pe.wait_ge(dma["ctx"], 16)
                for c in range(2):
                    for r in range(2):
                        last = nc.tensor.transpose(o[:, D * c + P * r:D * c + P * r + P],
                                                   ctx_nat[:, e, r, P * c:P * c + P], ident[:, :])
                end(("ctx", e), last)

            pe.wait_ge(dma["convw"], 16)
            conv("kv", 0)
            conv("q", 0)
            conv("kv", 1)
            t_products(0)
            conv("q", 1)
            scores(0)
            for h in range(HALVES):
                value_tokens(h)
            o = begin("wsum")
            pe.wait_ge(acc_w, 3)
            end("wsum", mm(o[:, 0:3], ones[:, :], wsum[:, :], start=True, stop=True))
            t_products(1)
            for e in range(E):
                ctx_transposes(e)
            transposed_p(0)
            scores(1)
            mixed_values(0)
            heads_out(0)
            transposed_p(1)
            project(0)
            mixed_values(1)
            heads_out(1)
            transposes(2, 0)
            project(1)

            def up(k):
                h, c = k // CHUNKS % 2, k % CHUNKS
                if k < NX:
                    e, r = c // 2, c % 2
                    o = begin(("up", k))
                    pe.wait_ge(mhi_ready, E * h + e + 1)
                    if e:
                        pe.wait_ge(mlo_ready, MLO * h + 2 * e)
                    else:
                        pe.wait_ge(mlo0_ready, h + 1)
                    n = 0
                    for w, m in ((ctxT_hi, hm_hi[h]), (ctxT_lo, hm_hi[h]), (ctxT_hi, hm_lo[h])):
                        for j in range(2):
                            last = mm(o[:, :], w[:, j, e, P * r:P * r + P], m[:, e, j, :],
                                      start=(n == 0), stop=(n == 5))
                            n += 1
                    end(("up", k), last)
                else:
                    pe.wait_ge(hlo_ready, 2 * (HALVES + h + 1))
                    for use, w in (("up", upT), ("gate", gateT)):
                        o = begin((use, k))
                        n = 0
                        for j in range(2):
                            for m in (hT_hi, hT_lo):
                                last = mm(o[:, :], w[:, j, P * c:P * c + P], m[:, j, NT * h:NT * (h + 1)],
                                          start=(n == 0), stop=(n == 3))
                                n += 1
                        end((use, k), last)

            def down(k):
                n, c = k // CHUNKS, k % CHUNKS
                if c == 0:
                    outs[:] = [begin(("down", n, j)) for j in range(2)]
                pe.wait_ge(hidlo_ready, k + 1)
                for i in range(TILES):
                    o = outs[i // 2][:, D * (i % 2):D * (i % 2) + D]
                    if k < NX:
                        e, cc = c // 2, c % 2
                        pairs = [(hid_hi, ctxT_hi[:, cc, e, :]), (hid_hi, ctxT_lo[:, cc, e, :]),
                                 (hid_lo, ctxT_hi[:, cc, e, :])]
                    else:
                        pairs = [(hid_hi, downT[:, c, :]), (hid_lo, downT[:, c, :])]
                    for m, (lhs, rhs) in enumerate(pairs):
                        last = mm(o, lhs[:, k % HID, P * i:P * i + P], rhs, start=(c == 0 and m == 0 and i % 2 == 0),
                                  stop=(c == CHUNKS - 1 and m == len(pairs) - 1), skip_group_check=True)
                    if c == CHUNKS - 1 and i % 2:
                        end(("down", n, i // 2), last)
                if c < CHUNKS - 1:
                    last.then_inc(down_done, 1)

            outs = []
            pe.wait_ge(chi_ready, E)
            pe.wait_ge(clo_ready, E)
            for k in range(2 * NX + LAG):
                if k == NX:
                    pe.wait_ge(ffT_ready, len(FF))
                if k < 2 * NX:
                    up(k)
                if k == TR2:
                    transposes(2, 1)
                for i in FF_AT.get(k, ()):
                    ff_transposes(i)
                if k in (TR3, TR3 + CHUNKS):
                    transposes(3, (k - TR3) // CHUNKS)
                if k >= LAG:
                    down(k - LAG)


TR2 = 4
FF_AT = {8: (0, 1), 9: (2, 3), 10: (4, 5)}
TR3 = 14
NEWTON = 12
MLO = 6
T_SCALE = 9
C_SCALE = 17
WMEAN = 24
TERN = 35

_INS = [("x", "x"), ("ids", "itok_BxS_13_99985"), ("ctx", "ctx_2048"), ("conv_w", "L0_attn_conv_w"),
        ("conv_b", "L0_attn_conv_b"), ("wq", "L0_attn_wq"), ("bq", "L0_attn_bq"), ("wk", "L0_attn_wk"),
        ("bk", "L0_attn_bk"), ("wv", "L0_attn_wv"), ("bv", "L0_attn_bv"), ("wo", "L0_attn_wo"),
        ("bo", "L0_attn_bo"), ("proj_w", "L0_attn_proj_w"), ("proj_b", "L0_attn_proj_b"),
        ("w_up", "L0_ffn_W_up"), ("w_gate", "L0_ffn_W_gate"), ("w_down", "L0_ffn_W_down")]


def kernel(**inputs):
    import numpy as _np
    import concourse.bacc as _bacc
    from concourse import mybir as _mybir
    from concourse.bass_utils import run_bass_kernel_spmd as _run

    nc = _bacc.Bacc("TRN2", target_bir_lowering=False, num_devices=1)
    arrays, args = {}, []
    for short, name in _INS:
        a = _np.ascontiguousarray(inputs[name])
        arrays[f"in_{short}_dram"] = a
        args.append(nc.dram_tensor(f"in_{short}_dram", a.shape, _mybir.dt.from_np(a.dtype), kind="ExternalInput").ap())
    result = nc.dram_tensor("out_dram", (B, S, D), F32, kind="ExternalOutput").ap()
    decoder_kernel(nc, *args, result)
    r = _run(nc, [arrays], core_ids=[0])
    return r.results[0]["out_dram"]
```

```python
from contextlib import ExitStack

import concourse.bass as bass
from concourse import mybir

ALU = mybir.AluOpType
ACT = mybir.ActivationFunctionType
AX = mybir.AxisListType
F32 = mybir.dt.float32
F16 = mybir.dt.float16
I32 = mybir.dt.int32
U32 = mybir.dt.uint32
ADD_ALL = bass.bass_isa.ReduceOp.add
ABSMAX_ALL = bass.bass_isa.ReduceOp.absmax

P = 128
B, S, D = 4, 256, 256
TAPS = 3
W = 64
H = 8
BLK = 16
E = 4
FE = 1024
PER_EXPERT = 12500 // E
LN_EPS = 1e-5
Q_EPS = 1e-8
NEG = -1e9
EXPONENT = 0x7F800000

HALVES = 2
TILES = 4
NT = 512
NB = NT // BLK
LAG = 3
HID = 4
CHUNKS = 8
NX = HALVES * CHUNKS
MAGIC = 0x5F3759DF
CONV = 6 * TAPS
W1 = W + 1




def plan_banks(uses):
    count, readers, out = {}, {}, {}
    for name, bank, read_by in uses:
        out[name] = (bank, count.get(bank, 0) + 1, readers.get(bank, []))
        count[bank] = count.get(bank, 0) + 1
        readers[bank] = read_by
    return out


def decoder_kernel(nc, x, ids, ctx_w, conv_w, conv_b, wq, bq, wk, bk, wv, bv, wo, bo,
                   proj_w, proj_b, w_up, w_gate, w_down, out):
    stack = ExitStack()
    with stack:
        def sb(name, shape, dt=F32):
            return stack.enter_context(nc.sbuf_tensor(name, shape, dt))

        def sem(name):
            return stack.enter_context(nc.semaphore(name))

        x_sb = sb("x_sb", [P, 8, D])
        ln_sb = sb("ln_sb", [P, 8, D])
        stats = sb("stats", [P, 8, 6])
        mv = sb("mv", [P, 8, 2])
        root = sb("root", [P, 3, 8])
        rstd = sb("rstd", [P, 8])
        ident = sb("ident", [P, P])
        ident16 = sb("ident16", [P, P], F16)
        ones = sb("ones", [P, P])
        table = sb("table", [P, 2])
        key_ok = sb("key_ok", [P, H, BLK])
        causal = sb("causal", [P, BLK])
        blkmask = sb("blkmask", [P, 8])
        convw_sb = sb("convw_sb", [P, TAPS, 2, 3 * W])
        convb_sb = sb("convb_sb", [P, 2])
        wq_sb = sb("wq_sb", [W1, H * W])
        wk_sb = sb("wk_sb", [W1, H * W])
        wv_sb = sb("wv_sb", [W1, H * W])
        wqT = sb("wqT", [P, 4, W1])
        wkT = sb("wkT", [P, 4, 2, W1])
        wvT = sb("wvT", [P, 4, 2, W])
        bvT = sb("bvT", [P, 4])
        wo_sb = sb("wo_sb", [P, 4, 2, W])
        bo_sb = sb("bo_sb", [P, 1])
        proj_sb = sb("proj_sb", [P, 2, D])
        projb_sb = sb("projb_sb", [P, D])
        A_sb = sb("A_sb", [P, H, W1])
        G_sb = sb("G_sb", [P, H, 2, W])
        ybias = sb("ybias", [P, 1])
        ids_sb = sb("ids_sb", [P, 8 * P], I32)
        mask = sb("mask", [P, E, 8 * P], F16)
        convw_hi, convw_lo = (
            mask[:, 2 * j:2 * j + 2, :].rearrange("p e n -> p (e n)")[:, 0:TAPS * 2 * 3 * W].rearrange(
                "p (t c f) -> p t c f", t=TAPS, c=2) for j in range(2))
        up_nat = sb("up_nat", [P, 8, D])
        gate_nat = sb("gate_nat", [P, 8, D])
        down_nat = sb("down_nat", [P, 2, FE])
        tern = sb("tern", [P, 3, FE * 2], F16)
        upT = sb("upT", [P, 2, FE], F16)
        gateT = sb("gateT", [P, 2, FE], F16)
        downT = sb("downT", [P, 8, D], F16)
        ctx_nat = sb("ctx_nat", [P, E, 2, D])
        ctxT_hi = sb("ctxT_hi", [P, 2, E, D], F16)
        ctxT_lo = sb("ctxT_lo", [P, 2, E, D], F16)
        maxes = sb("maxes", [P, 5])
        allmax = sb("allmax", [P, 5])
        wsum = sb("wsum", [P, 3])
        sc = sb("sc", [P, 48])
        xT_st = sb("xT_st", [P, 2, 2, B, S + 2], F16)
        xT_hi, xT_lo = xT_st[:, 0], xT_st[:, 1]
        q_sb = sb("q_sb", [P, B * S])
        k_sb = sb("k_sb", [W, B * S])
        vT_sb = sb("vT_sb", [P, B * S])
        k_hi = sb("k_hi", [W1, B * S], F16)
        k_lo = sb("k_lo", [W1, B * S], F16)
        t_hi_st = sb("t_hi_st", [P, 2 * NB * P], F16)
        t_lo_st = sb("t_lo_st", [P, 2 * NB * P], F16)
        t_hi = t_hi_st[0:W1, :].rearrange("p (b h q) -> p b h q", h=H, q=BLK)
        t_lo = t_lo_st[0:W1, :].rearrange("p (b h q) -> p b h q", h=H, q=BLK)
        s_sb = sb("s_sb", [P, HALVES, NB, BLK])
        smax = sb("smax", [P, HALVES, NB])
        ssum = sb("ssum", [P, HALVES, NB])
        rsum = sb("rsum", [P, HALVES, NB])
        pT_sb = sb("pT_sb", [P, HALVES, TILES, P])
        v_tok = sb("v_tok", [P, HALVES, TILES, W])
        v_bd = sb("v_bd", [P, 8, 4, 2, W])

        hm_hi = [None, None]
        hm_lo = [None, None]
        hm_hi[0] = t_lo_st[:, 0:4096].rearrange("p (e c n) -> p e c n", e=E, c=2)
        hm_lo[0] = t_lo_st[:, 4096:8192].rearrange("p (e c n) -> p e c n", e=E, c=2)
        hm_hi[1] = up_nat[:, :, :].rearrange("p a b -> p (a b)").bitcast(F16).rearrange(
            "p (e c n) -> p e c n", e=E, c=2)
        hm_lo[1] = gate_nat[:, :, :].rearrange("p a b -> p (a b)").bitcast(F16).rearrange(
            "p (e c n) -> p e c n", e=E, c=2)
        hT_hi = t_hi_st[:, 0:2048].rearrange("p (c n) -> p c n", c=2)
        hT_lo = t_hi_st[:, 2048:4096].rearrange("p (c n) -> p c n", c=2)
        silu_sb = t_hi_st[:, 4096:6144].bitcast(F32).rearrange("p (s n) -> p s n", s=2)
        y_sb = sb("y_sb", [P, HALVES, NT // 2])
        v_all = v_bd[:, :, :, :, :].rearrange("p i c b w -> p (i c b w)")
        hid = v_all[:, 0:2048].rearrange("p (s n) -> p s n", s=HID)
        hid_hi = v_all[:, 2048:3072].bitcast(F16).rearrange("p (s n) -> p s n", s=HID)
        hid_lo = v_all[:, 3072:4096].bitcast(F16).rearrange("p (s n) -> p s n", s=HID)
        x_nat = v_all[:, 0:2048].rearrange("p (i d) -> p i d", i=8)
        u_sb = xT_st[:, :, :, :, :].rearrange("p l c n s -> p (l c n s)")[:, 0:H * NT].bitcast(F32).rearrange(
            "p (h n) -> p h n", h=H)

        bank = [stack.enter_context(nc.psum_tensor(f"bank{i}", [P, 512], F32)) for i in range(8)]

        names = ["wmax", "pow_w", "inv_w", "w_scale", "w_back", "bound", "bound1", "pow_b", "inv_b", "one_k",
                 "amax", "pow_a", "inv_a", "t_scale",
                 "f_ab", "f_scale", "cmax", "pow_c", "inv_c", "c_scale", "silu_x", "hid_x", "c2", "y_x",
                 "m0", "m1", "m2", "h0", "h1", "h2", "n0", "n1", "n2", "silu_f", "inv_u", "hid_f",
                 "sg", "y_f"]
        col = {n: sc[:, i:i + 1] for i, n in enumerate(names)}

        dma = {n: sem("loaded_" + n) for n in
               ["n0", "n1", "x", "convw", "convb", "wq", "wk", "wv", "wo", "bo", "proj", "projb", "up", "gate",
                "down", "ctx", "ids"]}
        written = [sem(f"bank{i}_written") for i in range(8)]
        consts = sem("consts")
        wsum_ready = sem("wsum_ready")
        max_ready = sem("max_ready")
        allmax_ready = sem("allmax_ready")
        scalar_ready = sem("scalar_ready")
        xb_ready = sem("xb_ready")
        wT_ready = sem("wT_ready")
        A_ready = sem("A_ready")
        G_ready = sem("G_ready")
        yb_ready = sem("yb_ready")
        dve_ln = sem("dve_ln")
        ln_seed = sem("ln_seed")
        newton = sem("newton")
        ln_done = sem("ln_done")
        xT_ready = sem("xT_ready")
        xlo_ready = sem("xlo_ready")
        wabs_ready = sem("wabs_ready")
        whi_ready = sem("whi_ready")
        wlo_ready = sem("wlo_ready")
        kv_ready = sem("kv_ready")
        q_ready = sem("q_ready")
        row_ready = sem("row_ready")
        khi_ready = sem("khi_ready")
        klo_ready = sem("klo_ready")
        vtok_ready = sem("vtok_ready")
        vbd_ready = sem("vbd_ready")
        thi_ready = sem("thi_ready")
        tlo_ready = sem("tlo_ready")
        softmax_step = sem("softmax_step")
        exp_ready = sem("exp_ready")
        p_ready = sem("p_ready")
        pT_ready = sem("pT_ready")
        u_ready = sem("u_ready")
        y_ready = sem("y_ready")
        x1_ready = sem("x1_ready")
        chi_ready = sem("chi_ready")
        clo_ready = sem("clo_ready")
        mask_ready = sem("mask_ready")
        tlow_ready = sem("tlow_ready")
        tern_ready = sem("tern_ready")
        ffT_ready = sem("ffT_ready")
        hhi_ready = sem("hhi_ready")
        hlo_ready = sem("hlo_ready")
        mhi_ready = sem("mhi_ready")
        mlo_ready = sem("mlo_ready")
        silu_ready = sem("silu_ready")
        hid_ready = sem("hid_ready")
        hidhi_ready = sem("hidhi_ready")
        hidlo_ready = sem("hidlo_ready")
        stored = sem("stored")
        down_used = sem("down_used")
        down_done = sem("down_done")
        root_steps = sem("root_steps")
        dve_set = sem("dve_set")
        mlo0_ready = sem("mlo0_ready")

        def read_t(h, i):
            return [(thi_ready, H * h + i + 1), (tlo_ready, H * h + i + 1)]

        def ln_uses(which, h, first):
            k = HALVES * (which - 2) + h
            return [((f"tr{which}", h, c), first + c, [(hhi_ready, 2 * k + c + 1), (hlo_ready, 2 * k + c + 1)])
                    for c in range(2)]

        FF = [("up", 0), ("up", 1), ("gate", 0), ("gate", 1), ("down", 0), ("down", 1)]
        uses = [("wqT", 0, [(wT_ready, 1)]), ("wkT", 1, [(wT_ready, 3)])]
        uses += [(("tr1", 0, c), 6 + c, [(xT_ready, c + 1), (xlo_ready, c + 1)]) for c in range(2)]
        uses += [(("kv", 0), 2, [(kv_ready, 2)]), ("A0", 3, [(A_ready, 1)]), ("A1", 4, [(A_ready, 2)])]
        uses += [(("tr1", 1, c), 6 + c, [(xT_ready, c + 3), (xlo_ready, c + 3)]) for c in range(2)]
        uses += [("wvT", 0, [(wT_ready, 6)]), (("q", 0), 1, [(q_ready, 1)]),
                 ("wsum", 2, [(scalar_ready, WMEAN)]), ("G", 1, [(G_ready, 2)]),
                 (("v", 0), 0, [(vtok_ready, 1)])]
        uses += [(("t", 0, i), 3 + i % 4, read_t(0, i)) for i in range(H)]
        uses += [(("ctx", e), 1 + e, [(chi_ready, e + 1), (clo_ready, e + 1)]) for e in range(2)]
        uses += [(("kv", 1), 7, [(kv_ready, 4)]), (("q", 1), 0, [(q_ready, 2)]), (("s", 0), 2, [(softmax_step, 1)]),
                 (("v", 1), 1, [(vtok_ready, 2)])]
        uses += [(("t", 1, i), 3 + i % 4, read_t(1, i)) for i in range(H)]
        uses += [("yb", 7, [(yb_ready, 1)]), (("pT", 0), 0, [(pT_ready, 1)])]
        uses += [(("u", 0, i), (2, 0)[i % 2], [(u_ready, i + 1)]) for i in range(TILES)]
        uses += [(("ff", i), 3 + i, [(ffT_ready, i + 1)]) for i in (0, 1)]
        uses += [(("s", 1), 2, [(softmax_step, 6)]), (("y", 0), 7, [(y_ready, 1)])]
        uses += [(("proj", 0, n), n, [(x1_ready, n + 1)]) for n in range(2)]
        uses += [(("ff", i), 3 + i, [(ffT_ready, i + 1)]) for i in (2, 3, 4)]
        uses += [(("ff", 5), 3, [(ffT_ready, 6)])]
        uses += [(("ctx", e), e - 2, [(chi_ready, e + 1), (clo_ready, e + 1)]) for e in (2, 3)]
        uses += [(("pT", 1), 2, [(pT_ready, 2)])]
        uses += [(("u", 1, i), (4, 5, 6, 2)[i], [(u_ready, TILES + i + 1)]) for i in range(TILES)]
        uses += [(("tr2", 0, c), (3, 7)[c], [(hhi_ready, c + 1), (hlo_ready, c + 1)]) for c in range(2)]
        uses += [(("y", 1), 4, [(y_ready, 2)])]
        uses += [(("proj", 1, n), 6 + n, [(x1_ready, 2 + n + 1)]) for n in range(2)]
        for k in range(2 * NX):
            if k < NX:
                uses += [(("up", k), k % 4, [(silu_ready, k + 1), (hid_ready, k + 1)])]
            else:
                uses += [(("up", k), 2 * (k % 2), [(silu_ready, k + 1)]),
                         (("gate", k), 2 * (k % 2) + 1, [(hid_ready, k + 1)])]
            if k >= LAG and (k - LAG) % CHUNKS == 0:
                n = (k - LAG) // CHUNKS
                uses += [(("down", n, j), 4 + 2 * (n % 2) + j, [(down_used, 4 * n + 2 * j + 2)]) for j in range(2)]
            if k == TR2:
                uses += ln_uses(2, 1, 6)
            if k == TR3:
                uses += ln_uses(3, 0, 4)
            if k == TR3 + CHUNKS:
                uses += ln_uses(3, 1, 6)
        plan = plan_banks(uses)

        def filled(eng, name):
            b, n, _ = plan[name]
            eng.wait_ge(written[b], n)
            return bank[b]

        def down_read(eng, k):
            if k % CHUNKS == CHUNKS - 1:
                filled(eng, ("down", k // CHUNKS, 1))
            else:
                eng.wait_ge(down_done, (CHUNKS - 1) * (k // CHUNKS) + k % CHUNKS + 1)

        block = stack.enter_context(nc.Block())

        @block.sync
        def _(sp):
            xnat = x.rearrange("n (t p) d -> p (n t) d", p=P)
            for h in range(HALVES):
                sp.dma_start(x_nat[:, TILES * h:TILES * (h + 1), :],
                             xnat[:, TILES * h:TILES * (h + 1), :]).then_inc(dma[f"n{h}"], 16)
                if h == 0:
                    sp.dma_start(convw_sb[:, :, :, :],
                                 conv_w.rearrange("t (c p) f -> p t c f", p=P)).then_inc(dma["convw"], 16)
            sp.dma_start(wv_sb[0:W, :], wv.rearrange("d h k -> d (h k)")).then_inc(dma["wv"], 16)
            sp.dma_start(wv_sb[W:W1, :], bv.rearrange("h k -> (h k)").unsqueeze(0)).then_inc(dma["wv"], 16)
            sp.dma_start(convb_sb[:, 0:1], conv_b[W:3 * W].unsqueeze(1)).then_inc(dma["convb"], 16)
            sp.dma_start(convb_sb[0:W, 1:2], conv_b[0:W].unsqueeze(1)).then_inc(dma["convb"], 16)
            sp.wait_ge(dve_set, 3)
            for s in range(2):
                sp.dma_start(wo_sb[W * s:W * s + W, :, s, :],
                             wo.rearrange("(i s) k o -> s k i o", s=2)[s]).then_inc(dma["wo"], 16)
            sp.dma_start(up_nat[:, :, :], w_up.rearrange("(c p) d -> p c d", p=P)).then_inc(dma["up"], 16)
            sp.dma_start(gate_nat[:, :, :], w_gate.rearrange("(c p) d -> p c d", p=P)).then_inc(dma["gate"], 16)
            sp.dma_start(down_nat[:, :, :], w_down.rearrange("(c p) d -> p c d", p=P)).then_inc(dma["down"], 16)
            for s in range(2):
                sp.dma_start(bo_sb[W * s:W * s + W, :], bo.unsqueeze(1)).then_inc(dma["bo"], 16)
            for n in range(B):
                src = ids[n].rearrange("(t b r) -> b t r", t=2, b=2)
                for b in range(2):
                    sp.dma_start(ids_sb[:, S * n + P * b:S * n + P * (b + 1)].rearrange("p (t r) -> p t r", t=2),
                                 src[b].partition_broadcast(P)).then_inc(dma["ids"], 16)
            sp.dma_start(ctx_nat[:, :, :, :], ctx_w.rearrange("e (c p) d -> p e c d", p=P)).then_inc(dma["ctx"], 16)
            sp.wait_ge(dve_set, 7)
            for s in range(2):
                sp.dma_start(proj_sb[W * s:W * s + W, s, :], proj_w).then_inc(dma["proj"], 16)
            sp.dma_start(projb_sb[:, :], proj_b.partition_broadcast(P)).then_inc(dma["projb"], 16)
            xin = x.rearrange("n (t b r) d -> t r n b d", t=2, b=2)
            for h in range(HALVES):
                dst = x_sb[:, TILES * h:TILES * (h + 1), :].rearrange("p (n b) d -> p n b d", n=2)
                for n in range(2):
                    for t in range(2):
                        sp.dma_start(dst[64 * t:64 * t + 64, n], xin[t, :, 2 * h + n]).then_inc(dma["x"], 16)
            xout = out.rearrange("n (t b r) d -> t r n b d", t=2, b=2)
            for h in range(HALVES):
                src = x_sb[:, TILES * h:TILES * (h + 1), :].rearrange("p (n b) d -> p n b d", n=2)
                for n in range(2):
                    sp.wait_ge(down_used, 8 + 4 * h + 2 * n + 2)
                    for t in range(2 - h):
                        sp.dma_start(xout[t, :, 2 * h + n], src[64 * t:64 * t + 64, n]).then_inc(stored, 16)
            sp.wait_ge(stored, 16 * 4 * HALVES)

        @block.gpsimd
        def _(pool):
            built = 0

            def const(ins):
                nonlocal built
                built += 1
                ins.then_inc(consts, 1)
                pool.wait_ge(consts, built)

            const(nc.gpsimd.memset(ident[:, :], 0.0))
            const(nc.gpsimd.affine_select(out=ident[:, :], in_=ident[:, :], compare_op=ALU.not_equal, fill=1.0,
                                          base=0, pattern=[[-1, P]], channel_multiplier=1))
            const(nc.gpsimd.memset(key_ok[:, :, :], 1.0))
            const(nc.gpsimd.affine_select(out=key_ok[:, :, :], in_=key_ok[:, :, :], compare_op=ALU.is_ge, fill=0.0,
                                          base=0, pattern=[[-BLK, H], [-1, BLK]], channel_multiplier=1))
            const(nc.gpsimd.affine_select(out=key_ok[:, :, :], in_=key_ok[:, :, :], compare_op=ALU.is_ge, fill=0.0,
                                          base=BLK - 1, pattern=[[BLK, H], [0, BLK]], channel_multiplier=-1))
            const(nc.gpsimd.memset(blkmask[:, :], 1.0))
            const(nc.gpsimd.affine_select(out=blkmask[:, :], in_=blkmask[:, :], compare_op=ALU.is_ge, fill=0.0,
                                          base=0, pattern=[[-BLK, 8]], channel_multiplier=1))
            const(nc.gpsimd.affine_select(out=blkmask[:, :], in_=blkmask[:, :], compare_op=ALU.is_ge, fill=0.0,
                                          base=BLK - 1, pattern=[[BLK, 8]], channel_multiplier=-1))
            const(nc.gpsimd.tensor_copy(ident16[:, :], ident[:, :]))
            pool.wait_ge(wabs_ready, 1)
            nc.gpsimd.partition_all_reduce(allmax[:, 4:5], maxes[:, 4:5], P, ABSMAX_ALL).then_inc(allmax_ready, 1)
            pool.wait_ge(allmax_ready, 1)
            const(nc.gpsimd.memset(q_sb[W:P, :], 0.0))
            const(nc.gpsimd.memset(q_sb[W:W1, :], 1.0))
            const(nc.gpsimd.memset(G_sb[:, :, :, :], 0.0))
            const(nc.gpsimd.memset(k_lo[W:W1, :], 0.0))

            steps = 0

            def inverse_root(k):
                nonlocal steps
                tiles = slice(TILES * (k % 2), TILES * (k % 2 + 1))
                v, y, a = (root[:, j, tiles] for j in range(3))
                pool.wait_ge(ln_seed, 3 * (k + 1))

                def step(ins):
                    nonlocal steps
                    steps += 1
                    ins.then_inc(newton, 1)
                    if steps % NEWTON:
                        pool.wait_ge(newton, steps)
                for n in range(3):
                    step(nc.gpsimd.tensor_tensor(a, y, y, ALU.mult))
                    step(nc.gpsimd.tensor_tensor(a, a, v, ALU.mult))
                    step(nc.gpsimd.tensor_scalar(a, a, -0.5, 1.5, ALU.mult, ALU.add))
                    step(nc.gpsimd.tensor_tensor(y if n < 2 else rstd[:, tiles], y, a, ALU.mult))

            inverse_root(1)
            pool.wait_ge(max_ready, 2)
            nc.gpsimd.partition_all_reduce(allmax[:, 0:2], maxes[:, 0:2], P, ABSMAX_ALL).then_inc(allmax_ready, 1)
            pool.wait_ge(max_ready, 3)
            nc.gpsimd.partition_all_reduce(allmax[:, 3:4], maxes[:, 3:4], P, ABSMAX_ALL).then_inc(allmax_ready, 1)

            def spread_v(h):
                m = blkmask[:, :].rearrange("p (b c) -> p c b", b=2).unsqueeze(3).to_broadcast([P, 4, 2, W])
                pool.wait_ge(vtok_ready, h + 1)
                for i in range(TILES):
                    for b in range(2):
                        v = v_tok[:, h, i, :].unsqueeze(1).to_broadcast([P, 4, W])
                        nc.gpsimd.tensor_tensor(v_bd[:, TILES * h + i, :, b, :], v, m[:, :, b, :],
                                                ALU.mult).then_inc(vbd_ready, 1)

            def negative(i):
                w_nat = (up_nat, gate_nat, down_nat)[i]
                pool.wait_ge(scalar_ready, TERN)
                nc.gpsimd.tensor_scalar(tern[:, i, :], w_nat[:, :, :].rearrange("p a b -> p (a b)"),
                                        col[f"n{i}"], None, ALU.is_lt).then_inc(tlow_ready, 1)

            pool.wait_ge(allmax_ready, 3)
            pool.wait_ge(scalar_ready, ONE_K)
            nc.gpsimd.tensor_scalar(k_hi[W:W1, :], q_sb[W:W1, :], col["one_k"][W:W1], None,
                                    ALU.mult).then_inc(row_ready, 1)
            pool.wait_ge(row_ready, 1)
            negative(0)
            pool.wait_ge(max_ready, 4)
            nc.gpsimd.partition_all_reduce(allmax[:, 2:3], maxes[:, 2:3], P, ABSMAX_ALL).then_inc(allmax_ready, 1)
            negative(1)
            pool.wait_ge(ln_done, 8)
            spread_v(0)
            negative(2)
            pool.wait_ge(dma["projb"], 16)
            pool.wait_ge(dma["x"], 16 * 8)
            for h in range(HALVES):
                tiles = slice(TILES * h, TILES * (h + 1))
                nc.gpsimd.tensor_tensor(x_sb[:, tiles, :], x_sb[:, tiles, :],
                                        projb_sb[:, :].unsqueeze(1).to_broadcast([P, TILES, D]),
                                        ALU.add).then_inc(xb_ready, 1)
            spread_v(1)

            def mask_low(h):
                half = slice(NT * h, NT * (h + 1))
                pool.wait_ge(hlo_ready, 2 * h + 2)
                for e in range(1, E):
                    for c in range(2):
                        nc.gpsimd.tensor_tensor(hm_lo[h][:, e, c, :], hT_lo[:, c, half], mask[:, e, half],
                                                ALU.mult).then_inc(mlo_ready, 1)

            pool.wait_ge(mask_ready, 6)
            mask_low(0)
            inverse_root(3)
            pool.wait_ge(tern_ready, 2)
            mask_low(1)
            inverse_root(4)
            inverse_root(5)

        @block.scalar
        def _(act):
            for name, dst, wsrc, bsrc in (("wq", wq_sb, wq, bq), ("wk", wk_sb, wk, bk)):
                act.dma_start(dst[0:W, :], wsrc.rearrange("d h k -> d (h k)")).then_inc(dma[name], 16)
                act.dma_start(dst[W:W1, :], bsrc.rearrange("h k -> (h k)").unsqueeze(0)).then_inc(dma[name], 16)
                if name == "wq":
                    act.wait_ge(dve_set, 1)
                    nc.scalar.activation(table[:, 0:1], ones[:, 0:1], ACT.Exp)

            act.wait_ge(dma["convw"], 16)
            nc.scalar.activation(convw_hi[:, :, :, :], convw_sb[:, :, :, :], ACT.Abs,
                                 accum_out=maxes[:, 4:5]).then_inc(wabs_ready, 1)

            def features(h):
                for c in range(2):
                    src = filled(act, ("tr1", h, c))[:, :].rearrange("p (n s) -> p n s", n=2)
                    nc.scalar.activation(xT_hi[:, c, 2 * h:2 * h + 2, 2:], src, ACT.Copy,
                                         scale=2048.0).then_inc(xT_ready, 1)

            def abs_sum(i):
                name, w_nat = (("up", up_nat), ("gate", gate_nat), ("down", down_nat))[i]
                act.wait_ge(dma[name], 16)
                nc.scalar.activation(tern[:, i, :], w_nat[:, :, :].rearrange("p a b -> p (a b)"), ACT.Abs,
                                     accum_out=wsum[:, i:i + 1]).then_inc(wsum_ready, 1)

            def keys_values(h):
                half = slice(NT * h, NT * (h + 1))
                src = filled(act, ("kv", h))
                nc.scalar.activation(k_sb[:, half], src[0:W, :], ACT.Identity,
                                     bias=convb_sb[0:W, 0:1], scale=col["w_back"][0:W]).then_inc(kv_ready, 1)
                nc.scalar.activation(vT_sb[W:P, half], src[W:P, :], ACT.Identity,
                                     bias=convb_sb[W:P, 0:1], scale=col["w_back"][W:P]).then_inc(kv_ready, 1)

            def key_high(h):
                half = slice(NT * h, NT * (h + 1))
                act.wait_ge(kv_ready, 2 * h + 1)
                nc.scalar.activation(k_hi[0:W, half], k_sb[:, half], ACT.Copy,
                                     scale=col["one_k"][0:W]).then_inc(khi_ready, 1)

            def queries(h):
                src = filled(act, ("q", h))
                nc.scalar.activation(q_sb[0:W, NT * h:NT * (h + 1)], src[0:W, :], ACT.Identity,
                                     bias=convb_sb[0:W, 1:2], scale=col["w_back"][0:W]).then_inc(q_ready, 1)

            def value_tokens(h):
                src = filled(act, ("v", h))
                nc.scalar.activation(v_tok[:, h, :, :], src[:, 0:TILES * W].rearrange("p (i w) -> p i w", w=W),
                                     ACT.Copy).then_inc(vtok_ready, 1)

            def t_high(h, heads):
                for i in heads:
                    src = filled(act, ("t", h, i))[0:W1, :].rearrange("p (b q) -> p b q", q=BLK)
                    nc.scalar.activation(t_hi[:, NB * h:NB * (h + 1), i, :], src, ACT.Copy,
                                         scale=col["t_scale"][0:W1]).then_inc(thi_ready, 1)

            def softmax_exp(h):
                act.wait_ge(softmax_step, 5 * h + 3)
                nc.scalar.activation(s_sb[:, h], s_sb[:, h], ACT.Exp).then_inc(exp_ready, 1)

            def transposed_p(h):
                src = filled(act, ("pT", h))
                nc.scalar.activation(pT_sb[:, h], src[:, :].rearrange("p (i m) -> p i m", m=P),
                                     ACT.Copy).then_inc(pT_ready, 1)

            def mixed_values(h, i):
                if h and i == 0:
                    filled(act, ("y", h - 1))
                src = filled(act, ("u", h, i))[:, :].rearrange("p (c h q) -> p h c q", c=4, h=H)
                nc.scalar.activation(u_sb[:, :, 64 * i:64 * i + 64].rearrange("p h (c q) -> p h c q", c=4),
                                     src, ACT.Copy).then_inc(u_ready, 1)

            def heads_out(h):
                src = filled(act, ("y", h))
                nc.scalar.activation(y_sb[:, h], src[:, 0:NT // 2], ACT.Identity, bias=ybias[:, :]).then_inc(y_ready, 1)

            def ctx_high(e):
                src = filled(act, ("ctx", e))[:, :].rearrange("p (c r) -> p c r", c=2)
                nc.scalar.activation(ctxT_hi[:, :, e, :], src, ACT.Copy, scale=col["c_scale"]).then_inc(chi_ready, 1)

            def ff_evac(i):
                name, j = FF[i]
                src = filled(act, ("ff", i))[:, :].bitcast(F16)
                dst = {"up": upT, "gate": gateT}.get(name)
                dst = dst[:, j, :] if dst is not None else downT[:, 4 * j:4 * j + 4, :]
                if name == "down":
                    src = src.rearrange("p (c d) -> p c d", d=D)
                nc.scalar.activation(dst, src, ACT.Copy).then_inc(ffT_ready, 1)

            act.wait_ge(scalar_ready, W_SCALE)
            nc.scalar.activation(convw_hi[:, :, :, :], convw_sb[:, :, :, :], ACT.Copy,
                                 scale=col["w_scale"]).then_inc(whi_ready, 1)
            features(0)
            abs_sum(0)
            src = filled(act, "wqT")[:, 0:4 * W1].rearrange("p (i w) -> p i w", w=W1)
            nc.scalar.activation(wqT[:, :, :], src, ACT.Copy).then_inc(wT_ready, 1)
            act.wait_ge(dve_set, 7)
            src = filled(act, "wkT")[:, 0:4 * W1].rearrange("p (i w) -> p i w", w=W1)
            for s in range(2):
                rows = slice(W * s, W * s + W)
                nc.scalar.activation(wkT[rows, :, s, :], src[rows], ACT.Copy).then_inc(wT_ready, 1)
            abs_sum(1)
            act.wait_ge(dma["convb"], 32)
            act.wait_ge(scalar_ready, W_BACK)
            keys_values(0)
            for j in range(2):
                src = filled(act, f"A{j}")[0:W1, 0:4 * W1].rearrange("p (i w) -> p i w", w=W1)
                nc.scalar.activation(A_sb[0:W1, 4 * j:4 * j + 4, :], src, ACT.Copy).then_inc(A_ready, 1)
            src = filled(act, "wvT")[:, 0:4 * W1].rearrange("p (i w) -> p i w", w=W1)
            for s in range(2):
                nc.scalar.activation(wvT[:, :, s, :], src[:, :, 0:W], ACT.Copy).then_inc(wT_ready, 1)
            nc.scalar.activation(bvT[:, :], src[:, :, W], ACT.Copy).then_inc(wT_ready, 1)
            abs_sum(2)
            queries(0)
            features(1)
            act.wait_ge(consts, CONSTS)
            value_tokens(0)
            act.wait_ge(scalar_ready, ONE_K)
            key_high(0)
            act.wait_ge(scalar_ready, T_SCALE)
            t_high(0, range(0, 2))
            src = filled(act, "G")[:, :].rearrange("p (h w) -> p h w", w=W)
            for s in range(2):
                rows = slice(W * s, W * s + W)
                nc.scalar.activation(G_sb[rows, :, s, :], src[rows], ACT.Copy).then_inc(G_ready, 1)
            t_high(0, range(2, 4))
            act.wait_ge(scalar_ready, C_SCALE)
            for e in range(4):
                t_high(0, (4 + e,))
                if e < 2:
                    ctx_high(e)
            keys_values(1)
            key_high(1)
            queries(1)
            value_tokens(1)
            t_high(1, range(0, 3))
            softmax_exp(0)
            for i in range(3, H):
                t_high(1, (i,))
                if i == 6:
                    transposed_p(0)
            for i in range(TILES):
                mixed_values(0, i)
            ff_evac(0)
            ff_evac(1)
            act.wait_ge(yb_ready, 1)
            softmax_exp(1)
            heads_out(0)
            ff_evac(2)
            transposed_p(1)
            for i in range(3):
                ff_evac(3 + i)
                mixed_values(1, i)
            mixed_values(1, 3)
            ctx_high(2)
            ctx_high(3)

            def ln_high(which, h):
                if which == 3:
                    act.wait_ge(mhi_ready, E * (h + 1))
                for c in range(2):
                    src = filled(act, (f"tr{which}", h, c))
                    nc.scalar.activation(hT_hi[:, c, NT * h:NT * (h + 1)], src[:, :], ACT.Copy,
                                         scale=2048.0).then_inc(hhi_ready, 1)

            def hid_high(k):
                act.wait_ge(hid_ready, k + 1)
                if k >= HID:
                    down_read(act, k - HID)
                nc.scalar.activation(hid_hi[:, k % HID, :], hid[:, k % HID, :], ACT.Copy).then_inc(hidhi_ready, 1)

            ln_high(2, 0)
            nc.scalar.activation(table[:, 1:2], ones[:, 0:1], ACT.Silu)
            heads_out(1)
            for k in range(2 * NX):
                if k == NX:
                    act.wait_ge(scalar_ready, TERN)
                src = filled(act, ("up", k))
                if k >= 2:
                    act.wait_ge(hid_ready, k - 1)
                nc.scalar.activation(silu_sb[:, k % 2, :], src[:, :], ACT.Silu,
                                     scale=col["silu_x" if k < NX else "silu_f"]).then_inc(silu_ready, 1)
                if k:
                    hid_high(k - 1)
                if k == TR2:
                    ln_high(2, 1)
                if k in (TR3, TR3 + CHUNKS):
                    ln_high(3, (k - TR3) // CHUNKS)
            hid_high(2 * NX - 1)
            xout = out.rearrange("n (t b r) d -> t r n b d", t=2, b=2)
            src = x_sb[:, TILES:2 * TILES, :].rearrange("p (n b) d -> p n b d", n=2)
            for n in range(2):
                act.wait_ge(down_used, 12 + 2 * n + 2)
                act.dma_start(xout[1, :, 2 + n], src[64:128, n]).then_inc(stored, 16)

        @block.vector
        def _(dve):
            nc.vector.memset(ones[:, :], 1.0).then_inc(dve_set, 1)
            nc.vector.memset(xT_st[:, :, :, :, 0:2], 0.0).then_inc(dve_set, 1)
            nc.vector.memset(wo_sb[:, :, :, :], 0.0).then_inc(dve_set, 1)
            nc.vector.memset(convb_sb[W:P, 1:2], 0.0).then_inc(dve_set, 1)
            nc.vector.memset(wkT[:, :, :, :], 0.0).then_inc(dve_set, 1)
            nc.vector.memset(A_sb[W:P, :, :], 0.0).then_inc(dve_set, 1)
            nc.vector.memset(proj_sb[:, :, :], 0.0).then_inc(dve_set, 1)

            def stats_of(k, x_of):
                for i in range(TILES):
                    T = TILES * (k % 2) + i
                    nc.vector.bn_stats(stats[:, T, :], x_of[:, T, :]).then_inc(dve_ln, 1)

            def moments(k):
                tiles = slice(TILES * (k % 2), TILES * (k % 2 + 1))
                for i in range(TILES):
                    T = TILES * (k % 2) + i
                    dve.wait_ge(dve_ln, 8 * k + i + 1)
                    nc.vector.bn_aggr(mv[:, T, :], stats[:, T, :]).then_inc(dve_ln, 1)
                dve.wait_ge(dve_ln, 8 * (k + 1))
                if k in POOL_ROOTS[1:]:
                    dve.wait_ge(newton, NEWTON * POOL_ROOTS.index(k))
                v, y = root[:, 0, tiles], root[:, 1, tiles]
                nc.vector.tensor_scalar_add(v, mv[:, tiles, 1], LN_EPS).then_inc(ln_seed, 1)
                dve.wait_ge(ln_seed, 3 * k + 1)
                nc.vector.tensor_single_scalar(y.bitcast(U32), v.bitcast(U32), 1,
                                               ALU.logical_shift_right).then_inc(ln_seed, 1)
                dve.wait_ge(ln_seed, 3 * k + 2)
                nc.vector.tensor_scalar(y.bitcast(I32), y.bitcast(I32), -1.0, float(MAGIC), ALU.mult,
                                        ALU.add).then_inc(ln_seed, 1)

            def inverse_root(k):
                nonlocal roots
                tiles = slice(0, TILES)
                v, z, a = (root[:, j, tiles] for j in range(3))

                def step(ins):
                    nonlocal roots
                    roots += 1
                    ins.then_inc(root_steps, 1)
                    dve.wait_ge(root_steps, roots)
                dve.wait_ge(ln_seed, 3 * (k + 1))
                for c in (1.0, 2.0, 16.0):
                    step(nc.vector.tensor_tensor(a, z, z, ALU.mult))
                    if k == 0 and c == 16.0:
                        w_step(0)
                    step(nc.vector.tensor_tensor(a, a, v, ALU.mult))
                    if k == 0 and c == 16.0:
                        w_step(1)
                    step(nc.vector.scalar_tensor_tensor(z, a, 3.0 * c * c, z, ALU.subtract, ALU.mult))
                if k == 0:
                    w_step(2)
                step(nc.vector.tensor_single_scalar(rstd[:, tiles], z, -1.0 / 8192.0, ALU.mult))
                if k == 0:
                    w_step(3)

            roots = 0

            def normalise(k, x_of):
                if k in POOL_ROOTS:
                    dve.wait_ge(newton, NEWTON * (POOL_ROOTS.index(k) + 1))
                else:
                    inverse_root(k)
                if k >= 2:
                    for c in range(2):
                        filled(dve, (f"tr{k // 2}", k % 2, c))
                for i in range(TILES):
                    T = TILES * (k % 2) + i
                    nc.vector.tensor_scalar(ln_sb[:, T, :], x_of[:, T, :], mv[:, T, 0:1], rstd[:, T:T + 1],
                                            ALU.subtract, ALU.mult).then_inc(ln_done, 1)

            step = 0

            def scalar(*steps):
                nonlocal step
                for ins in steps:
                    ins.then_inc(scalar_ready, 1)
                    step += 1
                dve.wait_ge(scalar_ready, step)

            ts = nc.vector.tensor_scalar

            def w_step(i):
                nonlocal step
                if i == 0:
                    dve.wait_ge(allmax_ready, 1)
                    ins = ts(col["wmax"], allmax[:, 4:5], 1e-30, None, ALU.max)
                else:
                    dve.wait_ge(scalar_ready, i)
                if i == 1:
                    ins = nc.vector.tensor_single_scalar(col["pow_w"].bitcast(U32), col["wmax"].bitcast(U32),
                                                         EXPONENT, ALU.bitwise_and)
                elif i == 2:
                    ins = nc.vector.reciprocal(col["inv_w"], col["pow_w"])
                elif i == 3:
                    ins = ts(col["w_scale"], col["inv_w"], 2.0 ** 14, None, ALU.mult)
                ins.then_inc(scalar_ready, 1)
                step += 1

            def features_low(h):
                for c in range(2):
                    src = filled(dve, ("tr1", h, c))[:, :].rearrange("p (n s) -> p n s", n=2)
                    dve.wait_ge(xT_ready, 2 * h + c + 1)
                    nc.vector.scalar_tensor_tensor(xT_lo[:, c, 2 * h:2 * h + 2, 2:], src, 2048.0,
                                                   xT_hi[:, c, 2 * h:2 * h + 2, 2:], ALU.mult,
                                                   ALU.subtract).then_inc(xlo_ready, 1)

            dve.wait_ge(dma["n0"], 16)
            stats_of(0, x_nat)
            moments(0)
            normalise(0, x_nat)
            assert step == W_SCALE
            dve.wait_ge(dma["n1"], 16)
            stats_of(1, x_nat)
            dve.wait_ge(whi_ready, 1)
            nc.vector.scalar_tensor_tensor(convw_lo[:, :, :, :], convw_sb[:, :, :, :], col["w_scale"],
                                           convw_hi[:, :, :, :], ALU.mult, ALU.subtract).then_inc(wlo_ready, 1)
            features_low(0)
            moments(1)
            scalar(ts(col["w_back"], col["pow_w"], 2.0 ** -25, None, ALU.mult))
            assert step == W_BACK

            nc.vector.tensor_reduce(maxes[:, 0:1], convw_sb[:, :, :, :].rearrange("p a b c -> p (a b c)"), AX.X,
                                    ALU.max, apply_absolute_value=True).then_inc(max_ready, 1)
            dve.wait_ge(dma["convb"], 32)
            nc.vector.tensor_reduce(maxes[:, 1:2], convb_sb[:, :], AX.X, ALU.max,
                                    apply_absolute_value=True).then_inc(max_ready, 1)
            normalise(1, x_nat)
            dve.wait_ge(A_ready, 2)
            nc.vector.tensor_reduce(maxes[:, 3:4], A_sb[:, :, :].rearrange("p h w -> p (h w)"), AX.X, ALU.max,
                                    apply_absolute_value=True).then_inc(max_ready, 1)
            dve.wait_ge(allmax_ready, 2)
            bound = float(TAPS * D)
            scalar(nc.vector.scalar_tensor_tensor(col["bound"], allmax[:, 0:1], bound, allmax[:, 1:2],
                                                  ALU.mult, ALU.add))
            scalar(nc.vector.tensor_scalar_add(col["bound1"], col["bound"], 1.0))
            scalar(nc.vector.tensor_single_scalar(col["pow_b"].bitcast(U32), col["bound1"].bitcast(U32), EXPONENT,
                                                  ALU.bitwise_and))
            scalar(nc.vector.reciprocal(col["inv_b"], col["pow_b"]))
            scalar(ts(col["one_k"], col["inv_b"], 2.0 ** 14, None, ALU.mult))
            assert step == ONE_K
            dve.wait_ge(allmax_ready, 3)
            scalar(ts(col["amax"], allmax[:, 3:4], 1e-30, None, ALU.max))
            scalar(nc.vector.tensor_single_scalar(col["pow_a"].bitcast(U32), col["amax"].bitcast(U32), EXPONENT,
                                                  ALU.bitwise_and))
            scalar(nc.vector.reciprocal(col["inv_a"], col["pow_a"]))
            scalar(ts(col["t_scale"], col["inv_a"], col["inv_b"], 2.0 ** 6, ALU.mult, ALU.mult))
            assert step == T_SCALE
            scalar(ts(col["f_ab"], col["pow_a"], col["pow_b"], 2.0 ** -23, ALU.mult, ALU.mult))
            scalar(ts(col["f_scale"], col["f_ab"], col["pow_b"], None, ALU.mult))
            scalar(nc.vector.tensor_reduce(causal[:, :], key_ok[:, :, :].rearrange("p h k -> p k h"), AX.X, ALU.add))
            scalar(ts(causal[:, :], causal[:, :], 1.0, -NEG, ALU.subtract, ALU.mult))
            features_low(1)

            src = filled(dve, "wsum")
            scalar(*(ts(col[f"m{i}"], src[:, i:i + 1], 1.0 / (FE * D), Q_EPS, ALU.mult, ALU.add) for i in range(3)))
            assert step == WMEAN
            scalar(*(ts(col[f"n{i}"], col[f"m{i}"], -0.5, None, ALU.mult) for i in range(3)))
            scalar(*(ts(col[f"h{i}"], col[f"m{i}"], 0.5, None, ALU.mult) for i in range(3)))
            assert step == TERN
            scalar(ts(col["silu_f"], col["m0"], 2.0 ** -11, None, ALU.mult),
                   nc.vector.reciprocal(col["inv_u"], col["m0"]),
                   ts(col["sg"], col["m0"], col["m1"], 2.0, ALU.mult, ALU.mult))
            scalar(ts(col["hid_f"], col["inv_u"], 2.0 ** -12, None, ALU.mult),
                   ts(col["y_f"], col["sg"], col["m2"], None, ALU.mult))

            def key_low(h):
                half = slice(NT * h, NT * (h + 1))
                dve.wait_ge(khi_ready, h + 1)
                nc.vector.scalar_tensor_tensor(k_lo[0:W, half], k_sb[:, half], col["one_k"][0:W], k_hi[0:W, half],
                                               ALU.mult, ALU.subtract).then_inc(klo_ready, 1)

            def t_low(h, heads):
                for i in heads:
                    src = filled(dve, ("t", h, i))[0:W1, :].rearrange("p (b q) -> p b q", q=BLK)
                    dve.wait_ge(thi_ready, H * h + i + 1)
                    nc.vector.scalar_tensor_tensor(t_lo[:, NB * h:NB * (h + 1), i, :], src, col["t_scale"][0:W1],
                                                   t_hi[:, NB * h:NB * (h + 1), i, :], ALU.mult,
                                                   ALU.subtract).then_inc(tlo_ready, 1)

            def softmax_in(h):
                src = filled(dve, ("s", h))[:, :].rearrange("p (b k) -> p b k", k=BLK)
                nc.vector.scalar_tensor_tensor(s_sb[:, h], src, col["f_scale"],
                                               causal[:, :].unsqueeze(1).to_broadcast([P, NB, BLK]),
                                               ALU.mult, ALU.add).then_inc(softmax_step, 1)
                dve.wait_ge(softmax_step, 5 * h + 1)
                nc.vector.tensor_reduce(smax[:, h], s_sb[:, h], AX.X, ALU.max).then_inc(softmax_step, 1)
                dve.wait_ge(softmax_step, 5 * h + 2)
                nc.vector.tensor_tensor(s_sb[:, h], s_sb[:, h], smax[:, h].unsqueeze(2).to_broadcast([P, NB, BLK]),
                                        ALU.subtract).then_inc(softmax_step, 1)

            def softmax_out(h):
                dve.wait_ge(exp_ready, h + 1)
                nc.vector.tensor_reduce(ssum[:, h], s_sb[:, h], AX.X, ALU.add).then_inc(softmax_step, 1)
                dve.wait_ge(softmax_step, 5 * h + 4)
                nc.vector.reciprocal(rsum[:, h], ssum[:, h]).then_inc(softmax_step, 1)
                dve.wait_ge(softmax_step, 5 * h + 5)
                nc.vector.tensor_tensor(s_sb[:, h], s_sb[:, h], rsum[:, h].unsqueeze(2).to_broadcast([P, NB, BLK]),
                                        ALU.mult).then_inc(p_ready, 1)

            def ctx_low(e):
                dve.wait_ge(chi_ready, e + 1)
                src = filled(dve, ("ctx", e))[:, :].rearrange("p (c r) -> p c r", c=2)
                nc.vector.scalar_tensor_tensor(ctxT_lo[:, :, e, :], src, col["c_scale"], ctxT_hi[:, :, e, :],
                                               ALU.mult, ALU.subtract).then_inc(clo_ready, 1)

            def ternary(i):
                w_nat = (up_nat, gate_nat, down_nat)[i]
                dve.wait_ge(tlow_ready, i + 1)
                nc.vector.scalar_tensor_tensor(tern[:, i, :], w_nat[:, :, :].rearrange("p a b -> p (a b)"),
                                               col[f"h{i}"], tern[:, i, :], ALU.is_gt,
                                               ALU.subtract).then_inc(tern_ready, 1)

            key_low(0)
            t_low(0, range(0, 2))
            dve.wait_ge(dma["ctx"], 16)
            nc.vector.tensor_reduce(maxes[:, 2:3], ctx_nat[:, :, :, :].rearrange("p e c d -> p (e c d)"), AX.X,
                                    ALU.max, apply_absolute_value=True).then_inc(max_ready, 1)
            t_low(0, range(2, 4))
            dve.wait_ge(allmax_ready, 4)
            scalar(ts(col["cmax"], allmax[:, 2:3], 1e-12, None, ALU.max))
            scalar(nc.vector.tensor_single_scalar(col["pow_c"].bitcast(U32), col["cmax"].bitcast(U32), EXPONENT,
                                                  ALU.bitwise_and))
            scalar(nc.vector.reciprocal(col["inv_c"], col["pow_c"]))
            scalar(ts(col["c_scale"], col["inv_c"], 2.0 ** 14, None, ALU.mult))
            assert step == C_SCALE
            scalar(ts(col["silu_x"], col["pow_c"], 2.0 ** -25, None, ALU.mult))
            scalar(ts(col["hid_x"], col["inv_c"], 2.0 ** -28, None, ALU.mult))
            scalar(ts(col["c2"], col["pow_c"], col["pow_c"], 2.0 ** -11, ALU.mult, ALU.mult))
            scalar(ts(col["y_x"], col["c2"], col["pow_c"], None, ALU.mult))
            assert step == SCALARS
            t_low(0, range(4, 5))
            for e in range(2):
                ctx_low(e)
                t_low(0, (5 + e,))
            t_low(0, (7,))
            key_low(1)
            ternary(0)
            ternary(1)
            t_low(1, range(0, 2))
            softmax_in(0)
            t_low(1, range(2, 3))
            softmax_out(0)
            t_low(1, range(3, H))
            dve.wait_ge(dma["bo"], 32)
            src = filled(dve, "yb")
            nc.vector.tensor_tensor(ybias[:, :], src[:, 0:1], bo_sb[:, :], ALU.add).then_inc(yb_ready, 1)
            ternary(2)
            dve.wait_ge(dma["ids"], 16 * 2 * B)
            filled(dve, ("q", 1))
            for e in range(1, E):
                ts(mask[:, e, :], ids_sb[:, :], float(e * PER_EXPERT), None, ALU.is_ge).then_inc(mask_ready, 1)
            dve.wait_ge(mask_ready, 1)
            ts(mask[:, 0, :], mask[:, 1, :], -1.0, 1.0, ALU.mult, ALU.add).then_inc(mask_ready, 1)
            for e in (1, 2):
                dve.wait_ge(mask_ready, 3 + e)
                nc.vector.tensor_tensor(mask[:, e, :], mask[:, e, :], mask[:, e + 1, :],
                                        ALU.subtract).then_inc(mask_ready, 1)
            softmax_in(1)

            def add_attention(h):
                for n in range(2):
                    src = filled(dve, ("proj", h, n))[:, :].rearrange("p (b d) -> p b d", b=2)
                    tiles = slice(TILES * h + 2 * n, TILES * h + 2 * n + 2)
                    nc.vector.tensor_tensor(x_sb[:, tiles, :], src, x_sb[:, tiles, :], ALU.add).then_inc(x1_ready, 1)
                dve.wait_ge(x1_ready, 2 * h + 2)

            softmax_out(1)
            dve.wait_ge(xb_ready, 2)
            add_attention(0)
            stats_of(2, x_sb)
            moments(2)
            normalise(2, x_sb)
            ctx_low(2)
            ctx_low(3)

            def ln_low(which, h):
                if which == 3:
                    dve.wait_ge(mlo_ready, MLO * (h + 1))
                k = HALVES * (which - 2) + h
                for c in range(2):
                    src = filled(dve, (f"tr{which}", h, c))
                    dve.wait_ge(hhi_ready, 2 * k + c + 1)
                    nc.vector.scalar_tensor_tensor(hT_lo[:, c, NT * h:NT * (h + 1)], src[:, :], 2048.0,
                                                   hT_hi[:, c, NT * h:NT * (h + 1)], ALU.mult,
                                                   ALU.subtract).then_inc(hlo_ready, 1)

            def masked(dst, src, h, e):
                half = slice(NT * h, NT * (h + 1))
                return nc.vector.tensor_tensor(dst[h][:, e, :, :], src[:, :, half],
                                               mask[:, e, half].unsqueeze(1).to_broadcast([P, 2, NT]), ALU.mult)

            def mask_high(h, e):
                dve.wait_ge(hhi_ready, 2 * h + 2)
                masked(hm_hi, hT_hi, h, e).then_inc(mhi_ready, 1)

            def mask_low(h):
                dve.wait_ge(hlo_ready, 2 * h + 2)
                masked(hm_lo, hT_lo, h, 0).then_inc(mlo0_ready, 1)

            def hid_low(k):
                dve.wait_ge(hidhi_ready, k + 1)
                nc.vector.tensor_tensor(hid_lo[:, k % HID, :], hid[:, k % HID, :], hid_hi[:, k % HID, :],
                                        ALU.subtract).then_inc(hidlo_ready, 1)

            def add_down(n):
                for i in range(TILES):
                    src = filled(dve, ("down", n, i // 2))[:, D * (i % 2):D * (i % 2) + D]
                    T = TILES * (n % 2) + i
                    nc.vector.scalar_tensor_tensor(x_sb[:, T, :], src, col["y_x" if n < 2 else "y_f"],
                                                   x_sb[:, T, :], ALU.mult, ALU.add).then_inc(down_used, 1)

            dve.wait_ge(mask_ready, 6)
            mask_high(0, 0)
            ln_low(2, 0)
            mask_low(0)
            mask_high(0, 1)
            def between_chunks(k):
                if k == 0:
                    add_attention(1)
                    stats_of(3, x_sb)
                if k == 1:
                    moments(3)
                if k in (1, 2):
                    mask_high(0, k + 1)
                if k == 3:
                    normalise(3, x_sb)
                if k == TR2:
                    ln_low(2, 1)
                if k == TR2 + 1:
                    mask_high(1, 0)
                    mask_low(1)
                if TR2 + 1 < k <= TR2 + E:
                    mask_high(1, k - TR2 - 1)
                n, after = (k - LAG) // CHUNKS - 1, (k - LAG) % CHUNKS
                if after == CHUNKS - 1 and -1 <= n < 2:
                    add_down(n + 1)
                if n in (0, 1):
                    if after == 0:
                        dve.wait_ge(down_used, 4 * n + 4)
                        stats_of(4 + n, x_sb)
                        moments(4 + n)
                    if after == 2:
                        normalise(4 + n, x_sb)
                if k in (TR3, TR3 + CHUNKS):
                    ln_low(3, (k - TR3) // CHUNKS)

            for k in range(2 * NX):
                src = filled(dve, ("up", k) if k < NX else ("gate", k))
                dve.wait_ge(silu_ready, k + 1)
                if k >= HID:
                    dve.wait_ge(hidlo_ready, k - HID + 1)
                nc.vector.scalar_tensor_tensor(hid[:, k % HID, :], src[:, :], col["hid_x" if k < NX else "hid_f"],
                                               silu_sb[:, k % 2, :], ALU.mult, ALU.mult).then_inc(hid_ready, 1)
                if k:
                    hid_low(k - 1)
                between_chunks(k)
            hid_low(2 * NX - 1)
            add_down(3)

        @block.tensor
        def _(pe):
            def begin(name):
                b, _, readers = plan[name]
                for s, v in readers:
                    pe.wait_ge(s, v)
                return bank[b]

            def end(name, ins):
                ins.then_inc(written[plan[name][0]], 1)

            mm = nc.tensor.matmul
            pe.wait_ge(consts, 2)

            def weight_transposes(name, w_sb):
                o = begin(name + "T")
                pe.wait_ge(dma[name], 32)
                for i in range(4):
                    last = nc.tensor.transpose(o[:, W1 * i:W1 * i + W1], w_sb[:, P * i:P * i + P], ident[0:W1, 0:W1])
                end(name + "T", last)

            def transposes(which, h):
                o = [begin((f"tr{which}", h, c)) for c in range(2)]
                for i in range(TILES):
                    pe.wait_ge(ln_done, 8 * (which - 1) + TILES * h + i + 1)
                    for c in range(2):
                        last = nc.tensor.transpose(o[c][:, P * i:P * i + P],
                                                   ln_sb[:, TILES * h + i, P * c:P * c + P], ident[:, :])
                        if i == TILES - 1:
                            end((f"tr{which}", h, c), last)

            def score_weights():
                pe.wait_ge(wT_ready, 3)
                for j in range(2):
                    o = begin(f"A{j}")
                    for i in range(2):
                        last = mm(o[0:W1, 2 * W1 * i:2 * W1 * (i + 1)], wqT[:, 2 * j + i, :],
                                  wkT[:, 2 * j + i, :, :].rearrange("p s w -> p (s w)"), start=True, stop=True)
                    end(f"A{j}", last)

            def value_weights():
                pe.wait_ge(wT_ready, 6)
                o = begin("G")
                pe.wait_ge(dma["wo"], 32)
                for i in range(4):
                    last = mm(o[:, P * i:P * i + P], wvT[:, i, :, :].rearrange("p s w -> p (s w)"),
                              wo_sb[:, i, :, :].rearrange("p s w -> p (s w)"), start=True, stop=True)
                end("G", last)

            def head_bias():
                o = begin("yb")
                for s in range(2):
                    for i in range(4):
                        for g in range(2):
                            last = mm(o[W * s:W * s + W, 0:1], wo_sb[:, i, g, :], bvT[:, i:i + 1],
                                      start=(i == 0 and g == 0), stop=(i == 3 and g == 1))
                end("yb", last)

            def conv(name, h, part=range(CONV)):
                if part[0] == 0:
                    begin((name, h))
                o = bank[plan[(name, h)][0]]
                cols = slice(W, 3 * W) if name == "kv" else slice(0, W)
                m = P if name == "kv" else W
                for i in part:
                    product, c, tap = i // (2 * TAPS), i // TAPS % 2, i % TAPS
                    w, xs = ((convw_hi, xT_hi), (convw_lo, xT_hi), (convw_hi, xT_lo))[product]
                    if i == 0:
                        pe.wait_ge(whi_ready, 1)
                    if product == 1:
                        pe.wait_ge(wlo_ready, 1)
                    if tap == 0 and product != 1:
                        pe.wait_ge(xlo_ready if product else xT_ready, 2 * h + c + 1)
                    last = mm(o[0:m, :].rearrange("p (n s) -> p n s", n=2), w[:, tap, c, cols],
                              xs[:, c, 2 * h:2 * h + 2, tap:tap + S],
                              start=(i == 0), stop=(i == CONV - 1))
                if part[-1] == CONV - 1:
                    end((name, h), last)

            def value_tokens(h):
                o = begin(("v", h))
                pe.wait_ge(kv_ready, 2 * h + 2)
                for i in range(TILES):
                    last = nc.tensor.transpose(o[:, W * i:W * i + W],
                                               vT_sb[W:P, NT * h + P * i:NT * h + P * (i + 1)], ident[W:P, W:P])
                end(("v", h), last)

            def t_product(h, i):
                if i == 0:
                    pe.wait_ge(consts, CONSTS)
                    pe.wait_ge(A_ready, 2)
                    pe.wait_ge(q_ready, h + 1)
                o = begin(("t", h, i))
                end(("t", h, i), mm(o[0:W1, :], A_sb[:, i, :], q_sb[:, NT * h:NT * (h + 1)], start=True, stop=True))

            def scores(h, blocks):
                o = bank[plan[("s", h)][0]]
                if blocks[0] == 0:
                    begin(("s", h))
                    pe.wait_ge(row_ready, 1)
                    pe.wait_ge(klo_ready, h + 1)
                    pe.wait_ge(tlo_ready, H * (h + 1))
                for j in blocks:
                    g = NB * h + j
                    cols = slice(BLK * g, BLK * (g + 1))
                    th = t_hi[:, g, :, :].rearrange("p h q -> p (h q)")
                    tl = t_lo[:, g, :, :].rearrange("p h q -> p (h q)")
                    d = o[:, BLK * j:BLK * (j + 1)]
                    mm(d, th, k_hi[:, cols], start=True, stop=False)
                    mm(d, th, k_lo[:, cols], start=False, stop=False)
                    last = mm(d, tl, k_hi[:, cols], start=False, stop=True)
                if blocks[-1] == NB - 1:
                    end(("s", h), last)

            def transposed_p(h):
                o = begin(("pT", h))
                pe.wait_ge(p_ready, h + 1)
                for i in range(TILES):
                    last = nc.tensor.transpose(o[:, P * i:P * i + P],
                                               s_sb[:, h, 8 * i:8 * i + 8, :].rearrange("p b k -> p (b k)"),
                                               ident[:, :])
                end(("pT", h), last)

            def mixed_values(h, i):
                pe.wait_ge(pT_ready, h + 1)
                o = begin(("u", h, i))
                pe.wait_ge(vbd_ready, 2 * (TILES * h + i + 1))
                for c in range(4):
                    last = mm(o[:, P * c:P * c + P],
                              v_bd[:, TILES * h + i, c, :, :].rearrange("p b w -> p (b w)"),
                              pT_sb[:, h, i, :], start=True, stop=True)
                end(("u", h, i), last)

            def heads_out(h):
                pe.wait_ge(G_ready, 2)
                o = begin(("y", h))
                pe.wait_ge(u_ready, TILES * (h + 1))
                for i in range(H):
                    last = mm(o[:, 0:NT // 2], G_sb[:, i, :, :].rearrange("p b w -> p (b w)"), u_sb[:, i, :],
                              start=(i == 0), stop=(i == H - 1))
                end(("y", h), last)

            def project(h):
                pe.wait_ge(y_ready, h + 1)
                pe.wait_ge(dma["proj"], 32)
                for n in range(2):
                    o = begin(("proj", h, n))
                    end(("proj", h, n), mm(o[:, :], y_sb[:, h, P * n:P * n + P],
                                           proj_sb[:, :, :].rearrange("p b d -> p (b d)"), start=True, stop=True))

            def ff_transposes(i):
                name, j = FF[i]
                k = ("up", "gate", "down").index(name)
                o = begin(("ff", i))[:, :].bitcast(F16)
                pe.wait_ge(tern_ready, k + 1)
                for a in range(8):
                    if name == "down":
                        c, f = a % 2, 4 * j + a // 2
                        src = tern[:, 2, FE * c + P * f:FE * c + P * f + P]
                        dst = o[:, D * (a // 2) + P * c:D * (a // 2) + P * c + P]
                    else:
                        src = tern[:, k, D * a + P * j:D * a + P * j + P]
                        dst = o[:, P * a:P * a + P]
                    last = nc.tensor.transpose(dst, src, ident16[:, :])
                end(("ff", i), last)

            def ctx_transposes(e):
                o = begin(("ctx", e))
                pe.wait_ge(dma["ctx"], 16)
                for c in range(2):
                    for r in range(2):
                        last = nc.tensor.transpose(o[:, D * c + P * r:D * c + P * r + P],
                                                   ctx_nat[:, e, r, P * c:P * c + P], ident[:, :])
                end(("ctx", e), last)

            def warm_up(n):
                for i in range(n):
                    mm(bank[5][:, 0:P], ones[:, :], ones[:, :], start=True, stop=True)

            pe.wait_ge(dve_set, 6)
            warm_up(WARM[0])
            weight_transposes("wq", wq_sb)
            weight_transposes("wk", wk_sb)
            warm_up(WARM[1])
            transposes(1, 0)
            warm_up(WARM[2])
            conv("kv", 0)
            score_weights()
            weight_transposes("wv", wv_sb)
            conv("q", 0)
            transposes(1, 1)
            value_tokens(0)
            o = begin("wsum")
            pe.wait_ge(wsum_ready, 3)
            end("wsum", mm(o[:, 0:3], ones[:, :], wsum[:, :], start=True, stop=True))
            for i in range(H):
                t_product(0, i)
                if i == 1:
                    value_weights()
                if 1 <= i < 7:
                    conv("kv", 1, range(3 * i - 3, 3 * i))
                if i in (4, 5):
                    ctx_transposes(i - 4)
            conv("q", 1)
            scores(0, range(0, 8))
            value_tokens(1)
            t_product(1, 0)
            scores(0, range(8, 16))
            for i in range(1, H):
                t_product(1, i)
                if i < 3:
                    scores(0, range(8 * i + 8, 8 * i + 16))
                if i == 5:
                    head_bias()
                if i == 6:
                    transposed_p(0)
            for i in range(TILES):
                mixed_values(0, i)
            ff_transposes(0)
            ff_transposes(1)
            scores(1, range(NB))
            heads_out(0)
            ff_transposes(2)
            project(0)
            transposed_p(1)
            for i in range(3):
                ff_transposes(3 + i)
                mixed_values(1, i)
            mixed_values(1, 3)
            ctx_transposes(2)
            ctx_transposes(3)
            transposes(2, 0)
            heads_out(1)

            def up(k):
                h, c = k // CHUNKS % 2, k % CHUNKS
                if k < NX:
                    e, r = c // 2, c % 2
                    o = begin(("up", k))
                    pe.wait_ge(mhi_ready, E * h + e + 1)
                    n = 0
                    for w, m in ((ctxT_hi, hm_hi[h]), (ctxT_lo, hm_hi[h]), (ctxT_hi, hm_lo[h])):
                        if n == 4:
                            if e:
                                pe.wait_ge(mlo_ready, MLO * h + 2 * e)
                            else:
                                pe.wait_ge(mlo0_ready, h + 1)
                        for j in range(2):
                            last = mm(o[:, :], w[:, j, e, P * r:P * r + P], m[:, e, j, :],
                                      start=(n == 0), stop=(n == 5))
                            n += 1
                    end(("up", k), last)
                else:
                    pe.wait_ge(hhi_ready, 2 * (HALVES + h + 1))
                    for use, w in (("up", upT), ("gate", gateT)):
                        o = begin((use, k))
                        n = 0
                        for m in (hT_hi, hT_lo):
                            if n:
                                pe.wait_ge(hlo_ready, 2 * (HALVES + h + 1))
                            for j in range(2):
                                last = mm(o[:, :], w[:, j, P * c:P * c + P], m[:, j, NT * h:NT * (h + 1)],
                                          start=(n == 0), stop=(n == 3))
                                n += 1
                        end((use, k), last)

            def down(k):
                n, c = k // CHUNKS, k % CHUNKS
                if c == 0:
                    outs[:] = [begin(("down", n, j)) for j in range(2)]
                pe.wait_ge(hidlo_ready, k + 1)
                for i in range(TILES):
                    o = outs[i // 2][:, D * (i % 2):D * (i % 2) + D]
                    if k < NX:
                        e, cc = c // 2, c % 2
                        pairs = [(hid_hi, ctxT_hi[:, cc, e, :]), (hid_hi, ctxT_lo[:, cc, e, :]),
                                 (hid_lo, ctxT_hi[:, cc, e, :])]
                    else:
                        pairs = [(hid_hi, downT[:, c, :]), (hid_lo, downT[:, c, :])]
                    for m, (lhs, rhs) in enumerate(pairs):
                        last = mm(o, lhs[:, k % HID, P * i:P * i + P], rhs, start=(c == 0 and m == 0 and i % 2 == 0),
                                  stop=(c == CHUNKS - 1 and m == len(pairs) - 1), skip_group_check=True)
                    if c == CHUNKS - 1 and i % 2:
                        end(("down", n, i // 2), last)
                if c < CHUNKS - 1:
                    last.then_inc(down_done, 1)

            outs = []
            pe.wait_ge(chi_ready, E)
            pe.wait_ge(clo_ready, E)
            for k in range(2 * NX + LAG):
                if k == NX:
                    pe.wait_ge(ffT_ready, len(FF))
                if k < 2 * NX:
                    up(k)
                if k == 0:
                    project(1)
                if k >= LAG:
                    down(k - LAG)
                if k == TR2:
                    transposes(2, 1)
                if k in (TR3, TR3 + CHUNKS):
                    transposes(3, (k - TR3) // CHUNKS)


TR2 = 5
TR3 = 14
WARM = (12, 5, 3)
POOL_ROOTS = (1, 3, 4, 5)
NEWTON = 12
MLO = 6
W_SCALE = 4
W_BACK = 5
ONE_K = 10
T_SCALE = 14
WMEAN = 21
TERN = 27
C_SCALE = 36
SCALARS = 40
CONSTS = 13

_INS = [("x", "x"), ("ids", "itok_BxS_13_99985"), ("ctx", "ctx_2048"), ("conv_w", "L0_attn_conv_w"),
        ("conv_b", "L0_attn_conv_b"), ("wq", "L0_attn_wq"), ("bq", "L0_attn_bq"), ("wk", "L0_attn_wk"),
        ("bk", "L0_attn_bk"), ("wv", "L0_attn_wv"), ("bv", "L0_attn_bv"), ("wo", "L0_attn_wo"),
        ("bo", "L0_attn_bo"), ("proj_w", "L0_attn_proj_w"), ("proj_b", "L0_attn_proj_b"),
        ("w_up", "L0_ffn_W_up"), ("w_gate", "L0_ffn_W_gate"), ("w_down", "L0_ffn_W_down")]


def kernel(**inputs):
    import numpy as _np
    import concourse.bacc as _bacc
    from concourse import mybir as _mybir
    from concourse.bass_utils import run_bass_kernel_spmd as _run

    nc = _bacc.Bacc("TRN2", target_bir_lowering=False, num_devices=1)
    arrays, args = {}, []
    for short, name in _INS:
        a = _np.ascontiguousarray(inputs[name])
        arrays[f"in_{short}_dram"] = a
        args.append(nc.dram_tensor(f"in_{short}_dram", a.shape, _mybir.dt.from_np(a.dtype), kind="ExternalInput").ap())
    result = nc.dram_tensor("out_dram", (B, S, D), F32, kind="ExternalOutput").ap()
    decoder_kernel(nc, *args, result)
    r = _run(nc, [arrays], core_ids=[0])
    return r.results[0]["out_dram"]
```
